# Optimizing a Trainium2 kernel written in Bass

```python
import numpy as np
import jax
import jax.numpy as jnp

def _softmax(x, axis=-1):
    return jax.nn.softmax(x, axis=axis)

def _gelu(x):
    return jax.nn.gelu(x, approximate=True)

def _silu(x):
    return jax.nn.silu(x)

def _sigmoid(x):
    return jax.nn.sigmoid(x)

def _layernorm(x, axis=-1, eps=1e-05):
    m = jnp.mean(x, axis=axis, keepdims=True)
    v = jnp.var(x, axis=axis, keepdims=True)
    return (x - m) / jnp.sqrt(v + eps)

def _scatter_add(tgt, idx, src, axis=0):
    return tgt.at[idx].add(src)

def _segment_sum(src, seg, n):
    return jax.ops.segment_sum(src, seg, n)
kernel_name = 'mk_gnn_ffn_d2_gnn_r8_a89f4a'

def setup_inputs(seed: int=0):
    np.random.seed(seed)
    _w = jnp.asarray

    def _rec_inputs():
        import jax
        import jax.numpy as jnp
        _gk = jax.random.key(seed)
        x = -0.0003713 + 1 * jax.random.normal(jax.random.fold_in(_gk, 1), (6250, 256), jnp.float32)
        src = jax.random.randint(jax.random.fold_in(_gk, 2), (100000,), 0, 6250, jnp.int32)
        dst = jnp.minimum((6250 * jax.random.uniform(jax.random.fold_in(_gk, 3), (100000,)) ** 2.0).astype(jnp.int32), 49999)
        _o = jnp.argsort(dst, stable=True)
        src = src[_o]
        dst = dst[_o]
        edge_type_16 = jax.random.randint(jax.random.fold_in(_gk, 13), (100000,), 0, 16, jnp.int32)
        edge_weight = jax.random.uniform(jax.random.fold_in(_gk, 14), (100000,), jnp.float32, 0.0, 0.999999)
        return (x, src, dst, edge_type_16, edge_weight)
    x, src, dst, edge_type_16, edge_weight = _rec_inputs()

    def _L0_gnn_setup():
        import jax, jax.numpy as jnp
        import numpy as np
        N = 6250
        E = 100000
        D = 256
        R = 16
        B = 8
        LN_EPS = 1e-05

        def _layer_norm(x, g, b):
            mu = jnp.mean(x, axis=-1, keepdims=True)
            var = jnp.mean(jnp.square(x - mu), axis=-1, keepdims=True)
            return (x - mu) * jax.lax.rsqrt(var + LN_EPS) * g + b

        def _rgcn_layer(x, edge_index, edge_type, edge_attr, basis, att, root, bias):
            n = x.shape[0]
            r = att.shape[0]
            weight = jnp.einsum('rb,bio->rio', att, basis)
            H = jnp.einsum('ni,rio->nro', x, weight)
            loop = jnp.arange(n, dtype=edge_index.dtype)
            src = jnp.concatenate([edge_index[0], loop])
            dst = jnp.concatenate([edge_index[1], loop])
            et = jnp.concatenate([edge_type, jnp.full((n,), r - 1, dtype=edge_type.dtype)])
            ea = jnp.concatenate([edge_attr, jnp.ones((n,), dtype=x.dtype)])
            msg = H[src, et] * ea[:, None]
            summ = jax.ops.segment_sum(msg, dst, num_segments=n)
            cnt = jax.ops.segment_sum(jnp.ones_like(ea), dst, num_segments=n)
            agg = summ / cnt[:, None]
            return agg + x @ root + bias
        key = jax.random.key(seed)
        ks = jax.random.split(key, 20)
        s_basis = np.sqrt(2.0 / (D + D)).astype(np.float32)
        s_att = np.sqrt(2.0 / (R + B)).astype(np.float32)
        inp = {'x': jax.random.normal(ks[0], (N, D), dtype=jnp.float32), 'edge_index': jax.random.randint(ks[1], (2, E), 0, N), 'edge_type': jax.random.randint(ks[2], (E,), 0, R), 'edge_attr': jax.random.uniform(ks[3], (E,), dtype=jnp.float32), 'basis1': jax.random.normal(ks[4], (B, D, D), dtype=jnp.float32) * s_basis, 'att1': jax.random.normal(ks[5], (R, B), dtype=jnp.float32) * s_att, 'root1': jax.random.normal(ks[6], (D, D), dtype=jnp.float32) * s_basis, 'bias1': jnp.zeros((D,), dtype=jnp.float32), 'ln1_g': jnp.ones((D,), dtype=jnp.float32), 'ln1_b': jnp.zeros((D,), dtype=jnp.float32), 'basis2': jax.random.normal(ks[7], (B, D, D), dtype=jnp.float32) * s_basis, 'att2': jax.random.normal(ks[8], (R, B), dtype=jnp.float32) * s_att, 'root2': jax.random.normal(ks[9], (D, D), dtype=jnp.float32) * s_basis, 'bias2': jnp.zeros((D,), dtype=jnp.float32), 'ln2_g': jnp.ones((D,), dtype=jnp.float32), 'ln2_b': jnp.zeros((D,), dtype=jnp.float32)}
        return inp
    _L0_gnn_all = _L0_gnn_setup()
    _L0_gnn_in = {k: v for k, v in _L0_gnn_all.items() if k in ('basis1', 'att1', 'root1', 'bias1', 'ln1_g', 'ln1_b', 'basis2', 'att2', 'root2', 'bias2', 'ln2_g', 'ln2_b')}
    del _L0_gnn_all

    def _L0_ffn_setup():
        import jax, jax.numpy as jnp
        import numpy as np
        B, S, D = (8, 512, 256)
        H = 4 * D
        CAPACITY = 0.5
        key = jax.random.key(seed)
        ks = jax.random.split(key, 6)
        x = jax.random.normal(ks[0], (B, S, D), dtype=jnp.float32)
        attention_mask = jnp.zeros((B, 1, 1, S), dtype=jnp.float32)
        wr = jax.random.normal(ks[1], (D, 1), dtype=jnp.float32) * 0.02
        br = jnp.zeros((1,), dtype=jnp.float32)
        w1 = jax.random.normal(ks[2], (D, H), dtype=jnp.float32) * 0.02
        b1 = jnp.zeros((H,), dtype=jnp.float32)
        w2 = jax.random.normal(ks[3], (H, D), dtype=jnp.float32) * 0.02
        b2 = jnp.zeros((D,), dtype=jnp.float32)
        return {'x': x, 'attention_mask': attention_mask, 'wr': wr, 'br': br, 'w1': w1, 'b1': b1, 'w2': w2, 'b2': b2}
    _L0_ffn_all = _L0_ffn_setup()
    _L0_ffn_in = {k: v for k, v in _L0_ffn_all.items() if k in ('attention_mask', 'wr', 'br', 'w1', 'b1', 'w2', 'b2')}
    del _L0_ffn_all

    def _L1_gnn_setup():
        import jax, jax.numpy as jnp
        import numpy as np
        N = 5000
        E = 80000
        D = 256
        H = 8
        DH = D // H
        DFF = 4 * D
        SCALE = D ** (-0.5)
        EPS = 1e-05

        def layernorm(x, g, b):
            mu = jnp.mean(x, axis=-1, keepdims=True)
            var = jnp.mean(jnp.square(x - mu), axis=-1, keepdims=True)
            return (x - mu) * jax.lax.rsqrt(var + EPS) * g + b
        key = jax.random.key(seed)
        ks = jax.random.split(key, 12)
        inv = 1.0 / np.sqrt(D)
        invf = 1.0 / np.sqrt(DFF)
        return {'triplet_h': jax.random.normal(ks[0], (N, D), dtype=jnp.float32), 'src': jax.random.randint(ks[1], (E,), 0, N, dtype=jnp.int32), 'dst': jax.random.randint(ks[2], (E,), 0, N, dtype=jnp.int32), 'Wqkv': jax.random.uniform(ks[3], (D, 3 * D), jnp.float32, -inv, inv), 'bqkv': jax.random.uniform(ks[4], (3 * D,), jnp.float32, -inv, inv), 'ln_attn_g': jnp.ones((D,), jnp.float32), 'ln_attn_b': jnp.zeros((D,), jnp.float32), 'ln_res_g': jnp.ones((D,), jnp.float32), 'ln_res_b': jnp.zeros((D,), jnp.float32), 'W_in': jax.random.uniform(ks[5], (D, DFF), jnp.float32, -inv, inv), 'b_in': jax.random.uniform(ks[6], (DFF,), jnp.float32, -inv, inv), 'W_out': jax.random.uniform(ks[7], (DFF, D), jnp.float32, -invf, invf), 'b_out': jax.random.uniform(ks[8], (D,), jnp.float32, -invf, invf)}
    _L1_gnn_all = _L1_gnn_setup()
    _L1_gnn_in = {k: v for k, v in _L1_gnn_all.items() if k in ('Wqkv', 'bqkv', 'ln_attn_g', 'ln_attn_b', 'ln_res_g', 'ln_res_b', 'W_in', 'b_in', 'W_out', 'b_out')}
    del _L1_gnn_all

    def _L1_ffn_setup():
        import jax, jax.numpy as jnp
        import numpy as np
        DIM = 256
        H = 8
        D = 64
        G = 64
        INNER = H * D
        SCALE = D ** (-0.5)
        key = jax.random.key(seed)
        ks = jax.random.split(key, 12)
        B, N = (4, 2048)
        x = jax.random.normal(ks[0], (B, N, DIM), dtype=jnp.float32)
        s = lambda fan_in: 1.0 / np.sqrt(fan_in)
        W_fx = jax.random.normal(ks[1], (DIM, INNER), dtype=jnp.float32) * s(DIM)
        b_fx = jnp.zeros((INNER,), dtype=jnp.float32)
        W_x = jax.random.normal(ks[2], (DIM, INNER), dtype=jnp.float32) * s(DIM)
        b_x = jnp.zeros((INNER,), dtype=jnp.float32)
        A = jax.random.normal(ks[3], (G, D), dtype=jnp.float32)
        Q, _ = jnp.linalg.qr(A.T)
        W_slice = Q[:, :G].astype(jnp.float32)
        b_slice = jnp.zeros((G,), dtype=jnp.float32)
        W_q = jax.random.normal(ks[4], (D, D), dtype=jnp.float32) * s(D)
        W_k = jax.random.normal(ks[5], (D, D), dtype=jnp.float32) * s(D)
        W_v = jax.random.normal(ks[6], (D, D), dtype=jnp.float32) * s(D)
        W_out = jax.random.normal(ks[7], (INNER, DIM), dtype=jnp.float32) * s(INNER)
        b_out = jnp.zeros((DIM,), dtype=jnp.float32)
        temperature = jnp.ones((1, H, 1, 1), dtype=jnp.float32) * 0.5
        return {'x': x, 'W_fx': W_fx, 'b_fx': b_fx, 'W_x': W_x, 'b_x': b_x, 'W_slice': W_slice, 'b_slice': b_slice, 'W_q': W_q, 'W_k': W_k, 'W_v': W_v, 'W_out': W_out, 'b_out': b_out, 'temperature': temperature}
    _L1_ffn_all = _L1_ffn_setup()
    _L1_ffn_in = {k: v for k, v in _L1_ffn_all.items() if k in ('W_fx', 'b_fx', 'W_x', 'b_x', 'W_slice', 'b_slice', 'W_q', 'W_k', 'W_v', 'W_out', 'b_out', 'temperature')}
    del _L1_ffn_all
    return {'x': x, 'src': src, 'dst': dst, 'edge_type_16': edge_type_16, 'edge_weight': edge_weight, 'L0_gnn_basis1': _L0_gnn_in['basis1'], 'L0_gnn_att1': _L0_gnn_in['att1'], 'L0_gnn_root1': _L0_gnn_in['root1'], 'L0_gnn_bias1': _L0_gnn_in['bias1'], 'L0_gnn_ln1_g': _L0_gnn_in['ln1_g'], 'L0_gnn_ln1_b': _L0_gnn_in['ln1_b'], 'L0_gnn_basis2': _L0_gnn_in['basis2'], 'L0_gnn_att2': _L0_gnn_in['att2'], 'L0_gnn_root2': _L0_gnn_in['root2'], 'L0_gnn_bias2': _L0_gnn_in['bias2'], 'L0_gnn_ln2_g': _L0_gnn_in['ln2_g'], 'L0_gnn_ln2_b': _L0_gnn_in['ln2_b'], 'L0_ffn_attention_mask': _L0_ffn_in['attention_mask'], 'L0_ffn_wr': _L0_ffn_in['wr'], 'L0_ffn_br': _L0_ffn_in['br'], 'L0_ffn_w1': _L0_ffn_in['w1'], 'L0_ffn_b1': _L0_ffn_in['b1'], 'L0_ffn_w2': _L0_ffn_in['w2'], 'L0_ffn_b2': _L0_ffn_in['b2'], 'L1_gnn_Wqkv': _L1_gnn_in['Wqkv'], 'L1_gnn_bqkv': _L1_gnn_in['bqkv'], 'L1_gnn_ln_attn_g': _L1_gnn_in['ln_attn_g'], 'L1_gnn_ln_attn_b': _L1_gnn_in['ln_attn_b'], 'L1_gnn_ln_res_g': _L1_gnn_in['ln_res_g'], 'L1_gnn_ln_res_b': _L1_gnn_in['ln_res_b'], 'L1_gnn_W_in': _L1_gnn_in['W_in'], 'L1_gnn_b_in': _L1_gnn_in['b_in'], 'L1_gnn_W_out': _L1_gnn_in['W_out'], 'L1_gnn_b_out': _L1_gnn_in['b_out'], 'L1_ffn_W_fx': _L1_ffn_in['W_fx'], 'L1_ffn_b_fx': _L1_ffn_in['b_fx'], 'L1_ffn_W_x': _L1_ffn_in['W_x'], 'L1_ffn_b_x': _L1_ffn_in['b_x'], 'L1_ffn_W_slice': _L1_ffn_in['W_slice'], 'L1_ffn_b_slice': _L1_ffn_in['b_slice'], 'L1_ffn_W_q': _L1_ffn_in['W_q'], 'L1_ffn_W_k': _L1_ffn_in['W_k'], 'L1_ffn_W_v': _L1_ffn_in['W_v'], 'L1_ffn_W_out': _L1_ffn_in['W_out'], 'L1_ffn_b_out': _L1_ffn_in['b_out'], 'L1_ffn_temperature': _L1_ffn_in['temperature']}

def reference(x, src, dst, edge_type_16, edge_weight, L0_gnn_basis1, L0_gnn_att1, L0_gnn_root1, L0_gnn_bias1, L0_gnn_ln1_g, L0_gnn_ln1_b, L0_gnn_basis2, L0_gnn_att2, L0_gnn_root2, L0_gnn_bias2, L0_gnn_ln2_g, L0_gnn_ln2_b, L0_ffn_attention_mask, L0_ffn_wr, L0_ffn_br, L0_ffn_w1, L0_ffn_b1, L0_ffn_w2, L0_ffn_b2, L1_gnn_Wqkv, L1_gnn_bqkv, L1_gnn_ln_attn_g, L1_gnn_ln_attn_b, L1_gnn_ln_res_g, L1_gnn_ln_res_b, L1_gnn_W_in, L1_gnn_b_in, L1_gnn_W_out, L1_gnn_b_out, L1_ffn_W_fx, L1_ffn_b_fx, L1_ffn_W_x, L1_ffn_b_x, L1_ffn_W_slice, L1_ffn_b_slice, L1_ffn_W_q, L1_ffn_W_k, L1_ffn_W_v, L1_ffn_W_out, L1_ffn_b_out, L1_ffn_temperature):
    import jax
    import jax.numpy as jnp

    def _L0_gnn_ref(x, edge_index, edge_type, edge_attr, basis1, att1, root1, bias1, ln1_g, ln1_b, basis2, att2, root2, bias2, ln2_g, ln2_b):
        import jax, jax.numpy as jnp
        import numpy as np
        N = 6250
        E = 100000
        D = 256
        R = 16
        B = 8
        LN_EPS = 1e-05

        def _layer_norm(x, g, b):
            mu = jnp.mean(x, axis=-1, keepdims=True)
            var = jnp.mean(jnp.square(x - mu), axis=-1, keepdims=True)
            return (x - mu) * jax.lax.rsqrt(var + LN_EPS) * g + b

        def _rgcn_layer(x, edge_index, edge_type, edge_attr, basis, att, root, bias):
            n = x.shape[0]
            r = att.shape[0]
            weight = jnp.einsum('rb,bio->rio', att, basis)
            H = jnp.einsum('ni,rio->nro', x, weight)
            loop = jnp.arange(n, dtype=edge_index.dtype)
            src = jnp.concatenate([edge_index[0], loop])
            dst = jnp.concatenate([edge_index[1], loop])
            et = jnp.concatenate([edge_type, jnp.full((n,), r - 1, dtype=edge_type.dtype)])
            ea = jnp.concatenate([edge_attr, jnp.ones((n,), dtype=x.dtype)])
            msg = H[src, et] * ea[:, None]
            summ = jax.ops.segment_sum(msg, dst, num_segments=n)
            cnt = jax.ops.segment_sum(jnp.ones_like(ea), dst, num_segments=n)
            agg = summ / cnt[:, None]
            return agg + x @ root + bias
        h = x
        h_out = _rgcn_layer(h, edge_index, edge_type, edge_attr, basis1, att1, root1, bias1)
        h = jax.nn.relu(_layer_norm(h + h_out, ln1_g, ln1_b))
        h_out = _rgcn_layer(h, edge_index, edge_type, edge_attr, basis2, att2, root2, bias2)
        h = jax.nn.relu(_layer_norm(h + h_out, ln2_g, ln2_b))
        return h

    def _L0_ffn_ref(x, attention_mask, wr, br, w1, b1, w2, b2):
        import jax, jax.numpy as jnp
        import numpy as np
        B, S, D = (8, 512, 256)
        H = 4 * D
        CAPACITY = 0.5
        b, s, d = x.shape
        weights = (jnp.einsum('bsd,do->bso', x, wr) + br)[..., 0]
        k = max(1, int(CAPACITY * s))
        kk = k - 1 if k > 1 else 1
        _, idx = jax.lax.top_k(weights, k)
        sel_idx = idx[:, :kk]
        sel = jnp.take_along_axis(x, sel_idx[:, :, None], axis=1)
        h = jax.nn.gelu(jnp.einsum('bkd,dh->bkh', sel, w1) + b1)
        y = jnp.einsum('bkh,hd->bkd', h, w2) + b2
        w_sel = jnp.take_along_axis(weights, sel_idx, axis=1)
        y = y * w_sel[..., None]
        batch_idx = jnp.arange(b)[:, None]
        processed = jnp.zeros_like(x).at[batch_idx, sel_idx].set(y)
        return processed + x

    def _L1_gnn_ref(triplet_h, src, dst, Wqkv, bqkv, ln_attn_g, ln_attn_b, ln_res_g, ln_res_b, W_in, b_in, W_out, b_out):
        import jax, jax.numpy as jnp
        import numpy as np
        N = 5000
        E = 80000
        D = 256
        H = 8
        DH = D // H
        DFF = 4 * D
        SCALE = D ** (-0.5)
        EPS = 1e-05

        def layernorm(x, g, b):
            mu = jnp.mean(x, axis=-1, keepdims=True)
            var = jnp.mean(jnp.square(x - mu), axis=-1, keepdims=True)
            return (x - mu) * jax.lax.rsqrt(var + EPS) * g + b
        n = triplet_h.shape[0]
        h = layernorm(triplet_h, ln_attn_g, ln_attn_b)
        qkv = (h @ Wqkv + bqkv).reshape(n, 3, H, DH)
        q = qkv[:, 0] * SCALE
        k = qkv[:, 1]
        v = qkv[:, 2]
        scores = jnp.einsum('ehd,ehd->eh', q[src], k[dst])
        m = jax.ops.segment_max(scores, dst, num_segments=n)
        e = jnp.exp(scores - m[dst])
        s = jax.ops.segment_sum(e, dst, num_segments=n)
        sa = e / s[dst]
        he = (v[src] * sa[:, :, None]).reshape(-1, D)
        agg = jax.ops.segment_sum(he, dst, num_segments=n)
        x = triplet_h + agg
        y = layernorm(x, ln_res_g, ln_res_b)
        y = jax.nn.gelu(y @ W_in + b_in, approximate=False) @ W_out + b_out
        return x + y

    def _L1_ffn_ref(x, W_fx, b_fx, W_x, b_x, W_slice, b_slice, W_q, W_k, W_v, W_out, b_out, temperature):
        import jax, jax.numpy as jnp
        import numpy as np
        DIM = 256
        H = 8
        D = 64
        G = 64
        INNER = H * D
        SCALE = D ** (-0.5)
        B, N, _ = x.shape
        fx_mid = (x @ W_fx + b_fx).reshape(B, N, H, D).transpose(0, 2, 1, 3)
        x_mid = (x @ W_x + b_x).reshape(B, N, H, D).transpose(0, 2, 1, 3)
        temp = jnp.clip(temperature, 0.1, 5.0)
        slice_weights = jax.nn.softmax((x_mid @ W_slice + b_slice) / temp, axis=-1)
        slice_norm = slice_weights.sum(axis=2)
        slice_token = jnp.einsum('bhnc,bhng->bhgc', fx_mid, slice_weights)
        slice_token = slice_token / (slice_norm[..., None] + 1e-05)
        q = slice_token @ W_q
        k = slice_token @ W_k
        v = slice_token @ W_v
        attn = jax.nn.softmax(jnp.einsum('bhgc,bhkc->bhgk', q, k) * SCALE, axis=-1)
        out_slice = jnp.einsum('bhgk,bhkc->bhgc', attn, v)
        out_x = jnp.einsum('bhgc,bhng->bhnc', out_slice, slice_weights)
        out_x = out_x.transpose(0, 2, 1, 3).reshape(B, N, INNER)
        return out_x @ W_out + b_out
    edge_index = jnp.stack([src, dst])
    x = x + _L0_gnn_ref(_layernorm(x, axis=-1), edge_index, edge_type_16, edge_weight, L0_gnn_basis1, L0_gnn_att1, L0_gnn_root1, L0_gnn_bias1, L0_gnn_ln1_g, L0_gnn_ln1_b, L0_gnn_basis2, L0_gnn_att2, L0_gnn_root2, L0_gnn_bias2, L0_gnn_ln2_g, L0_gnn_ln2_b)
    x = x + _L0_ffn_ref(_layernorm(x, axis=-1)[None], L0_ffn_attention_mask, L0_ffn_wr, L0_ffn_br, L0_ffn_w1, L0_ffn_b1, L0_ffn_w2, L0_ffn_b2)[0]
    x = x + _L1_gnn_ref(_layernorm(x, axis=-1), src, dst, L1_gnn_Wqkv, L1_gnn_bqkv, L1_gnn_ln_attn_g, L1_gnn_ln_attn_b, L1_gnn_ln_res_g, L1_gnn_ln_res_b, L1_gnn_W_in, L1_gnn_b_in, L1_gnn_W_out, L1_gnn_b_out)
    x = x + _L1_ffn_ref(_layernorm(x, axis=-1)[None], L1_ffn_W_fx, L1_ffn_b_fx, L1_ffn_W_x, L1_ffn_b_x, L1_ffn_W_slice, L1_ffn_b_slice, L1_ffn_W_q, L1_ffn_W_k, L1_ffn_W_v, L1_ffn_W_out, L1_ffn_b_out, L1_ffn_temperature)[0]
    return x

_drawn_inputs = setup_inputs


def setup_inputs(seed=0):
    import zlib

    import numpy as np

    out = dict(_drawn_inputs(seed))
    spreads = {'L0_gnn_bias1': (0.0, 0.1),
     'L0_gnn_ln1_g': (1.0, 0.2),
     'L0_gnn_ln1_b': (0.0, 0.1),
     'L0_gnn_bias2': (0.0, 0.1),
     'L0_gnn_ln2_g': (1.0, 0.2),
     'L0_gnn_ln2_b': (0.0, 0.1),
     'L0_ffn_b1': (0.0, 0.8),
     'L0_ffn_b2': (0.0, 0.799),
     'L1_gnn_ln_attn_g': (1.0, 0.6),
     'L1_gnn_ln_attn_b': (0.0, 0.413),
     'L1_gnn_ln_res_g': (1.0, 0.6),
     'L1_gnn_ln_res_b': (0.0, 0.8),
     'L1_ffn_b_fx': (0.0, 0.274),
     'L1_ffn_b_x': (0.0, 2.0),
     'L1_ffn_b_slice': (0.0, 2.0),
     'L1_ffn_b_out': (0.0, 0.283),
     'L1_ffn_temperature': (0.5, 0.6)}
    factors = {'L0_ffn_wr': 4.261,
     'L0_ffn_w1': 5.124,
     'L0_ffn_w2': 4.798,
     'L1_gnn_bqkv': 5.123,
     'L1_gnn_b_in': 8.0,
     'L1_gnn_b_out': 8.0,
     'L1_ffn_W_x': 8.0,
     'L1_ffn_W_slice': 8.0,
     'L1_ffn_W_q': 8.0,
     'L1_ffn_W_k': 8.0}
    for name, (base, spread) in spreads.items():
        noise = np.random.default_rng([zlib.crc32(name.encode()), seed]).standard_normal(out[name].shape)
        drawn = base * np.exp(spread * noise) if base else spread * noise
        out[name] = jnp.asarray(drawn.astype(out[name].dtype))
    for name, factor in factors.items():
        out[name] = (out[name] * factor).astype(out[name].dtype)
    return out
```

```python
from contextlib import ExitStack

import concourse.bass as bass
from concourse import mybir

F32 = mybir.dt.float32
I32 = mybir.dt.int32
ALU = mybir.AluOpType
ACT = mybir.ActivationFunctionType
AX = mybir.AxisListType.X

P = 128
N, D, E = 6250, 256, 100000
NT = -(-N // P)
NP = NT * P
LAST = N - (NT - 1) * P
R, B = 16, 8
H = 8
DH = D // H
DFF = 4 * D
C2 = D // P
ERP, ERJ = 112, 7
ETILES = ERP * ERJ
EFULL, EREST = E // P, E % P
PAIRP = next(p for p in range(P, 0, -1) if (E - 1) % p == 0)
PAIRE = (E - 1) // PAIRP
STEPS = ETILES + NT - 1
SP_, SJ = 104, 8
CH = 16
CS = STEPS // CH
CL = CS * P
BATCH = 8
NBATCH = STEPS // BATCH
AW = 264
PADDST = NP - 1
TOPK = N // 2 - 1
BIG = 1e30
EPS = 1e-5
INNER, G, DS = 512, 64, 64
assert STEPS == SP_ * SJ == CH * CS


class Mem:
    pass


def semaphore(nc, m, name):
    handle = nc.alloc_semaphore(name=name)
    m.semaphores.append(handle)
    return handle


def recycle_semaphores(nc, m):
    nc.all_engine_barrier()
    nc.clear_and_free_semaphores(m.semaphores)
    nc.all_engine_barrier()
    m.semaphores = []


def tiles(eng, body):
    with eng.Fori(0, (NT - 1) // 2) as i:
        for k in range(2):
            body(i * 2 + k, k, False)
    body(NT - 1, (NT - 1) % 2, True)


def batches(eng, body):
    with eng.Fori(0, NBATCH // 2 - 1) as i:
        for q in range(2):
            body(i * 2 + q, q, False)
    body(NBATCH - 2, 0, False)
    body(NBATCH - 1, 1, True)


def at(ap3, t):
    return ap3[:, bass.ds(t, 1), :].rearrange("p a d -> p (a d)")


def col(ap2, s):
    return ap2[:, bass.ds(s, 1)]


def setup(nc, ctx, m, a):
    sem = lambda n: semaphore(nc, m, n)
    zeroed, iotas, loaded, edges_in, fields, stored, pairs_in, totalled = (sem(n) for n in (
        "su_zeroed", "su_iotas", "su_loaded", "su_edges_in", "su_fields", "su_stored", "su_pairs_in", "su_totalled"))
    q2 = slice(0, PAIRP)
    pair = m.AGG[:, 0:2 * PAIRE].bitcast(I32).rearrange("p (i e) -> p i e", i=2)
    later = m.AGG[:, 2 * PAIRE:3 * PAIRE]
    ei = m.SC[:, 0:3 * ERJ * P].bitcast(I32).rearrange("p (f j e) -> p f j e", f=3, j=ERJ)
    ew = m.SC[:, 3 * ERJ * P:4 * ERJ * P].rearrange("p (j e) -> p j e", j=ERJ)
    ef = m.WT[:, 0:ERJ * 4 * P].rearrange("p (j f e) -> p j f e", j=ERJ, f=4)
    with nc.Block() as block:
        @block.gpsimd
        def _(g):
            g.memset(m.ident[:, :], 0.0).then_inc(iotas, 1)
            g.wait_ge(iotas, 1)
            g.affine_select(out=m.ident[:, :], in_=m.ident[:, :], compare_op=ALU.not_equal, fill=1.0,
                            base=0, pattern=[[-1, P]], channel_multiplier=1).then_inc(iotas, 1)
            g.iota(m.iota[:, :], [[1, P]], base=0, channel_multiplier=0,
                   allow_small_or_imprecise_dtypes=True).then_inc(iotas, 1)
            g.memset(m.ones[:, :], 1.0).then_inc(iotas, 1)
            g.memset(m.upper[:, :], 1.0).then_inc(iotas, 1)
            g.wait_ge(iotas, 5)
            g.affine_select(out=m.upper[:, :], in_=m.upper[:, :], compare_op=ALU.is_gt, fill=0.0,
                            base=0, pattern=[[1, P]], channel_multiplier=-1).then_inc(iotas, 1)
            g.memset(m.valid[:, :], 1.0).then_inc(iotas, 1)
            g.wait_ge(iotas, 7)
            g.affine_select(out=m.valid[:, :], in_=m.valid[:, :], compare_op=ALU.is_gt, fill=0.0,
                            base=N, pattern=[[-P, NT]], channel_multiplier=-1).then_inc(iotas, 1)

        @block.vector
        def _(v):
            v.memset(m.HB[:, NT - 1, :], 0.0).then_inc(zeroed, 1)
            v.memset(ei[:, 0, ERJ - 1, :], 0).then_inc(zeroed, 1)
            v.memset(ei[:, 1, ERJ - 1, :], PADDST).then_inc(zeroed, 1)
            v.memset(ei[:, 2, ERJ - 1, :], 0).then_inc(zeroed, 1)
            v.memset(ew[:, ERJ - 1, :], 0.0).then_inc(zeroed, 1)
            v.wait_ge(edges_in, 12 * 16)
            q = slice(0, ERP)
            v.tensor_copy(ef[q, :, 0, :], ei[q, 1]).then_inc(fields, 1)
            v.tensor_copy(ef[q, :, 2, :], ei[q, 0]).then_inc(fields, 1)
            v.tensor_copy(ef[q, :, 3, :], ew[q]).then_inc(fields, 1)
            v.scalar_tensor_tensor(ef[q, :, 1, :], ei[q, 0], float(R), ei[q, 2], ALU.mult, ALU.add).then_inc(fields, 1)
            v.wait_ge(pairs_in, 32)
            v.tensor_tensor(later[q2], pair[q2, 0], pair[q2, 1], ALU.is_gt).then_inc(fields, 1)
            v.memset(m.small[:, 0:1], 0.0).then_inc(fields, 1)
            v.wait_ge(fields, 6)
            v.tensor_reduce(m.small[q2, 0:1], later[q2], AX, ALU.add).then_inc(fields, 1)
            v.wait_ge(totalled, 1)
            v.tensor_copy(m.unsorted[:, :], m.ps[0][0:1, 0:1]).then_inc(fields, 1)

        @block.tensor
        def _(pe):
            pe.wait_ge(fields, 7)
            pe.wait_ge(iotas, 4)
            pe.matmul(m.ps[0][:, 0:1], m.ones[:, :], m.small[:, 0:1], start=True, stop=True).then_inc(totalled, 1)

        @block.sync
        def _(s):
            s.dma_start(m.HB[:, 0:NT - 1, :], a["x"][0:(NT - 1) * P].rearrange("(t p) d -> p t d", p=P)).then_inc(loaded, 16)
            s.wait_ge(zeroed, 5)
            s.dma_start(m.HB[0:LAST, NT - 1, :], a["x"][(NT - 1) * P:N]).then_inc(loaded, 16)
            full = (ERJ - 1) * ERP
            for dst, name in ((ei[:, 0], "src"), (ei[:, 1], "dst"), (ei[:, 2], "edge_type_16"), (ew, "edge_weight")):
                v = a[name]
                s.dma_start(dst[0:ERP, 0:ERJ - 1, :], v[0:full * P].rearrange("(j p e) -> p j e", p=ERP, e=P)).then_inc(edges_in, 16)
                s.dma_start(dst[0:EFULL - full, ERJ - 1, :], v[full * P:EFULL * P].rearrange("(p e) -> p e", e=P)).then_inc(edges_in, 16)
                s.dma_start(dst[EFULL - full:EFULL - full + 1, ERJ - 1, 0:EREST], v[EFULL * P:E].rearrange("(p e) -> p e", p=1)).then_inc(edges_in, 16)
            for i in range(2):
                s.dma_start(pair[q2, i], a["dst"][i:i + E - 1].rearrange("(p e) -> p e", p=PAIRP)).then_inc(pairs_in, 16)
            s.wait_ge(fields, 4)
            s.dma_start(m.edg.rearrange("(j p) (f e) -> p j f e", p=ERP, f=4), ef[0:ERP]).then_inc(stored, 16)
            s.dma_start(m.dsts.rearrange("(j p e) -> p j e", p=ERP, e=P), ef[0:ERP, :, 0, :]).then_inc(stored, 16)
            s.wait_ge(stored, 32)
            s.wait_ge(loaded, 32)
            s.dma_start(m.xs.rearrange("(t p) d -> p t d", p=P), m.HB).then_inc(stored, 16)
            s.wait_ge(stored, 48)
            s.wait_ge(fields, 8)


def sort_edges(nc, ctx, m):
    sem = lambda n: semaphore(nc, m, f"so_{n}")
    loaded, chunk_in, chunk_used, ranked, placed, moved, iotas, carry = (sem(n) for n in (
        "loaded", "chunk_in", "chunk_used", "ranked", "placed", "moved", "iotas", "carry"))
    NC = 16
    CE = ETILES * P // NC
    dch, pos = m.AGG[:, 0:CE], m.AGG[:, CE:2 * CE]
    mask = m.WT[:, 0:CE]
    rec = m.SC[:, 0:4 * ETILES].rearrange("p (i f) -> p i f", f=4)
    rank, mine = m.SC[:, 4 * ETILES:5 * ETILES], m.SC[:, 5 * ETILES:6 * ETILES]
    less, same = m.small[:, 0:1], m.small[:, 1:2]
    one_rec, one_rank = m.small[:, 4:8], m.smalli[:, 0:1]
    dcol = rec[:, :, 0]
    with nc.Block() as block:
        @block.sync
        def _(s):
            unsorted = s.value_load(m.unsorted[0:1, 0:1], min_val=0, max_val=E)
            with s.If(unsorted > 0):
                for f in range(4):
                    s.dma_start(rec[:, :, f], m.edg[:, f * P:(f + 1) * P].rearrange("i e -> e i")).then_inc(loaded, 16)
                with s.Fori(0, NC) as c:
                    s.wait_ge(chunk_used, c + 1)
                    s.dma_start(dch, m.dsts[bass.ds(c * CE, CE)].partition_broadcast(P)).then_inc(chunk_in, 16)
                s.wait_ge(placed, 16 * ETILES)
                with s.Fori(0, ETILES) as i:
                    s.dma_start(m.edg[bass.ds(i, 1), :].rearrange("o (f e) -> (o f) e", f=4),
                                m.srec[bass.ds(i * P, P), :].rearrange("e f -> f e")).then_inc(moved, 16)
                    s.wait_ge(moved, i * 16 + 16)
                    s.sem_inc(carry, 1)
            s.nop()

        @block.vector
        def _(v):
            unsorted = v.value_load(m.unsorted[0:1, 0:1], min_val=0, max_val=E)
            with v.If(unsorted > 0):
                v.sem_inc(chunk_used, 1)
                v.wait_ge(iotas, 2)
                v.wait_ge(loaded, 64)
                v.memset(rank, 0.0)
                with v.Fori(0, NC) as c:
                    v.wait_ge(chunk_in, c * 16 + 16)
                    v.sem_inc(carry, 1)
                    with v.Fori(0, ETILES) as i:
                        v.drain()
                        v.tensor_scalar(mask, pos, col(mine, i), None, ALU.is_lt)
                        v.drain()
                        v.scalar_tensor_tensor(mask, dch, col(dcol, i), mask, ALU.is_equal, ALU.mult, accum_out=same)
                        v.drain()
                        v.tensor_scalar(mask, dch, col(dcol, i), 0.0, ALU.is_lt, ALU.add, accum_out=less)
                        v.drain()
                        v.tensor_tensor(col(rank, i), col(rank, i), same, ALU.add)
                        v.drain()
                        v.tensor_tensor(col(rank, i), col(rank, i), less, ALU.add)
                    v.drain()
                    v.tensor_scalar(mine, mine, -float(CE), None, ALU.add).then_inc(chunk_used, 1)
                v.drain()
                v.sem_inc(ranked, 1)
            v.nop()

        @block.gpsimd
        def _(g):
            unsorted = g.value_load(m.unsorted[0:1, 0:1], min_val=0, max_val=E)
            with g.If(unsorted > 0):
                g.iota(pos, [[1, CE]], base=0, channel_multiplier=0, allow_small_or_imprecise_dtypes=True).then_inc(iotas, 1)
                g.iota(mine, [[P, ETILES]], base=0, channel_multiplier=1, allow_small_or_imprecise_dtypes=True).then_inc(iotas, 1)
                g.wait_ge(ranked, 1)
                with g.Fori(0, ETILES) as i:
                    g.drain()
                    g.tensor_copy(one_rank, col(rank, i))
                    g.tensor_copy(one_rec, rec[:, bass.ds(i, 1), :].rearrange("p i f -> p (i f)"))
                    g.drain()
                    g.indirect_dma_start(m.srec, bass.IndirectOffsetOnAxis(ap=one_rank, axis=0), one_rec, None).then_inc(placed, 16)
                    g.wait_ge(placed, i * 16 + 16)
                    g.sem_inc(carry, 1)
            g.nop()


def schedule(nc, ctx, m):
    sem = lambda n: semaphore(nc, m, n)
    rows_in, iotas, v_done, idx_ready, rows_got, turned, copied, stored = (sem(n) for n in (
        "sc_rows_in", "sc_iotas", "sc_vector", "sc_idx", "sc_rows", "sc_turned", "sc_copied", "sc_stored"))
    ends_in, ends, ends_out = (sem(n) for n in ("sc_ends_in", "sc_ends", "sc_ends_out"))
    t = ETILES
    ln, aw, pin, dif, junk, io = (m.WT[:, i * t:(i + 1) * t] for i in range(6))
    scol, icol, wcol, ncol, vcol = (m.small[0:SP_, i * SJ:(i + 1) * SJ] for i in range(5))
    wint = m.smalli[0:SP_, 0:SJ]
    iint = m.smalli[0:SP_, SJ:2 * SJ]
    gr = m.SC[0:SP_, 0:SJ * 4 * P].rearrange("p (j f) -> p j f", j=SJ)
    rel = m.G[0:SP_, 0:SJ * P].rearrange("p (j e) -> p j e", j=SJ)
    tabs = (m.TDR, m.TCI, m.TSI, m.TEA)
    with nc.Block() as block:
        @block.sync
        def _(s):
            for j, e in ((0, 0), (1, P - 1)):
                s.dma_start(m.ab[0:ERP, j, :], m.edg[:, e:e + 1].rearrange("(j p) e -> p (j e)", p=ERP)).then_inc(ends_in, 16)
            s.wait_ge(ends, 4)
            for j in range(2):
                s.dma_start(m.abd[j].rearrange("(j p) -> p j", p=ERP), m.ab[0:ERP, j, :]).then_inc(ends_out, 16)
            s.wait_ge(ends_out, 32)
            s.dma_start(aw, m.abd[0].partition_broadcast(P)).then_inc(rows_in, 16)
            s.dma_start(ln, m.abd[1].partition_broadcast(P)).then_inc(rows_in, 16)
            s.wait_ge(rows_got, 16 * SJ)
            s.dma_start(m.keyd.rearrange("(j p) e -> p j e", p=SP_), gr[:, :, 0:P]).then_inc(stored, 16)
            s.wait_ge(v_done, 4 + 6 * SJ)
            s.dma_start(m.reld.rearrange("(j p) e -> p j e", p=SP_), rel).then_inc(stored, 16)
            s.dma_start(m.wind.rearrange("(j p) -> p j", p=SP_), wint).then_inc(stored, 16)
            s.wait_ge(stored, 48)
            s.dma_start(m.win[:, :], m.wind.rearrange("(a s) -> a s", a=1)).then_inc(rows_in, 16)
            s.wait_ge(rows_in, 48)

        @block.gpsimd
        def _(g):
            g.iota(scol, [[SP_, SJ]], base=0, channel_multiplier=1, allow_small_or_imprecise_dtypes=True).then_inc(iotas, 1)
            g.iota(io, [[1, t]], base=0, channel_multiplier=0, allow_small_or_imprecise_dtypes=True).then_inc(iotas, 1)
            g.wait_ge(idx_ready, 1)
            for j in range(SJ):
                g.indirect_dma_start(gr[:, j, :], None, m.edg, bass.IndirectOffsetOnAxis(ap=iint[:, j:j + 1], axis=0)).then_inc(rows_got, 16)

        @block.vector
        def _(v):
            q = slice(0, ERP)
            v.wait_ge(ends_in, 32)
            v.tensor_copy(m.abi[q, :, :], m.ab[q, :, :]).then_inc(ends, 1)
            v.wait_ge(ends, 1)
            v.tensor_scalar(m.abi[q, :, :], m.abi[q, :, :], P.bit_length() - 1, None, ALU.arith_shift_right).then_inc(ends, 1)
            v.wait_ge(ends, 2)
            v.tensor_copy(m.ab[q, :, :], m.abi[q, :, :]).then_inc(ends, 1)
            v.wait_ge(ends, 3)
            v.scalar_tensor_tensor(m.ab[q, 1, :], m.ab[q, 1, :], 1.0, m.ab[q, 0, :], ALU.add, ALU.subtract).then_inc(ends, 1)
            v.wait_ge(rows_in, 32)
            v.wait_ge(iotas, 2)
            v.tensor_tensor_scan(pin, m.ones[:, 0:1].broadcast_to([P, t]), ln, 0.0, ALU.mult, ALU.add).then_inc(v_done, 1)
            v.tensor_tensor(dif, aw, ln, ALU.add).then_inc(v_done, 1)
            v.wait_ge(v_done, 2)
            v.tensor_tensor(dif, dif, pin, ALU.subtract).then_inc(v_done, 1)
            for j in range(SJ):
                v.wait_ge(v_done, 3 + j)
                v.tensor_scalar(junk[0:SP_], pin[0:SP_], scol[:, j:j + 1], 0.0, ALU.is_le, ALU.add,
                                accum_out=icol[:, j:j + 1]).then_inc(v_done, 1)
            v.wait_ge(v_done, 3 + SJ)
            v.tensor_scalar(icol, icol, float(t - 1), None, ALU.min).then_inc(v_done, 1)
            v.wait_ge(v_done, 4 + SJ)
            v.tensor_copy(iint, icol).then_inc(idx_ready, 1)
            for j in range(SJ):
                v.wait_ge(v_done, 4 + SJ + j)
                v.scalar_tensor_tensor(junk[0:SP_], io[0:SP_], icol[:, j:j + 1], dif[0:SP_], ALU.is_equal, ALU.mult,
                                       accum_out=vcol[:, j:j + 1]).then_inc(v_done, 1)
            v.wait_ge(v_done, 4 + 2 * SJ)
            v.tensor_tensor(wcol, vcol, scol, ALU.add).then_inc(v_done, 1)
            v.wait_ge(v_done, 5 + 2 * SJ)
            v.tensor_scalar(ncol, wcol, -float(P), None, ALU.mult).then_inc(v_done, 1)
            v.tensor_scalar(wcol, wcol, float(NT - 1), None, ALU.min).then_inc(v_done, 1)
            v.wait_ge(v_done, 7 + 2 * SJ)
            v.tensor_copy(wint, wcol).then_inc(v_done, 1)
            v.wait_ge(rows_got, 16 * SJ)
            for j in range(SJ):
                v.tensor_scalar(rel[:, j, :], gr[:, j, 0:P], ncol[:, j:j + 1], None, ALU.add).then_inc(v_done, 1)
            for j in range(SJ):
                v.wait_ge(turned, j + 1)
                last = None
                for f, tab in enumerate(tabs):
                    last = v.tensor_copy(tab[:, j * SP_:(j + 1) * SP_], m.ps[j % 2][:, f * SP_:(f + 1) * SP_])
                    if f < 3:
                        last.then_inc(v_done, 1)
                last.then_inc(copied, 1)

        @block.tensor
        def _(pe):
            pe.wait_ge(v_done, 8 + 3 * SJ)
            for j in range(SJ):
                if j >= 2:
                    pe.wait_ge(copied, j - 1)
                for f in range(4):
                    src = rel[:, j, :] if f == 0 else gr[:, j, f * P:(f + 1) * P]
                    last = pe.transpose(m.ps[j % 2][:, f * SP_:(f + 1) * SP_], src, m.ident[0:SP_, 0:SP_])
                last.then_inc(turned, 1)


def normalise(nc, ctx, m, name, src, dst, gain=None, shift=None, relu=False, before=None, nbefore=0, loads=(),
              spill=None, after=None):
    sem = lambda n: semaphore(nc, m, f"{name}_{n}")
    done, stats_in, root_done, loaded, stored = (sem(n) for n in ("vector", "variance", "root", "loaded", "stored"))
    st, mean, var, rstd, tmp = m.st, m.mean, m.var, m.rstd, m.tmp
    with nc.Block() as block:
        @block.sync
        def _(s):
            for d, x in loads:
                s.dma_start(d, x).then_inc(loaded, 16)
            if gain is not None:
                s.dma_start(m.VG[:, :], gain.partition_broadcast(P)).then_inc(loaded, 16)
                s.dma_start(m.VB[:, :], shift.partition_broadcast(P)).then_inc(loaded, 16)
            if spill is not None:
                s.wait_ge(done, nbefore)
                s.dma_start(spill.rearrange("(t p) d -> p t d", p=P), src).then_inc(stored, 16)
                s.wait_ge(stored, 16)

        @block.scalar
        def _(s):
            s.wait_ge(stats_in, 1)
            s.activation(rstd[:, :], var[:, :], ACT.Sqrt).then_inc(root_done, 1)

        @block.vector
        def _(v):
            n = 16 * (len(loads) + (2 if gain is not None else 0))
            if n:
                v.wait_ge(loaded, n)
            if before is not None:
                before(v, done)
                v.wait_ge(done, nbefore)
            c = nbefore
            with v.Fori(0, NT) as t:
                v.bn_stats(at(st, t), at(src, t)).then_inc(done, 1)
            c += NT
            v.wait_ge(done, c)
            v.tensor_tensor(tmp[:, :], st[:, :, 1], st[:, :, 4], ALU.subtract).then_inc(done, 1)
            v.tensor_tensor(mean[:, :], st[:, :, 1], st[:, :, 4], ALU.add).then_inc(done, 1)
            v.tensor_tensor(var[:, :], st[:, :, 2], st[:, :, 5], ALU.add).then_inc(done, 1)
            v.wait_ge(done, c + 3)
            v.tensor_tensor(tmp[:, :], tmp[:, :], tmp[:, :], ALU.mult).then_inc(done, 1)
            v.tensor_scalar(mean[:, :], mean[:, :], 0.5, None, ALU.mult).then_inc(done, 1)
            v.tensor_scalar(var[:, :], var[:, :], 1.0 / D, EPS, ALU.mult, ALU.add).then_inc(done, 1)
            v.wait_ge(done, c + 6)
            v.scalar_tensor_tensor(var[:, :], tmp[:, :], 0.25, var[:, :], ALU.mult, ALU.add).then_inc(stats_in, 1)
            v.wait_ge(root_done, 1)
            v.reciprocal(rstd[:, :], rstd[:, :]).then_inc(done, 1)
            c += 7
            v.wait_ge(done, c)
            if spill is not None:
                v.wait_ge(stored, 16)
            with v.Fori(0, NT) as t:
                v.tensor_scalar(at(dst, t), at(src, t), col(mean, t), col(rstd, t), ALU.subtract, ALU.mult).then_inc(done, 1)
            c += NT
            v.wait_ge(done, c)
            if gain is not None:
                v.tensor_tensor(dst, dst, m.VG[:, :].unsqueeze(1).broadcast_to([P, NT, D]), ALU.mult).then_inc(done, 1)
                v.wait_ge(done, c + 1)
                v.tensor_tensor(dst, dst, m.VB[:, :].unsqueeze(1).broadcast_to([P, NT, D]), ALU.add).then_inc(done, 1)
                c += 2
                v.wait_ge(done, c)
            if relu:
                v.tensor_scalar(dst, dst, 0.0, None, ALU.max).then_inc(done, 1)
                c += 1
                v.wait_ge(done, c)
            if after is not None:
                after(v, done, c)


def relation_weights(nc, ctx, m, l, basis, att, root):
    sem = lambda n: semaphore(nc, m, f"rw{l}_{n}")
    loaded, mixed = sem("loaded"), sem("mixed")
    bs = m.SC[:, 0:B * C2 * D].rearrange("p (b c o) -> p b c o", b=B, c=C2)
    wt = m.WT.rearrange("p (c r o) -> p c r o", c=C2, r=R)
    with nc.Block() as block:
        @block.sync
        def _(s):
            for b in range(B):
                s.dma_start(bs[:, b], basis[b].rearrange("(c p) o -> p c o", p=P)).then_inc(loaded, 16)
            s.dma_start(m.ROOT, root.rearrange("(c p) o -> p c o", p=P)).then_inc(loaded, 16)
            s.dma_start(m.ATT[:, :], att.rearrange("r b -> (r b)").partition_broadcast(P)).then_inc(loaded, 16)
            s.wait_ge(loaded, 16 * (B + 2))

        @block.vector
        def _(v):
            v.wait_ge(loaded, 16 * (B + 2))
            for b in range(B):
                for r in range(R):
                    w = m.ATT[:, r * B + b:r * B + b + 1]
                    if b == 0:
                        v.tensor_scalar(wt[:, :, r, :], bs[:, b], w, None, ALU.mult).then_inc(mixed, 1)
                    else:
                        v.wait_ge(mixed, (b - 1) * R + r + 1)
                        v.scalar_tensor_tensor(wt[:, :, r, :], bs[:, b], w, wt[:, :, r, :], ALU.mult, ALU.add).then_inc(mixed, 1)


def relation_product(nc, ctx, m, l):
    sem = lambda n: semaphore(nc, m, f"rp{l}_{n}")
    staged, turned, turn_free, group_done, group_read, root_done, root_read = (sem(n) for n in (
        "staged", "turned", "turn_read", "group_done", "group_read", "root_done", "root_read"))
    stored = [sem(f"stored{g}") for g in range(4)]
    wt = m.WT.rearrange("p (c r o) -> p c r o", c=C2, r=R)
    hst = m.SC[:, 0:4 * 1024].rearrange("p (g n) -> p g n", g=4)
    hs = m.SC[:, 4096:4096 + 512].rearrange("p (k d) -> p k d", k=2)
    ht = m.SC[:, 4608:4608 + 512].rearrange("p (k c n) -> p k c n", k=2, c=C2)
    psT, psR = (m.ps[4], m.ps[6]), (m.ps[5], m.ps[7])
    with nc.Block() as block:
        @block.gpsimd
        def _(g):
            def body(t, k, last):
                g.wait_ge(turned, t + 1)
                g.tensor_copy(hs[:, k, :], at(m.HB, t)).then_inc(staged, 1)
            tiles(g, body)

        @block.tensor
        def _(pe):
            pe.sem_inc(turned, 2)
            pe.sem_inc(root_done, 2)

            def turn(t, k):
                pe.wait_ge(staged, t + 1)
                pe.wait_ge(turn_free, t + 1)
                for c in range(C2):
                    last = pe.transpose(psT[k][:, c * P:(c + 1) * P], hs[:, k, c * P:(c + 1) * P], m.ident[:, :])
                last.then_inc(turned, 1)

            def group(t, k, g):
                pe.wait_ge(group_read, t * 4 + g + 1)
                for c in range(C2):
                    for b in range(2):
                        r = 4 * g + 2 * b
                        last = pe.matmul(m.ps[2 * (g % 2) + b][:, :], ht[:, k, c, :],
                                         wt[:, c, r:r + 2, :].rearrange("p r o -> p (r o)"), start=(c == 0), stop=(c == 1))
                last.then_inc(group_done, 1)

            turn(0, 0)

            def body(t, k, last):
                pe.wait_ge(turn_free, t + 3)
                group(t, k, 0)
                group(t, k, 1)
                if not last:
                    turn(t + 1, 1 - k)
                group(t, k, 2)
                group(t, k, 3)
                pe.wait_ge(root_read, t + 1)
                for c in range(C2):
                    mm = pe.matmul(psR[k][:, 0:D], ht[:, k, c, :], m.ROOT[:, c, :], start=(c == 0), stop=(c == 1))
                mm.then_inc(root_done, 1)
            tiles(pe, body)

        @block.scalar
        def _(s):
            s.sem_inc(group_read, 2)

            def body(t, k, last):
                for g in range(4):
                    s.wait_ge(group_done, t * 4 + g + 1)
                    s.wait_ge(stored[g], t * 16 + 16)
                    for b in range(2):
                        if g == 3 and b == 1:
                            s.activation(at(m.AGG3, t)[:, 0:D], m.ps[3][:, D:2 * D], ACT.Copy)
                        mm = s.activation(hst[:, g, b * 512:(b + 1) * 512], m.ps[2 * (g % 2) + b][:, :], ACT.Copy)
                    mm.then_inc(group_read, 1)
            tiles(s, body)

        @block.vector
        def _(v):
            v.sem_inc(turn_free, 2)
            v.sem_inc(root_read, 2)

            def turn_out(t, k):
                v.wait_ge(turned, t + 3)
                v.wait_ge(root_done, t + 1)
                v.tensor_copy(ht[:, k].rearrange("p c n -> p (c n)"), psT[k][:, 0:D]).then_inc(turn_free, 1)

            turn_out(0, 0)

            def body(t, k, last):
                if not last:
                    turn_out(t + 1, 1 - k)
                v.wait_ge(root_done, t + 3)
                v.tensor_tensor(at(m.HB, t), psR[k][:, 0:D], at(m.HB, t), ALU.add).then_inc(root_read, 1)
            tiles(v, body)

        @block.sync
        def _(s):
            for g in range(4):
                s.sem_inc(stored[g], 16)

            def body(t, k, last):
                for g in range(4):
                    s.wait_ge(group_read, t * 4 + g + 3)
                    s.dma_start(m.hrel[bass.ds(t * P, P), g * 1024:(g + 1) * 1024], hst[:, g, :]).then_inc(stored[g], 16)
            tiles(s, body)
            for g in range(4):
                s.wait_ge(stored[g], 16 * (NT + 1))


def relation_sum(nc, ctx, m, l):
    sem = lambda n: semaphore(nc, m, f"rs{l}_{n}")
    idx_ready, scaled, onehot, summed, added = (sem(n) for n in ("idx", "scaled", "onehot", "summed", "added"))
    asked = sem("asked")
    landed = [sem(f"landed{k}") for k in range(BATCH)]
    init = sem("init")
    rows = m.hrel.rearrange("n (r o) -> (n r) o", r=R)
    g8 = m.G.rearrange("p (k d) -> p k d", k=BATCH)
    gs, oh, ix = m.GS, m.OH, m.IX
    with nc.Block() as block:
        @block.scalar
        def _(s):
            s.sem_inc(scaled, BATCH)
            for k in range(BATCH):
                s.activation(gs[:, k, D:D + 1], m.ones[:, 0:1], ACT.Copy).then_inc(init, 1)
            s.activation(ix[:, 0, :], m.TCI[:, 0:BATCH], ACT.Copy).then_inc(idx_ready, 1)

            def body(b, q, last):
                if not last:
                    s.activation(ix[:, 1 - q, :], m.TCI[:, bass.ds(b * BATCH + BATCH, BATCH)], ACT.Copy).then_inc(idx_ready, 1)
                for k in range(BATCH):
                    st = b * BATCH + k
                    s.wait_ge(landed[k], b * 16 + 16)
                    s.wait_ge(summed, st + 1)
                    s.activation(gs[:, k, 0:D], g8[:, k, :], ACT.Copy, scale=col(m.TEA, st)).then_inc(scaled, 1)
            batches(s, body)

        @block.gpsimd
        def _(g):
            def body(b, q, last):
                g.wait_ge(idx_ready, b + 1)
                for k in range(BATCH):
                    g.wait_ge(scaled, b * BATCH + k + 1)
                    g.sem_inc(asked, 1)
                    g.indirect_dma_start(g8[:, k, :], None, rows, bass.IndirectOffsetOnAxis(ap=ix[:, q, k:k + 1], axis=0)).then_inc(landed[k], 16)
            batches(g, body)

        @block.vector
        def _(v):
            v.sem_inc(added, BATCH)
            if l == 1:
                v.memset(m.AGG3[:, :, D:D + 1], 1.0)
            one_hots(v, m, 0, 0, onehot)

            def body(b, q, last):
                if not last:
                    one_hots(v, m, b + 1, 1 - q, onehot)
                add_windows(v, m, b, summed, added, D + 1 if l == 1 else D)
            batches(v, body)

        @block.tensor
        def _(pe):
            pe.sem_inc(summed, BATCH)
            pe.wait_ge(init, BATCH)

            def body(b, q, last):
                pe.wait_ge(onehot, b + 1)
                for k in range(BATCH):
                    st = b * BATCH + k
                    pe.wait_ge(scaled, st + 1 + BATCH)
                    pe.wait_ge(added, st + 1)
                    pe.matmul(m.ps[k][:, 0:D + 1], oh[:, q, k, :], gs[:, k, 0:D + 1], start=True, stop=True).then_inc(summed, 1)
            batches(pe, body)


def one_hots(v, m, b, q, onehot):
    v.tensor_tensor(m.OH[:, q], m.iota[:, :].unsqueeze(1).broadcast_to([P, BATCH, P]),
                    m.TDR[:, bass.ds(b * BATCH, BATCH)].unsqueeze(2).broadcast_to([P, BATCH, P]), ALU.is_equal).then_inc(onehot, 1)


def add_window(v, m, b, k, summed, added, width):
    st = b * BATCH + k
    w = v.value_load(m.win[0:1, bass.ds(st, 1)], min_val=0, max_val=NT - 1)
    v.wait_ge(summed, st + 1 + BATCH)
    v.wait_ge(added, st + BATCH)
    acc = at(m.AGG3, w)[:, 0:width]
    v.tensor_tensor(acc, m.ps[k][:, 0:width], acc, ALU.add).then_inc(added, 1)


def add_windows(v, m, b, summed, added, width):
    for k in range(BATCH):
        add_window(v, m, b, k, summed, added, width)


def select_rows(nc, ctx, m, a):
    sem = lambda n: semaphore(nc, m, f"sl_{n}")
    loaded, done, pe_done, stored, sgn, iot = (sem(n) for n in ("loaded", "vector", "tensor", "stored", "roots", "iota"))
    W = m.MW
    s = m.small
    all_w = m.WT[:, 0:NP]
    key = m.SC[:, 0:NP]
    cnt, kk, m1, b1, T, cand, fl, tf = (s[:, i:i + 1] for i in range(8))
    Ti, ci, ii, one_i = (m.smalli[:, i:i + 1] for i in range(4))
    eq, gt, pre, off = (m.SEL[:, i * NT:(i + 1) * NT] for i in range(4))
    shifts = ((24, 7), (18, 6), (12, 6), (6, 6), (0, 6))
    wrb = m.VG
    with nc.Block() as block:
        @block.gpsimd
        def _(g):
            g.iota(ii, [[0, 1]], base=0, channel_multiplier=1).then_inc(iot, 1)

        @block.sync
        def _(e):
            e.dma_start(wrb[:, :], a["L0_ffn_wr"].rearrange("d o -> (d o)").partition_broadcast(P)).then_inc(loaded, 16)
            e.dma_start(b1, a["L0_ffn_br"].partition_broadcast(P)).then_inc(loaded, 16)
            e.wait_ge(done, NT + 4)
            e.dma_start(m.wd.rearrange("(t p) -> p t", p=P), m.SEL[:, 0:NT]).then_inc(stored, 16)
            e.wait_ge(stored, 16)
            e.dma_start(all_w, m.wd.partition_broadcast(P)).then_inc(loaded, 16)

        @block.vector
        def _(v):
            c = [0]

            def step(ins):
                c[0] += 1
                ins.then_inc(done, 1)
                v.wait_ge(done, c[0])
            v.wait_ge(loaded, 32)
            v.wait_ge(iot, 1)
            junk = m.SC[:, 0:D]
            with v.Fori(0, NT) as t:
                v.tensor_tensor(junk, at(m.HB, t), wrb[:, :], ALU.mult).then_inc(sgn, 1)
                v.wait_ge(sgn, t + 1)
                v.tensor_reduce(col(W, t), junk, AX, ALU.add).then_inc(done, 1)
                v.wait_ge(done, t + 1)
            c[0] = NT
            step(v.tensor_scalar(W, W, b1, None, ALU.add))
            step(v.tensor_tensor(eq, W, m.valid[:, :], ALU.mult))
            step(v.tensor_scalar(gt, m.valid[:, :], 1.0, BIG, ALU.subtract, ALU.mult))
            step(v.tensor_tensor(eq, eq, gt, ALU.add))
            v.wait_ge(loaded, 48)
            step(v.tensor_scalar(key, all_w, 0.0, 0.0, ALU.is_ge, ALU.add, accum_out=cnt))
            step(v.tensor_scalar(m1, cnt, float(TOPK), None, ALU.is_ge))
            step(v.tensor_scalar(fl, m1, 2.0, 1.0, ALU.mult, ALU.subtract))
            step(v.tensor_scalar(kk, m1, float(2 * TOPK - N - 1), float(N + 1 - TOPK), ALU.mult, ALU.add))
            step(v.tensor_scalar(key, all_w, fl, None, ALU.mult))
            step(v.tensor_scalar(key[:, N:NP], all_w[:, N:NP], 1.0, None, ALU.mult))
            step(v.memset(Ti, 0))
            for n, (sh, bits) in enumerate(shifts):
                step(v.tensor_scalar(ci, ii, (1 << bits) - 1, sh, ALU.bitwise_and, ALU.logical_shift_left))
                step(v.tensor_tensor(ci, ci, Ti, ALU.bitwise_or))
                step(v.tensor_scalar(m.SC2, key, ci.bitcast(F32), 0.0, ALU.is_ge, ALU.add, accum_out=cnt))
                step(v.tensor_tensor(tf, cnt, kk, ALU.is_ge))
                v.wait_ge(pe_done, n + 1)
                step(v.tensor_scalar(tf, m.ps[0][:, 0:1], float(1 << bits) / P, -1.0, ALU.mult, ALU.add))
                step(v.tensor_copy(one_i, tf))
                step(v.tensor_scalar(one_i, one_i, sh, None, ALU.logical_shift_left))
                step(v.tensor_tensor(Ti, Ti, one_i, ALU.bitwise_or))
            step(v.tensor_scalar(T, Ti.bitcast(F32), fl, None, ALU.mult))
            step(v.tensor_scalar(gt, m.SEL[:, 0:NT], T, None, ALU.is_gt))
            step(v.tensor_reduce(cnt, gt, AX, ALU.add))
            step(v.tensor_scalar(eq, m.SEL[:, 0:NT], T, None, ALU.is_equal))
            v.wait_ge(pe_done, 6)
            step(v.tensor_copy(pre, m.ps[1][:, 0:NT]))
            step(v.tensor_copy(off, m.ps[1][:, 64:64 + NT]))
            step(v.tensor_copy(kk, m.ps[1][:, 128:129]))
            step(v.tensor_tensor_scan(m.tmp[:, :], m.ones[:, 0:1].broadcast_to([P, NT]), off, 0.0, ALU.mult, ALU.add))
            step(v.tensor_tensor(m.tmp[:, :], m.tmp[:, :], off, ALU.subtract))
            step(v.tensor_tensor(pre, pre, m.tmp[:, :], ALU.add))
            step(v.tensor_scalar(kk, kk, -1.0, float(TOPK), ALU.mult, ALU.add))
            step(v.tensor_scalar(pre, pre, kk, None, ALU.is_lt))
            step(v.tensor_tensor(eq, eq, pre, ALU.mult))
            step(v.tensor_tensor(eq, eq, gt, ALU.add))
            step(v.tensor_tensor(W, W, eq, ALU.mult))

        @block.tensor
        def _(pe):
            base = NT + 11
            for n in range(len(shifts)):
                pe.wait_ge(done, base + 8 * n + 4)
                pe.matmul(m.ps[0][:, 0:1], m.ones[:, :], tf, start=True, stop=True).then_inc(pe_done, 1)
            pe.wait_ge(done, base + 8 * len(shifts) + 4)
            pe.matmul(m.ps[1][:, 0:NT], m.upper[:, :], eq, start=True, stop=True)
            pe.matmul(m.ps[1][:, 64:64 + NT], m.ones[:, :], eq, start=True, stop=True)
            pe.matmul(m.ps[1][:, 128:129], m.ones[:, :], cnt, start=True, stop=True).then_inc(pe_done, 1)


def feed_forward(nc, ctx, m, name, src, w1, b1, w2, b2, act, out_steps, nout):
    sem = lambda n: semaphore(nc, m, f"{name}_{n}")
    loaded, staged, turned, turn_read, up, gelu, down, outs = (sem(n) for n in (
        "loaded", "staged", "turned", "turn_read", "up", "gelu", "down", "outs"))
    F = DFF // P
    W1 = m.WT[:, 0:C2 * DFF].rearrange("p (c f) -> p c f", c=C2)
    W2 = m.WT[:, 2048:2048 + F * D].rearrange("p (f d) -> p f d", f=F)
    hid = m.SC[:, 0:2 * DFF].rearrange("p (k f n) -> p k f n", k=2, f=F)
    hs = m.SC[:, 4096:4096 + 512].rearrange("p (k d) -> p k d", k=2)
    ht = m.SC[:, 4608:4608 + 512].rearrange("p (k c n) -> p k c n", k=2, c=C2)
    b1c = m.small[:, 0:F]
    psT, psY = (m.ps[4], m.ps[6]), (m.ps[5], m.ps[7])
    with nc.Block() as block:
        @block.sync
        def _(s):
            s.dma_start(W1, w1.rearrange("(c p) f -> p c f", p=P)).then_inc(loaded, 16)
            s.dma_start(W2, w2.rearrange("(f p) d -> p f d", p=P)).then_inc(loaded, 16)
            s.dma_start(b1c, b1.rearrange("(f p) -> p f", p=P)).then_inc(loaded, 16)
            s.dma_start(m.VB[:, :], b2.partition_broadcast(P)).then_inc(loaded, 16)

        @block.gpsimd
        def _(g):
            def body(t, k, last):
                g.wait_ge(turned, t + 1)
                g.tensor_copy(hs[:, k, :], at(src, t)).then_inc(staged, 1)
            tiles(g, body)

        @block.tensor
        def _(pe):
            pe.wait_ge(loaded, 64)
            pe.sem_inc(turned, 2)
            pe.sem_inc(down, 2)

            def turn(t, k):
                pe.wait_ge(staged, t + 1)
                pe.wait_ge(turn_read, t + 1)
                for c in range(C2):
                    last = pe.transpose(psT[k][:, c * P:(c + 1) * P], hs[:, k, c * P:(c + 1) * P], m.ident[:, :])
                last.then_inc(turned, 1)

            turn(0, 0)

            def body(t, k, last):
                pe.wait_ge(turn_read, t + 3)
                for f in range(F):
                    if f % 4 == 0:
                        pe.wait_ge(gelu, t * F + f + 4)
                    for c in range(C2):
                        mm = pe.matmul(m.ps[2 * k + f // 4][:, (f % 4) * P:(f % 4 + 1) * P], W1[:, c, f * P:(f + 1) * P], ht[:, k, c, :],
                                       start=(c == 0), stop=(c == 1))
                    if f % 4 == 3:
                        mm.then_inc(up, 1)
                if not last:
                    turn(t + 1, 1 - k)
                pe.wait_ge(outs, t * nout + 1)
                for f in range(F):
                    pe.wait_ge(gelu, t * F + f + 1 + 2 * F)
                    mm = pe.matmul(psY[k][:, 0:D], hid[:, k, f, :], W2[:, f, :], start=(f == 0), stop=(f == F - 1))
                mm.then_inc(down, 1)
            tiles(pe, body)

        @block.scalar
        def _(s):
            s.wait_ge(loaded, 64)
            s.sem_inc(gelu, 2 * F)

            def body(t, k, last):
                s.wait_ge(down, t + 1)
                for f in range(F):
                    if f % 4 == 0:
                        s.wait_ge(up, t * 2 + f // 4 + 1)
                    s.activation(hid[:, k, f, :], m.ps[2 * k + f // 4][:, (f % 4) * P:(f % 4 + 1) * P], act, bias=b1c[:, f:f + 1]).then_inc(gelu, 1)
            tiles(s, body)

        @block.vector
        def _(v):
            v.wait_ge(loaded, 64)
            v.sem_inc(turn_read, 2)
            v.sem_inc(outs, 2 * nout)

            def turn_out(t, k):
                v.wait_ge(turned, t + 3)
                v.wait_ge(down, t + 1)
                v.tensor_copy(ht[:, k].rearrange("p c n -> p (c n)"), psT[k][:, 0:D]).then_inc(turn_read, 1)

            turn_out(0, 0)

            def body(t, k, last):
                if not last:
                    turn_out(t + 1, 1 - k)
                v.wait_ge(down, t + 3)
                out_steps(v, t, psY[k][:, 0:D], outs)
            tiles(v, body)


def make_qkv(nc, ctx, m, a):
    sem = lambda n: semaphore(nc, m, f"qkv_{n}")
    loaded, staged, turned, turn_read, prod, q_out, kv_out, scaled = (sem(n) for n in (
        "loaded", "staged", "turned", "turn_read", "product", "q_out", "kv_out", "scaled"))
    stored = [sem(f"stored{k}") for k in range(2)]
    W = m.WT[:, 0:C2 * 3 * D].rearrange("p (c f) -> p c f", c=C2)
    bq = m.WT[:, 1536:1536 + 3 * D]
    hs = m.SC[:, 4096:4096 + 512].rearrange("p (k d) -> p k d", k=2)
    ht = m.SC[:, 4608:4608 + 512].rearrange("p (k c n) -> p k c n", k=2, c=C2)
    qv = m.SC[:, 0:4 * D].rearrange("p (k j d) -> p k j d", k=2, j=2)
    qr = m.SC[:, 1024:1024 + 2 * D].rearrange("p (k d) -> p k d", k=2)
    psT = (m.ps[4], m.ps[6])
    with nc.Block() as block:
        @block.sync
        def _(s):
            s.dma_start(W, a["L1_gnn_Wqkv"].rearrange("(c p) f -> p c f", p=P)).then_inc(loaded, 16)
            s.dma_start(bq, a["L1_gnn_bqkv"].partition_broadcast(P)).then_inc(loaded, 16)
            for k in range(2):
                s.sem_inc(stored[k], 32)

            def body(t, k, last):
                s.wait_ge(scaled, t + 1)
                s.dma_start(m.qt[bass.ds(t * P, P), :], qv[:, k, 0, :]).then_inc(stored[k], 16)
                s.wait_ge(kv_out, t * 2 + 2)
                s.dma_start(m.vt[bass.ds(t * P, P), :], qv[:, k, 1, :]).then_inc(stored[k], 16)
            tiles(s, body)
            s.wait_ge(stored[0], 32 * (NT // 2 + 2))
            s.wait_ge(stored[1], 32 * (NT // 2 + 1))

        @block.gpsimd
        def _(g):
            def body(t, k, last):
                g.wait_ge(turned, t + 1)
                g.tensor_copy(hs[:, k, :], at(m.HB, t)).then_inc(staged, 1)
            tiles(g, body)

        @block.tensor
        def _(pe):
            pe.wait_ge(loaded, 32)
            pe.sem_inc(turned, 2)
            pe.sem_inc(prod, 2)

            def turn(t, k):
                pe.wait_ge(staged, t + 1)
                pe.wait_ge(turn_read, t + 1)
                for c in range(C2):
                    last = pe.transpose(psT[k][:, c * P:(c + 1) * P], hs[:, k, c * P:(c + 1) * P], m.ident[:, :])
                last.then_inc(turned, 1)

            turn(0, 0)

            def body(t, k, last):
                if not last:
                    turn(t + 1, 1 - k)
                pe.wait_ge(turn_read, t + 3)
                pe.wait_ge(q_out, t + 1)
                for n, (lo, hi) in enumerate(((0, 512), (512, 768))):
                    for c in range(C2):
                        mm = pe.matmul(m.ps[2 * k + n][:, 0:hi - lo], ht[:, k, c, :], W[:, c, lo:hi], start=(c == 0), stop=(c == 1))
                mm.then_inc(prod, 1)
            tiles(pe, body)

        @block.scalar
        def _(s):
            def body(t, k, last):
                s.wait_ge(q_out, t + 3)
                s.activation(qv[:, k, 0, :], qr[:, k, :], ACT.Copy, scale=float(D) ** -0.5).then_inc(scaled, 1)
            with s.Fori(0, (NT - 1) // 2) as i:
                for k in range(2):
                    s.wait_ge(stored[k], i * 32 + 32)
                    body(i * 2 + k, k, False)
            s.wait_ge(stored[0], 32 * (NT // 2 + 1))
            body(NT - 1, 0, True)

        @block.vector
        def _(v):
            v.wait_ge(loaded, 32)
            v.sem_inc(turn_read, 2)
            v.sem_inc(q_out, 2)

            def turn_out(t, k):
                v.wait_ge(turned, t + 3)
                v.wait_ge(prod, t + 1)
                v.tensor_copy(ht[:, k].rearrange("p c n -> p (c n)"), psT[k][:, 0:D]).then_inc(turn_read, 1)

            turn_out(0, 0)

            def body(t, k, last, i):
                if not last:
                    turn_out(t + 1, 1 - k)
                v.wait_ge(prod, t + 3)
                v.wait_ge(stored[k], i * 32 + 32)
                v.tensor_tensor(at(m.HB, t), m.ps[2 * k][:, D:2 * D], bq[:, D:2 * D], ALU.add).then_inc(kv_out, 1)
                v.tensor_tensor(qv[:, k, 1, :], m.ps[2 * k + 1][:, 0:D], bq[:, 2 * D:3 * D], ALU.add).then_inc(kv_out, 1)
                v.tensor_tensor(qr[:, k, :], m.ps[2 * k][:, 0:D], bq[:, 0:D], ALU.add).then_inc(q_out, 1)
            with v.Fori(0, (NT - 1) // 2) as i:
                for k in range(2):
                    body(i * 2 + k, k, False, i)
            body(NT - 1, 0, True, NT // 2)


def edge_scores(nc, ctx, m):
    sem = lambda n: semaphore(nc, m, f"es_{n}")
    idx_ready, onehot, turned, turn_out, keys, mult, reduced = (sem(n) for n in (
        "idx", "onehot", "turned", "turn_out", "keys", "multiplied", "reduced"))
    asked = sem("asked")
    landed = [sem(f"landed{k}") for k in range(BATCH)]
    g8 = m.G.rearrange("p (k d) -> p k d", k=BATCH)
    oh, ix = m.OH, m.IX
    oht = m.GS.rearrange("p k d -> p (k d)")[:, 0:2 * 4 * P].rearrange("p (u k e) -> p u k e", u=2, k=4)
    pr = m.WT[:, 0:8 * D].rearrange("p (u k d) -> p u k d", u=2, k=4)
    sc3 = m.SC.rearrange("p (s h) -> p s h", h=H)
    NU = STEPS // 4
    psT = [m.ps[4], m.ps[5]]
    with nc.Block() as block:
        @block.scalar
        def _(s):
            s.sem_inc(turn_out, 2)

            def evac(u, w):
                s.wait_ge(turned, u + 1)
                s.wait_ge(keys, u * 4 + 1)
                s.activation(oht[:, w].rearrange("p k e -> p (k e)"), psT[w][:, :], ACT.Copy).then_inc(turn_out, 1)

            s.activation(ix[:, 0, :], m.TSI[:, 0:BATCH], ACT.Copy).then_inc(idx_ready, 1)
            evac(0, 0)

            def body(b, q, last):
                if not last:
                    s.wait_ge(mult, b * BATCH + BATCH)
                    s.activation(ix[:, 1 - q, :], m.TSI[:, bass.ds(b * BATCH + BATCH, BATCH)], ACT.Copy).then_inc(idx_ready, 1)
                evac(b * 2 + 1, 1)
                if not last:
                    evac(b * 2 + 2, 0)
            batches(s, body)

        @block.gpsimd
        def _(g):
            def body(b, q, last):
                g.wait_ge(idx_ready, b + 1)
                for k in range(BATCH):
                    g.wait_ge(mult, b * BATCH + k + 1)
                    g.sem_inc(asked, 1)
                    g.indirect_dma_start(g8[:, k, :], None, m.qt, bass.IndirectOffsetOnAxis(ap=ix[:, q, k:k + 1], axis=0)).then_inc(landed[k], 16)
            batches(g, body)

        @block.tensor
        def _(pe):
            pe.sem_inc(keys, 8)

            def turn(u, w, q, half):
                pe.wait_ge(turn_out, u + 1)
                for k in range(4):
                    mm = pe.transpose(psT[w][:, k * P:(k + 1) * P], oh[:, q, 4 * half + k, :], m.ident[:, :])
                mm.then_inc(turned, 1)

            def unit(b, u, w):
                pe.wait_ge(turn_out, u + 3)
                for k in range(4):
                    st = u * 4 + k
                    win = pe.value_load(m.win[0:1, bass.ds(st, 1)], min_val=0, max_val=NT - 1)
                    pe.wait_ge(mult, st + 5)
                    pe.matmul(m.ps[k][:, 0:D], oht[:, w, k, :], at(m.HB, win), start=True, stop=True).then_inc(keys, 1)

            pe.wait_ge(onehot, 1)
            turn(0, 0, 0, 0)

            def body(b, q, last):
                turn(b * 2 + 1, 1, q, 1)
                unit(b, b * 2, 0)
                if not last:
                    pe.wait_ge(onehot, b + 2)
                    turn(b * 2 + 2, 0, 1 - q, 0)
                unit(b, b * 2 + 1, 1)
            batches(pe, body)

        @block.vector
        def _(v):
            v.sem_inc(mult, BATCH)
            one_hots(v, m, 0, 0, onehot)

            def body(b, q, last):
                if not last:
                    one_hots(v, m, b + 1, 1 - q, onehot)
                for k in range(BATCH):
                    st = b * BATCH + k
                    v.wait_ge(landed[k], b * 16 + 16)
                    v.wait_ge(keys, st + 9)
                    v.tensor_tensor(pr[:, k // 4, k % 4, :], m.ps[k % 4][:, 0:D], g8[:, k, :], ALU.mult).then_inc(mult, 1)
                    if k % 4 == 3:
                        v.wait_ge(mult, st + 9)
                        v.tensor_reduce(sc3[:, bass.ds(st - 3, 4), :].rearrange("p s h -> p (s h)"),
                                        pr[:, k // 4].rearrange("p k (h e) -> p (k h) e", h=H), AX, ALU.add).then_inc(reduced, 1)
            batches(v, body)


def edge_softmax(nc, ctx, m):
    sem = lambda n: semaphore(nc, m, f"sm_{n}")
    loaded, packed, turned, unturned, done, pe_done, expd, ready = (sem(n) for n in (
        "loaded", "packed", "turned", "unturned", "vector", "tensor", "exp", "ready"))
    L = CL + 8
    S, PEN, F, Bk = (m.R1[:, i * L:(i + 1) * L] for i in range(4))
    rel = F
    key = Bk
    stage = m.G.rearrange("p (k n) -> p k n", k=4)
    sc = m.SC.rearrange("p (c j h) -> p j h c", c=CH, j=CS)
    NG = CS // 4
    rowK = m.rows
    row = lambda i: rowK[0:1, i, :]
    cF, cB, cKf, cKl, cL, cR = (m.small[:, i:i + 1] for i in range(6))
    with nc.Block() as block:
        @block.sync
        def _(s):
            for h in range(H):
                s.dma_start(rel[h * CH:(h + 1) * CH, 0:CL], m.reld.rearrange("(c j) e -> c (j e)", c=CH)).then_inc(loaded, 16)
                s.dma_start(key[h * CH:(h + 1) * CH, 0:CL], m.keyd.rearrange("(c j) e -> c (j e)", c=CH)).then_inc(loaded, 16)

        @block.gpsimd
        def _(g):
            for i in range(NG):
                if i >= 2:
                    g.wait_ge(turned, i - 1)
                for k in range(4):
                    mm = g.tensor_copy(stage[:, i % 2, k * P:(k + 1) * P].rearrange("p (h c) -> p h c", h=H), sc[:, 4 * i + k])
                mm.then_inc(packed, 1)

        @block.tensor
        def _(pe):
            for i in range(NG):
                pe.wait_ge(packed, i + 1)
                if i >= 2:
                    pe.wait_ge(unturned, i - 1)
                for k in range(4):
                    mm = pe.transpose(m.ps[i % 2][:, k * P:(k + 1) * P], stage[:, i % 2, k * P:(k + 1) * P], m.ident[:, :])
                mm.then_inc(turned, 1)
            pe.wait_ge(ready, 1)
            for i, c in enumerate((cF, cB, cKf, cKl)):
                mm = pe.transpose(m.ps[4][0:1, i * P:(i + 1) * P], c, m.ident[:, :])
            mm.then_inc(pe_done, 1)
            pe.wait_ge(ready, 2)
            for i in range(2):
                mm = pe.matmul(m.ps[5][:, i:i + 1], row(8 + i), m.ones[0:1, 0:1], start=True, stop=True)
            mm.then_inc(pe_done, 1)
            for i in range(NG):
                pe.wait_ge(expd, i + 1)
                if i >= 2:
                    pe.wait_ge(unturned, NG + i - 1)
                for k in range(4):
                    mm = pe.transpose(m.ps[i % 2][:, k * P:(k + 1) * P], S[:, (4 * i + k) * P:(4 * i + k + 1) * P], m.ident[:, :])
                mm.then_inc(turned, 1)

        @block.scalar
        def _(s):
            for i in range(NG):
                s.wait_ge(turned, i + 1)
                s.activation(S[:, i * 512:(i + 1) * 512], m.ps[i % 2][:, :], ACT.Copy).then_inc(unturned, 1)
            s.wait_ge(ready, 3)
            for i in range(NG):
                s.activation(S[:, i * 512:(i + 1) * 512], S[:, i * 512:(i + 1) * 512], ACT.Exp).then_inc(expd, 1)

        @block.vector
        def _(v):
            c = [0]

            def step(ins, wait=True):
                c[0] += 1
                ins.then_inc(done, 1)
                if wait:
                    v.wait_ge(done, c[0])
            v.wait_ge(loaded, 16 * 2 * H)
            SS, FF, BB = S[:, 0:CL], F[:, 0:CL], Bk[:, 0:CL]
            p0, p1 = PEN[:, 0:CL], PEN[:, 1:CL + 1]
            step(v.tensor_scalar(PEN[:, 0:CL], rel[:, 0:CL], 0.0, None, ALU.is_ge))
            step(v.scalar_tensor_tensor(rel[:, 0:CL], rel[:, 0:CL], float(P) - 0.5, PEN[:, 0:CL], ALU.is_lt, ALU.mult))
            v.wait_ge(unturned, NG)
            step(v.tensor_tensor(SS, SS, FF, ALU.mult))
            step(v.tensor_scalar(FF, FF, 1.0, BIG, ALU.subtract, ALU.mult))
            step(v.tensor_tensor(SS, SS, FF, ALU.add), wait=False)
            step(v.tensor_tensor(PEN[:, 1:CL], key[:, 1:CL], key[:, 0:CL - 1], ALU.is_equal))
            step(v.tensor_scalar(PEN[:, 1:CL], PEN[:, 1:CL], 1.0, BIG, ALU.subtract, ALU.mult), wait=False)
            step(v.memset(PEN[:, 0:1], 0.0), wait=False)
            step(v.memset(PEN[:, CL:CL + 1], 0.0), wait=False)
            step(v.tensor_copy(cKf, key[:, 0:1]), wait=False)
            step(v.tensor_copy(cKl, key[:, CL - 1:CL]))
            step(v.tensor_tensor_scan(FF, p0, SS, -BIG, ALU.add, ALU.max))
            step(v.tensor_tensor_scan(BB[:, ::-1], p1[:, ::-1], FF[:, ::-1], -BIG, ALU.add, ALU.max))
            step(v.tensor_copy(cF, F[:, CL - 1:CL]), wait=False)
            step(v.tensor_copy(cB, Bk[:, 0:1]))
            v.sem_inc(ready, 1)
            v.wait_ge(pe_done, 1)
            step(v.tensor_copy(rowK[0:1, 0:4, :].rearrange("p a b -> p (a b)"), m.ps[4][0:1, :]))
            rF, rB, rKf, rKl, pv, ps_, pn, t1, rL, rR, oL, oR, t2 = (row(i) for i in range(13))
            step(v.memset(pv, 0.0))
            step(v.tensor_tensor(pv[:, 1:P], rKf[:, 1:P], rKl[:, 0:P - 1], ALU.is_equal))
            step(v.memset(pv.rearrange("p (h c) -> p h c", h=H)[:, :, 0:1], 0.0))
            step(v.tensor_scalar(pv, pv, 1.0, BIG, ALU.subtract, ALU.mult))
            step(v.tensor_tensor(ps_, rKf, rKl, ALU.is_equal))
            step(v.tensor_scalar(ps_, ps_, 1.0, BIG, ALU.subtract, ALU.mult))
            step(v.tensor_tensor(t1, pv, ps_, ALU.add))
            step(v.tensor_tensor_scan(oL, t1, rF, -BIG, ALU.add, ALU.max))
            step(v.memset(rL, -BIG))
            step(v.tensor_tensor(rL[:, 1:P], oL[:, 0:P - 1], pv[:, 1:P], ALU.add))
            step(v.memset(pn, -BIG))
            step(v.tensor_copy(pn[:, 0:P - 1], pv[:, 1:P]))
            step(v.tensor_tensor(t2, pn, ps_, ALU.add))
            step(v.tensor_tensor_scan(oR[:, ::-1], t2[:, ::-1], rB[:, ::-1], -BIG, ALU.add, ALU.max))
            step(v.memset(rR, -BIG))
            step(v.tensor_tensor(rR[:, 0:P - 1], oR[:, 1:P], pn[:, 0:P - 1], ALU.add))
            v.sem_inc(ready, 1)
            v.wait_ge(pe_done, 2)
            step(v.tensor_copy(m.small[:, 4:6], m.ps[5][:, 0:2]))
            step(v.tensor_tensor_scan(FF, p0, SS, cL, ALU.add, ALU.max))
            step(v.tensor_tensor_scan(BB[:, ::-1], p1[:, ::-1], FF[:, ::-1], cR, ALU.add, ALU.max))
            step(v.tensor_tensor(SS, SS, BB, ALU.subtract))
            v.sem_inc(ready, 1)
            for i in range(NG):
                v.wait_ge(turned, NG + i + 1)
                for k in range(4):
                    mm = v.tensor_copy(sc[:, 4 * i + k], m.ps[i % 2][:, k * P:(k + 1) * P].rearrange("p (h c) -> p h c", h=H))
                mm.then_inc(unturned, 1)


def edge_values(nc, ctx, m):
    sem = lambda n: semaphore(nc, m, f"ev_{n}")
    idx_ready, weighted, pcols, onehot, summed, added, cleared, asked = (sem(n) for n in (
        "idx", "weighted", "pcols", "onehot", "summed", "added", "cleared", "asked"))
    landed = [sem(f"landed{k}") for k in range(BATCH)]
    U = BATCH // 2
    g8 = m.G.rearrange("p (k d) -> p k d", k=BATCH)
    sc3 = m.SC.rearrange("p (s h) -> p s h", h=H)
    gs, oh, ix = m.GS, m.OH, m.IX
    with nc.Block() as block:
        @block.scalar
        def _(s):
            s.activation(ix[:, 0, :], m.TSI[:, 0:BATCH], ACT.Copy).then_inc(idx_ready, 1)

            def body(b, q, last):
                if not last:
                    s.wait_ge(weighted, b * 2 + 2)
                    s.activation(ix[:, 1 - q, :], m.TSI[:, bass.ds(b * BATCH + BATCH, BATCH)], ACT.Copy).then_inc(idx_ready, 1)
                for w in range(2):
                    s.wait_ge(summed, b * BATCH + w * U + U)
                    s.activation(gs[:, w * U:w * U + U, D:AW], sc3[:, bass.ds(b * BATCH + w * U, U), :], ACT.Copy).then_inc(pcols, 1)
            batches(s, body)

        @block.gpsimd
        def _(g):
            def body(b, q, last):
                g.wait_ge(idx_ready, b + 1)
                for k in range(BATCH):
                    g.wait_ge(weighted, b * 2 + k // U + 1)
                    g.sem_inc(asked, 1)
                    g.indirect_dma_start(g8[:, k, :], None, m.vt, bass.IndirectOffsetOnAxis(ap=ix[:, q, k:k + 1], axis=0)).then_inc(landed[k], 16)
            batches(g, body)

        @block.vector
        def _(v):
            v.sem_inc(added, BATCH)
            v.sem_inc(weighted, 2)
            v.memset(m.AGG3, 0.0).then_inc(cleared, 1)
            v.wait_ge(cleared, 1)
            one_hots(v, m, 0, 0, onehot)

            def weigh(b, w):
                for k in range(w * U, w * U + U):
                    v.wait_ge(landed[k], b * 16 + 16)
                v.wait_ge(summed, b * BATCH + w * U + U)
                v.tensor_tensor(gs[:, w * U:w * U + U, 0:D].rearrange("p k (h e) -> p k h e", h=H),
                                g8[:, w * U:w * U + U, :].rearrange("p k (h e) -> p k h e", h=H),
                                sc3[:, bass.ds(b * BATCH + w * U, U), :].unsqueeze(3).broadcast_to([P, U, H, DH]), ALU.mult).then_inc(weighted, 1)

            weigh(0, 0)

            def body(b, q, last):
                if not last:
                    one_hots(v, m, b + 1, 1 - q, onehot)
                for w in range(2):
                    if w == 0:
                        weigh(b, 1)
                    elif not last:
                        weigh(b + 1, 0)
                    for k in range(w * U, w * U + U):
                        add_window(v, m, b, k, summed, added, AW)
            batches(v, body)

        @block.tensor
        def _(pe):
            pe.sem_inc(summed, BATCH)

            def body(b, q, last):
                pe.wait_ge(onehot, b + 1)
                for w in range(2):
                    pe.wait_ge(weighted, b * 2 + w + 3)
                    pe.wait_ge(pcols, b * 2 + w + 1)
                    pe.wait_ge(added, b * BATCH + w * U + U)
                    for k in range(w * U, w * U + U):
                        pe.matmul(m.ps[k][:, 0:AW], oh[:, q, k, :], gs[:, k, :], start=True, stop=True).then_inc(summed, 1)
            batches(pe, body)


def slice_weights(nc, ctx, m, a):
    sem = lambda n: semaphore(nc, m, f"sw_{n}")
    loaded, zeroed, turned, out_, prod, done = (sem(n) for n in ("loaded", "zeroed", "turned", "read", "product", "vector"))
    s_ = m.TS
    s_zero = zeroed
    with nc.Block() as block:
        @block.sync
        def _(s):
            s.dma_start(s_.wf, a["L1_ffn_W_fx"].rearrange("(c p) f -> p c f", p=P)).then_inc(loaded, 16)
            s.dma_start(s_.wx, a["L1_ffn_W_x"].rearrange("(c p) f -> p c f", p=P)).then_inc(loaded, 16)
            s.dma_start(s_.wo, a["L1_ffn_W_out"].rearrange("(c p) f -> p c f", p=P)).then_inc(loaded, 16)
            s.dma_start(s_.bfx, a["L1_ffn_b_fx"].partition_broadcast(P)).then_inc(loaded, 16)
            s.dma_start(m.VB[:, :], a["L1_ffn_b_out"].partition_broadcast(P)).then_inc(loaded, 16)
            s.dma_start(s_.bx, a["L1_ffn_b_x"].rearrange("(c p) -> p c", p=P)).then_inc(loaded, 16)
            s.dma_start(s_.bs, a["L1_ffn_b_slice"].partition_broadcast(P)).then_inc(loaded, 16)
            s.dma_start(s_.rt, a["L1_ffn_temperature"].rearrange("a h b c -> (a h b c)").partition_broadcast(P)).then_inc(loaded, 16)
            s.wait_ge(s_zero, 6)
            for dst, n in ((s_.ws, "W_slice"), (s_.wq, "W_q"), (s_.wk, "W_k"), (s_.wv, "W_v")):
                for i in range(2):
                    s.dma_start(dst[i * 64:(i + 1) * 64, i * 64:(i + 1) * 64], a["L1_ffn_" + n]).then_inc(loaded, 16)
            s.wait_ge(loaded, 16 * 16)

        @block.vector
        def _(v):
            c = [0]

            def step(ins):
                c[0] += 1
                ins.then_inc(done, 1)
                v.wait_ge(done, c[0])
            for x in (s_.ws, s_.wq, s_.wk, s_.wv, s_.tkb.rearrange("p a b -> p (a b)"), s_.atb.rearrange("p a b -> p (a b)")):
                v.memset(x, 0.0).then_inc(zeroed, 1)
            v.memset(s_.zero, 0.0)
            v.wait_ge(loaded, 16 * 16)
            step(v.tensor_scalar(s_.rt, s_.rt, 0.1, 5.0, ALU.max, ALU.min))
            step(v.reciprocal(s_.rt, s_.rt))
            for j in range(4):
                v.wait_ge(turned, j + 1)
                step(v.tensor_copy(s_.wxt[:, j], m.ps[j][:, 0:C2 * P].rearrange("p (c i) -> p c i", c=C2)))
            v.wait_ge(prod, 1)
            rt3 = s_.rt.unsqueeze(2).broadcast_to([P, H, G])
            for cc in range(C2):
                step(v.tensor_tensor(s_.wl[:, cc].rearrange("p (h g) -> p h g", h=H), m.ps[4 + cc][:, :].rearrange("p (h g) -> p h g", h=H), rt3, ALU.mult))
            bl3 = s_.bl.rearrange("p (h g) -> p h g", h=H)
            step(v.tensor_tensor(bl3, m.ps[6][:, :].rearrange("p (h g) -> p h g", h=H), s_.bs.unsqueeze(1).broadcast_to([P, H, G]), ALU.add))
            step(v.tensor_tensor(bl3, bl3, rt3, ALU.mult))

        @block.scalar
        def _(s):
            s.wait_ge(loaded, 16 * 16)
            for j in range(4):
                s.activation(s_.bxb[:, j, :], m.ones[:, :], ACT.Copy, scale=s_.bx[:, j:j + 1]).then_inc(out_, 1)

        @block.tensor
        def _(pe):
            pe.wait_ge(loaded, 16 * 16)
            for j in range(4):
                for c in range(C2):
                    mm = pe.transpose(m.ps[j][:, c * P:(c + 1) * P], s_.wx[:, c, j * P:(j + 1) * P], m.ident[:, :])
                mm.then_inc(turned, 1)
            pe.wait_ge(done, 6)
            pe.wait_ge(out_, 4)
            for j in range(4):
                for c in range(C2):
                    pe.matmul(m.ps[4 + c][:, j * P:(j + 1) * P], s_.wxt[:, j, c, :], s_.ws, start=True, stop=True)
                mm = pe.matmul(m.ps[6][:, j * P:(j + 1) * P], s_.bxb[:, j, :], s_.ws, start=True, stop=True)
            mm.then_inc(prod, 1)


def slice_pass(nc, ctx, m):
    sem = lambda n: semaphore(nc, m, f"sp_{n}")
    staged, turned, turn_read, prod, fx_out, mx_out, exp_out, w_out, tok, chain, init = (sem(n) for n in (
        "staged", "turned", "turn_read", "product", "fx_out", "shifted", "exp", "weights", "tokens", "vector", "init"))
    s_ = m.TS
    psT = (m.ps[4], m.ps[7])
    W3 = m.R1[:, 0:NT * INNER].rearrange("p (t n) -> p t n", t=NT)
    kept = sem("kept")
    with nc.Block() as block:
        @block.gpsimd
        def _(g):
            def body(t, k, last):
                if not last:
                    stage(t + 1, 1 - k)
                g.wait_ge(w_out, t + 1)
                g.tensor_copy(at(W3, t), s_.wst[:, k, :]).then_inc(kept, 1)

            def stage(t, k):
                g.wait_ge(turned, t + 1)
                g.tensor_copy(s_.hs[:, k, :], at(m.HB, t)).then_inc(staged, 1)
            g.sem_inc(kept, 2)
            stage(0, 0)
            tiles(g, body)

        @block.tensor
        def _(pe):
            pe.sem_inc(turned, 2)
            pe.sem_inc(prod, 2)
            pe.sem_inc(tok, 2)
            pe.wait_ge(init, 2)
            fx2 = s_.fx[:, 0].rearrange("p j n -> p (j n)")
            token_bank = lambda j: m.ps[5 + j // 2][:, (j % 2) * (P + 1):(j % 2 + 1) * (P + 1)]

            def turn(t, k):
                pe.wait_ge(staged, t + 1)
                pe.wait_ge(turn_read, t + 1)
                for c in range(C2):
                    last = pe.transpose(psT[k][:, c * P:(c + 1) * P], s_.hs[:, k, c * P:(c + 1) * P], m.ident[:, :])
                last.then_inc(turned, 1)

            def project(t, k):
                pe.wait_ge(turn_read, t + 3)
                pe.wait_ge(mx_out, t + 1)
                for n, w in enumerate((s_.wf, s_.wl)):
                    for c in range(C2):
                        mm = pe.matmul(m.ps[2 * k + n][:, :], s_.ht[:, k, c, :], w[:, c, :], start=(c == 0), stop=(c == 1))
                mm.then_inc(prod, 1)

            for i in range(2):
                pe.matmul(m.ps[5 + i][:, 0:2 * (P + 1)], s_.zero, fx2[:, 0:2 * (P + 1)], start=True, stop=False, skip_group_check=True)
            turn(0, 0)
            project(0, 0)

            def body(t, k, last):
                if not last:
                    turn(t + 1, 1 - k)
                    project(t + 1, 1 - k)
                pe.wait_ge(w_out, t + 1)
                pe.wait_ge(fx_out, t + 1)
                for j in range(4):
                    mm = pe.matmul(token_bank(j), s_.wst[:, k, j * P:(j + 1) * P], s_.fx[:, k, j, :],
                                   start=False, stop=False, skip_group_check=True)
                mm.then_inc(tok, 1)
            tiles(pe, body)
            for i in range(2):
                mm = pe.matmul(m.ps[5 + i][:, 0:2 * (P + 1)], s_.zero, fx2[:, 0:2 * (P + 1)], start=False, stop=True, skip_group_check=True)
            mm.then_inc(tok, 1)

        @block.scalar
        def _(s):
            def body(t, k, last):
                s.wait_ge(prod, t + 3)
                s.wait_ge(tok, t + 1)
                s.activation(s_.fx[:, k, :, 0:P], m.ps[2 * k][:, :].rearrange("p (j n) -> p j n", j=4), ACT.Copy).then_inc(fx_out, 1)
                s.wait_ge(mx_out, t + 3)
                s.activation(s_.lg[:, k, :], s_.lg[:, k, :], ACT.Exp).then_inc(exp_out, 1)
            tiles(s, body)

        @block.vector
        def _(v):
            v.sem_inc(turn_read, 2)
            v.sem_inc(mx_out, 2)
            for k in range(2):
                v.memset(s_.fx[:, k].rearrange("p j n -> p (j n)"), 1.0).then_inc(init, 1)

            def turn_out(t, k):
                v.wait_ge(turned, t + 3)
                v.wait_ge(prod, t + 1)
                v.tensor_copy(s_.ht[:, k].rearrange("p c n -> p (c n)"), psT[k][:, 0:D]).then_inc(turn_read, 1)

            turn_out(0, 0)

            def body(t, k, last):
                lg3 = s_.lg[:, k, :].rearrange("p (h g) -> p h g", h=H)

                def link(n):
                    v.wait_ge(chain, t * 5 + n)
                v.wait_ge(prod, t + 3)
                v.tensor_tensor(s_.lg[:, k, :], m.ps[2 * k + 1][:, :], s_.bl, ALU.add).then_inc(chain, 1)
                link(1)
                v.tensor_reduce(s_.mx, lg3, AX, ALU.max).then_inc(chain, 1)
                link(2)
                v.tensor_tensor(lg3, lg3, s_.mx.unsqueeze(2).broadcast_to([P, H, G]), ALU.subtract).then_inc(mx_out, 1)
                if not last:
                    turn_out(t + 1, 1 - k)
                v.wait_ge(exp_out, t + 1)
                v.tensor_reduce(s_.sm, lg3, AX, ALU.add).then_inc(chain, 1)
                link(3)
                v.reciprocal(s_.sm, s_.sm).then_inc(chain, 1)
                link(4)
                v.tensor_scalar(s_.sm, s_.sm, col(m.valid, t), None, ALU.mult).then_inc(chain, 1)
                link(5)
                v.wait_ge(tok, t + 1)
                v.wait_ge(kept, t + 1)
                v.tensor_tensor(s_.wst[:, k, :].rearrange("p (h g) -> p h g", h=H), lg3,
                                s_.sm.unsqueeze(2).broadcast_to([P, H, G]), ALU.mult).then_inc(w_out, 1)
            tiles(v, body)
            v.wait_ge(tok, NT + 3)
            a4 = s_.acc.rearrange("p (i n) -> p i n", i=2)
            for i in range(2):
                v.tensor_copy(a4[:, i], m.ps[5 + i][:, 0:2 * (P + 1)]).then_inc(init, 1)
            v.wait_ge(init, 4)
            a3 = s_.acc.rearrange("p (j n) -> p j n", j=4)
            for j in range(4):
                v.scalar_tensor_tensor(a3[:, j, 0:P], s_.bfx[:, j * P:(j + 1) * P], a3[:, j, P:P + 1], a3[:, j, 0:P], ALU.mult, ALU.add)


def slice_tokens(nc, ctx, m):
    sem = lambda n: semaphore(nc, m, f"st_{n}")
    done, pe_done, exp_out, at_ready = (sem(n) for n in ("vector", "tensor", "exp", "rows"))
    s_ = m.TS
    a3 = s_.acc.rearrange("p (j n) -> p j n", j=4)
    scale = float(DS) ** -0.5
    halves = ((slice(0, 64), slice(0, 64)), (slice(64, 128), slice(64, 128)))
    with nc.Block() as block:
        @block.vector
        def _(v):
            c = [0]

            def step(ins):
                c[0] += 1
                ins.then_inc(done, 1)
                v.wait_ge(done, c[0])
            step(v.tensor_scalar(s_.nr, a3[:, :, P:P + 1].rearrange("p j n -> p (j n)"), 1e-5, None, ALU.add))
            step(v.reciprocal(s_.nr, s_.nr))
            for rows, cols in halves:
                step(v.tensor_tensor(s_.tkb[rows, :, cols], a3[rows, :, cols], s_.nr[rows, :].unsqueeze(2).broadcast_to([64, 4, 64]), ALU.mult))
            assert c[0] == 4
            v.wait_ge(pe_done, 1)
            step(v.tensor_copy(s_.t1.rearrange("p j n -> p (j n)"), m.ps[0][:, :]))
            v.wait_ge(pe_done, 2)
            step(v.tensor_copy(s_.qT.rearrange("p j n -> p (j n)"), m.ps[1][:, :]))
            step(v.tensor_copy(s_.kT.rearrange("p j n -> p (j n)"), m.ps[2][:, :]))
            step(v.tensor_copy(s_.vv.rearrange("p j n -> p (j n)"), m.ps[3][:, :]))
            v.wait_ge(pe_done, 3)
            p3 = m.ps[4][:, :].rearrange("p (j n) -> p j n", j=4)
            for rows, cols in halves:
                step(v.tensor_copy(s_.att[rows], p3[rows, :, cols]))
            step(v.tensor_reduce(s_.am, s_.att, AX, ALU.max))
            step(v.tensor_tensor(s_.att, s_.att, s_.am.unsqueeze(2).broadcast_to([P, 4, 64]), ALU.subtract))
            v.wait_ge(exp_out, 1)
            step(v.tensor_reduce(s_.am, s_.att, AX, ALU.add))
            step(v.reciprocal(s_.am, s_.am))
            for rows, cols in halves:
                step(v.tensor_tensor(s_.atb[rows, :, cols], s_.att[rows], s_.am[rows, :].unsqueeze(2).broadcast_to([64, 4, 64]), ALU.mult))
            assert c[0] == 16
            v.wait_ge(pe_done, 4)
            step(v.tensor_copy(s_.t1.rearrange("p j n -> p (j n)"), m.ps[5][:, :]))
            v.wait_ge(pe_done, 5)
            step(v.tensor_copy(s_.qT.rearrange("p j n -> p (j n)"), m.ps[6][:, :]))
            v.wait_ge(pe_done, 6)
            for i in range(2):
                step(v.tensor_copy(s_.mo[:, 2 * i:2 * i + 2, :].rearrange("p j n -> p (j n)"), m.ps[i][:, :]))

        @block.scalar
        def _(s):
            s.wait_ge(done, 12)
            s.activation(s_.att, s_.att, ACT.Exp, scale=scale).then_inc(exp_out, 1)

        @block.tensor
        def _(pe):
            J = lambda ap, j: ap[:, j * P:(j + 1) * P]
            pe.wait_ge(done, 4)
            for j in range(4):
                mm = pe.transpose(J(m.ps[0], j), s_.tkb[:, j, :], m.ident[:, :])
            mm.then_inc(pe_done, 1)
            pe.wait_ge(done, 5)
            for j in range(4):
                pe.matmul(J(m.ps[1], j), s_.wq, s_.t1[:, j, :], start=True, stop=True)
                pe.matmul(J(m.ps[2], j), s_.wk, s_.t1[:, j, :], start=True, stop=True)
                mm = pe.matmul(J(m.ps[3], j), s_.t1[:, j, :], s_.wv, start=True, stop=True)
            mm.then_inc(pe_done, 1)
            pe.wait_ge(done, 8)
            for j in range(4):
                mm = pe.matmul(J(m.ps[4], j), s_.qT[:, j, :], s_.kT[:, j, :], start=True, stop=True)
            mm.then_inc(pe_done, 1)
            pe.wait_ge(done, 16)
            for j in range(4):
                mm = pe.transpose(J(m.ps[5], j), s_.atb[:, j, :], m.ident[:, :])
            mm.then_inc(pe_done, 1)
            pe.wait_ge(done, 17)
            for j in range(4):
                mm = pe.matmul(J(m.ps[6], j), s_.vv[:, j, :], s_.t1[:, j, :], start=True, stop=True)
            mm.then_inc(pe_done, 1)
            pe.wait_ge(done, 18)
            for j in range(4):
                mm = pe.matmul(m.ps[j // 2][:, (j % 2) * D:(j % 2 + 1) * D], s_.qT[:, j, :], s_.wo[:, j, :], start=True, stop=True)
            mm.then_inc(pe_done, 1)


def slice_output(nc, ctx, m, out):
    sem = lambda n: semaphore(nc, m, f"so_{n}")
    staged, turned, turn_read, prod, summed = (sem(n) for n in ("staged", "turned", "turn_read", "product", "summed"))
    loaded = [sem(f"loaded{k}") for k in range(2)]
    stored = [sem(f"stored{k}") for k in range(2)]
    chain = sem("bias")
    s_ = m.TS
    W3 = m.R1[:, 0:NT * INNER].rearrange("p (t n) -> p t n", t=NT)
    x3, ot = s_.hs, s_.ot
    with nc.Block() as block:
        @block.sync
        def _(s):
            for k in range(2):
                s.sem_inc(stored[k], 16)

            def load(t, k):
                s.dma_start(x3[:, k, :], m.x3[bass.ds(t * P, P), :]).then_inc(loaded[k], 16)

            def store(t, k):
                s.wait_ge(summed, t + 1)
                s.dma_start(out[bass.ds(t * P, P), :], ot[:, k, :]).then_inc(stored[k], 16)
            load(0, 0)
            load(1, 1)
            with s.Fori(0, (NT - 3) // 2) as i:
                for k in range(2):
                    store(i * 2 + k, k)
                    load(i * 2 + k + 2, k)
            store(NT - 3, 0)
            load(NT - 1, 0)
            store(NT - 2, 1)
            s.wait_ge(summed, NT)
            s.dma_start(out[(NT - 1) * P:N, :], ot[0:LAST, 0, :]).then_inc(stored[0], 16)
            s.wait_ge(stored[0], 16 * (NT // 2 + 2))
            s.wait_ge(stored[1], 16 * (NT // 2 + 1))

        @block.gpsimd
        def _(g):
            def body(t, k, last):
                g.wait_ge(turned, t + 1)
                g.tensor_copy(s_.wst[:, k, :], at(W3, t)).then_inc(staged, 1)
            tiles(g, body)

        @block.tensor
        def _(pe):
            pe.sem_inc(turned, 2)
            pe.sem_inc(prod, 2)

            def turn(t, k):
                pe.wait_ge(staged, t + 1)
                pe.wait_ge(turn_read, t + 1)
                for j in range(4):
                    mm = pe.transpose(m.ps[k][:, j * P:(j + 1) * P], s_.wst[:, k, j * P:(j + 1) * P], m.ident[:, :])
                mm.then_inc(turned, 1)
            turn(0, 0)

            def body(t, k, last):
                if not last:
                    turn(t + 1, 1 - k)
                pe.wait_ge(turn_read, t + 3)
                pe.wait_ge(chain, t + 1)
                for j in range(4):
                    mm = pe.matmul(m.ps[2 + k][:, 0:D], s_.wtt[:, k, j * P:(j + 1) * P], s_.mo[:, j, :], start=(j == 0), stop=(j == 3))
                mm.then_inc(prod, 1)
            tiles(pe, body)

        @block.scalar
        def _(s):
            s.sem_inc(turn_read, 2)

            def body(t, k, last):
                s.wait_ge(turned, t + 3)
                s.wait_ge(prod, t + 1)
                s.activation(s_.wtt[:, k, :], m.ps[k][:, :], ACT.Copy).then_inc(turn_read, 1)
            tiles(s, body)

        @block.vector
        def _(v):
            v.sem_inc(chain, 2)

            def body(t, k, i):
                v.wait_ge(prod, t + 3)
                v.wait_ge(stored[k], i * 16 + 16)
                v.tensor_tensor(ot[:, k, :], m.ps[2 + k][:, 0:D], m.VB[:, :], ALU.add).then_inc(chain, 1)
                v.wait_ge(chain, t + 3)
                v.wait_ge(loaded[k], i * 16 + 16)
                v.tensor_tensor(ot[:, k, :], ot[:, k, :], x3[:, k, :], ALU.add).then_inc(summed, 1)
            with v.Fori(0, (NT - 1) // 2) as i:
                for k in range(2):
                    body(i * 2 + k, k, i)
            body(NT - 1, 0, NT // 2)


def gnn_program(nc, a, out):
    with ExitStack() as ctx:
        ctx.enter_context(nc.allow_non_contiguous_dma(reason="small vectors and tables"))
        sb = lambda n, s, d=F32: ctx.enter_context(nc.sbuf_tensor(n, s, d))
        dr = lambda n, s, d=F32: nc.dram_tensor(n, s, d).ap()
        m = Mem()
        m.semaphores = []
        m.ps = [ctx.enter_context(nc.psum_tensor(f"bank{i}", [P, 512], F32)) for i in range(8)]
        big = NT * AW + NT * D + C2 * R * D
        m.R1 = sb("R1", [P, big])[:, :]
        m.AGG = m.R1[:, 0:NT * AW]
        m.AGG3 = m.AGG.rearrange("p (t d) -> p t d", t=NT)
        m.XV = m.R1[:, 0:NT * D].rearrange("p (t d) -> p t d", t=NT)
        m.HB = m.R1[:, NT * AW:NT * AW + NT * D].rearrange("p (t d) -> p t d", t=NT)
        m.WT = m.R1[:, NT * (AW + D):big]
        m.SC = sb("SC", [P, STEPS * H])[:, :]
        m.TDR, m.TCI, m.TSI, m.TEA = (sb(n, [P, STEPS])[:, :] for n in ("TDR", "TCI", "TSI", "TEA"))
        m.G = sb("G", [P, BATCH * D])[:, :]
        m.GS = sb("GS", [P, BATCH, AW])[:, :, :]
        m.OH = sb("OH", [P, 2, BATCH, P])[:, :, :, :]
        m.IX = sb("IX", [P, 2, BATCH], I32)[:, :, :]
        m.win = sb("win", [1, STEPS], I32)
        m.unsorted = sb("unsorted", [1, 1], I32)
        m.ident, m.iota, m.ones, m.upper = (sb(n, [P, P]) for n in ("ident", "iota", "ones", "upper"))
        m.valid = sb("valid", [P, NT])
        m.ab = sb("ab", [P, 2, ERJ])
        m.abi = sb("abi", [P, 2, ERJ], I32)
        m.small = sb("small", [P, 40])[:, :]
        m.smalli = sb("smalli", [P, 16], I32)[:, :]
        m.VG, m.VB = sb("VG", [P, D]), sb("VB", [P, D])
        m.ROOT = m.G[:, 0:C2 * D].rearrange("p (c o) -> p c o", c=C2)
        m.ATT = sb("ATT", [P, R * B])
        m.st = sb("st", [P, NT, 6])[:, :, :]
        m.mean, m.var, m.rstd, m.tmp = (sb(n, [P, NT])[:, :] for n in ("mean", "var", "rstd", "tmp"))
        m.MW = sb("MW", [P, NT])[:, :]
        m.SEL = m.G[:, 0:4 * NT]
        m.SC2 = m.AGG[:, 0:NP]
        m.rc = m.rstd
        m.rows = m.OH.rearrange("p a b c -> p (a b) c")
        m.hrel = dr("hrel", (NP, R * D))
        m.edg = dr("edg", (ETILES, 4 * P))
        m.abd = dr("abd", (2, ETILES))
        m.dsts = dr("dsts", (ETILES * P,))
        m.srec = dr("srec", (ETILES * P, 4))
        m.keyd, m.reld = dr("keyd", (STEPS, P)), dr("reld", (STEPS, P))
        m.wind = dr("wind", (STEPS,), I32)
        m.wd = dr("wd", (NP,))
        m.xs, m.x1, m.x2, m.zs = (dr(n, (NP, D)) for n in ("x0", "x1", "x2", "zs"))
        m.x3 = dr("x3", (NP, D))
        m.qt, m.vt = dr("qt", (NP, D)), dr("vt", (NP, D))
        s_ = m.TS = Mem()
        o = [0]

        def part(base, shape):
            n = 1
            for x in shape:
                n *= x
            ap = base[:, o[0]:o[0] + n]
            o[0] += n
            if len(shape) == 2:
                ap = ap.rearrange("p (a b) -> p a b", a=shape[0])
            if len(shape) == 3:
                ap = ap.rearrange("p (a b c) -> p a b c", a=shape[0], b=shape[1])
            return ap
        s_.wf, s_.wx, s_.wl = (part(m.WT, (C2, INNER)) for _ in range(3))
        s_.wo = part(m.WT, (4, D))
        s_.wxt = part(m.WT, (4, C2, P))
        s_.ws, s_.wq, s_.wk, s_.wv = (part(m.WT, (P,)) for _ in range(4))
        s_.bxb = part(m.WT, (4, P))
        s_.bfx, s_.bl = part(m.WT, (INNER,)), part(m.WT, (INNER,))
        s_.bx, s_.bs, s_.rt, s_.nr, s_.am, s_.mx, s_.sm = (part(m.WT, (n,)) for n in (4, G, H, 4, 4, H, H))
        assert o[0] <= C2 * R * D
        o[0] = 0
        s_.hs = part(m.SC, (2, D))
        s_.ot = part(m.SC, (2, D))
        s_.ht = part(m.SC, (2, C2, P))
        s_.lg = part(m.SC, (2, INNER))
        s_.wst = part(m.SC, (2, INNER))
        s_.fx = part(m.SC, (2, 4, P + 1))
        s_.acc = part(m.SC, (4 * (P + 1),))
        s_.att = part(m.SC, (4, 64))
        s_.zero = part(m.SC, (P,))
        assert o[0] <= STEPS * H
        o[0] = 0
        s_.tkb, s_.atb, s_.t1, s_.qT = (part(m.G, (4, P)) for _ in range(4))
        o[0] = 0
        oh = m.OH.rearrange("p a b c -> p (a b c)")
        s_.kT, s_.vv = part(oh, (4, P)), part(oh, (4, P))
        s_.mo = part(oh, (4, D))
        s_.wtt = s_.lg

        A3 = m.AGG3[:, :, 0:D]
        stages = m.stages = []
        setup(nc, ctx, m, a)
        sort_edges(nc, ctx, m)
        schedule(nc, ctx, m)
        normalise(nc, ctx, m, "ln0", m.HB, m.HB)
        for l in (1, 2):
            relation_weights(nc, ctx, m, l, a[f"L0_gnn_basis{l}"], a[f"L0_gnn_att{l}"], a[f"L0_gnn_root{l}"])
            relation_product(nc, ctx, m, l)
            relation_sum(nc, ctx, m, l)
            bias = m.ATT2 = m.small

            def mean_and_residual(v, done):
                v.reciprocal(m.tmp, m.AGG3[:, :, D:D + 1].rearrange("p t o -> p (t o)")).then_inc(done, 1)
                v.wait_ge(done, 1)
                v.tensor_tensor(A3, A3, m.tmp.unsqueeze(2).broadcast_to([P, NT, D]), ALU.mult).then_inc(done, 1)
                v.tensor_tensor(m.HB, m.HB, m.G[:, 0:D].unsqueeze(1).broadcast_to([P, NT, D]), ALU.add).then_inc(done, 1)
                v.wait_ge(done, 3)
                v.tensor_tensor(m.HB, m.HB, A3, ALU.add).then_inc(done, 1)
            normalise(nc, ctx, m, f"ln{l}", m.HB, m.HB, a[f"L0_gnn_ln{l}_g"], a[f"L0_gnn_ln{l}_b"], relu=True,
                      before=mean_and_residual, nbefore=4, loads=((m.G[:, 0:D], a[f"L0_gnn_bias{l}"].partition_broadcast(P)),))

        recycle_semaphores(nc, m)

        def add_spilled(v, done):
            v.tensor_tensor(m.XV, m.XV, m.HB, ALU.add).then_inc(done, 1)
        tiled = lambda ap: ap.rearrange("(t p) d -> p t d", p=P)
        normalise(nc, ctx, m, "ln3", m.XV, m.HB, before=add_spilled, nbefore=1, loads=((m.XV, tiled(m.xs)),), spill=m.x1)
        select_rows(nc, ctx, m, a)
        def gated(v, t, psum, outs):
            tmp = m.GS[:, 0, 0:D]
            v.wait_ge(outs, t * 3 + 6)
            v.tensor_tensor(tmp, psum, m.VB[:, :], ALU.add).then_inc(outs, 1)
            v.wait_ge(outs, t * 3 + 7)
            v.scalar_tensor_tensor(tmp, tmp, col(m.MW, t), at(m.HB, t), ALU.mult, ALU.add).then_inc(outs, 1)
            v.wait_ge(outs, t * 3 + 8)
            v.tensor_tensor(at(m.XV, t), at(m.XV, t), tmp, ALU.add).then_inc(outs, 1)
        reload(nc, ctx, m, "back1", m.XV, tiled(m.x1))
        feed_forward(nc, ctx, m, "ff0", m.HB, a["L0_ffn_w1"], a["L0_ffn_b1"], a["L0_ffn_w2"], a["L0_ffn_b2"],
                     ACT.Gelu_apprx_tanh, gated, 3)
        normalise(nc, ctx, m, "ln4", m.XV, m.HB, spill=m.x2)
        normalise(nc, ctx, m, "ln5", m.HB, m.HB, a["L1_gnn_ln_attn_g"], a["L1_gnn_ln_attn_b"], spill=m.zs)
        make_qkv(nc, ctx, m, a)
        recycle_semaphores(nc, m)
        edge_scores(nc, ctx, m)
        edge_softmax(nc, ctx, m)
        edge_values(nc, ctx, m)

        def attended(v, done):
            s3 = m.AGG3[:, :, D:AW]
            r3 = m.G[:, 0:NT * H].rearrange("p (t h) -> p t h", t=NT)
            v.tensor_scalar(r3, s3, 0.0, None, ALU.is_equal).then_inc(done, 1)
            v.wait_ge(done, 1)
            v.tensor_tensor(r3, r3, s3, ALU.add).then_inc(done, 1)
            v.wait_ge(done, 2)
            v.reciprocal(r3, r3).then_inc(done, 1)
            v.wait_ge(done, 3)
            for h in range(H):
                ah = m.AGG3[:, :, h * DH:(h + 1) * DH]
                v.tensor_tensor(ah, ah, r3[:, :, h:h + 1].broadcast_to([P, NT, DH]), ALU.mult).then_inc(done, 1)
            v.wait_ge(done, 3 + H)
            v.tensor_tensor(m.HB, m.HB, A3, ALU.add).then_inc(done, 1)
        normalise(nc, ctx, m, "ln6", m.HB, m.XV, a["L1_gnn_ln_res_g"], a["L1_gnn_ln_res_b"],
                  before=attended, nbefore=4 + H, loads=((m.HB, tiled(m.zs)),))

        def residual(v, t, psum, outs):
            tmp = m.GS[:, 0, 0:D]
            v.wait_ge(outs, t * 2 + 4)
            v.tensor_tensor(tmp, psum, m.VB[:, :], ALU.add).then_inc(outs, 1)
            v.wait_ge(outs, t * 2 + 5)
            v.tensor_tensor(at(m.HB, t), at(m.HB, t), tmp, ALU.add).then_inc(outs, 1)
        feed_forward(nc, ctx, m, "ff1", m.XV, a["L1_gnn_W_in"], a["L1_gnn_b_in"], a["L1_gnn_W_out"], a["L1_gnn_b_out"],
                     ACT.Gelu, residual, 2)
        normalise(nc, ctx, m, "ln7", m.XV, m.HB, before=add_spilled, nbefore=1, loads=((m.XV, tiled(m.x2)),), spill=m.x3)
        slice_weights(nc, ctx, m, a)
        slice_pass(nc, ctx, m)
        slice_tokens(nc, ctx, m)
        slice_output(nc, ctx, m, out)


def reload(nc, ctx, m, name, dst, src):
    loaded = semaphore(nc, m, name)
    with nc.Block() as block:
        @block.sync
        def _(s):
            s.dma_start(dst, src).then_inc(loaded, 16)
            s.wait_ge(loaded, 16)


_INS = ['x', 'src', 'dst', 'edge_type_16', 'edge_weight', 'L0_gnn_basis1', 'L0_gnn_att1', 'L0_gnn_root1', 'L0_gnn_bias1',
        'L0_gnn_ln1_g', 'L0_gnn_ln1_b', 'L0_gnn_basis2', 'L0_gnn_att2', 'L0_gnn_root2', 'L0_gnn_bias2', 'L0_gnn_ln2_g',
        'L0_gnn_ln2_b', 'L0_ffn_wr', 'L0_ffn_br', 'L0_ffn_w1', 'L0_ffn_b1', 'L0_ffn_w2', 'L0_ffn_b2', 'L1_gnn_Wqkv',
        'L1_gnn_bqkv', 'L1_gnn_ln_attn_g', 'L1_gnn_ln_attn_b', 'L1_gnn_ln_res_g', 'L1_gnn_ln_res_b', 'L1_gnn_W_in',
        'L1_gnn_b_in', 'L1_gnn_W_out', 'L1_gnn_b_out', 'L1_ffn_W_fx', 'L1_ffn_b_fx', 'L1_ffn_W_x', 'L1_ffn_b_x',
        'L1_ffn_W_slice', 'L1_ffn_b_slice', 'L1_ffn_W_q', 'L1_ffn_W_k', 'L1_ffn_W_v', 'L1_ffn_W_out', 'L1_ffn_b_out',
        'L1_ffn_temperature']


def kernel(**inputs):
    import numpy as _np
    import concourse.bacc as _bacc
    from concourse import mybir as _mybir
    from concourse.bass_utils import run_bass_kernel_spmd as _run

    nc = _bacc.Bacc("TRN2", target_bir_lowering=False, num_devices=1)
    arrays, args = {}, {}
    for name in _INS:
        x = _np.ascontiguousarray(inputs[name])
        arrays[f"in_{name}"] = x
        args[name] = nc.dram_tensor(f"in_{name}", x.shape, _mybir.dt.from_np(x.dtype), kind="ExternalInput").ap()
    out = nc.dram_tensor("out_0", (N, D), F32, kind="ExternalOutput").ap()
    gnn_program(nc, args, out)
    r = _run(nc, [arrays], core_ids=[0])
    return r.results[0]["out_0"]
```

```python
from contextlib import ExitStack

import concourse.bass as bass
from concourse import mybir

F32 = mybir.dt.float32
I32 = mybir.dt.int32
ALU = mybir.AluOpType
ACT = mybir.ActivationFunctionType
AX = mybir.AxisListType.X

P = 128
N, D, E = 6250, 256, 100000
NT = -(-N // P)
NP = NT * P
LAST = N - (NT - 1) * P
R, B = 16, 8
H = 8
DH = D // H
DFF = 4 * D
C2 = D // P
ERP, ERJ = 112, 7
ETILES = ERP * ERJ
EFULL, EREST = E // P, E % P
PAIRP = next(p for p in range(P, 0, -1) if (E - 1) % p == 0)
PAIRE = (E - 1) // PAIRP
STEPS = ETILES + NT - 1
SP_, SJ = 104, 8
CH = 16
CS = STEPS // CH
CL = CS * P
BATCH = 8
NBATCH = STEPS // BATCH
AW = 264
PADDST = NP - 1
TOPK = N // 2 - 1
BIG = 1e30
EPS = 1e-5
INNER, G, DS = 512, 64, 64
assert STEPS == SP_ * SJ == CH * CS


class Mem:
    pass


def semaphore(nc, m, name):
    handle = nc.alloc_semaphore(name=name)
    m.semaphores.append(handle)
    return handle


def recycle_semaphores(nc, m):
    nc.all_engine_barrier()
    nc.clear_and_free_semaphores(m.semaphores)
    nc.all_engine_barrier()
    m.semaphores = []


def tiles(eng, body):
    with eng.Fori(0, (NT - 1) // 2) as i:
        for k in range(2):
            body(i * 2 + k, k, False)
    body(NT - 1, (NT - 1) % 2, True)


def tiles_ahead(eng, body):
    with eng.Fori(0, (NT - 5) // 2) as i:
        for k in range(2):
            body(i * 2 + k, k, 4)
    for t in range(NT - 5, NT):
        body(t, t % 2, NT - 1 - t)


def batches(eng, body):
    with eng.Fori(0, NBATCH // 2 - 1) as i:
        for q in range(2):
            body(i * 2 + q, q, False)
    body(NBATCH - 2, 0, False)
    body(NBATCH - 1, 1, True)


def at(ap3, t):
    return ap3[:, bass.ds(t, 1), :].rearrange("p a d -> p (a d)")


def col(ap2, s):
    return ap2[:, bass.ds(s, 1)]


def setup(nc, ctx, m, a):
    sem = lambda n: semaphore(nc, m, n)
    zeroed, iotas, loaded, edges_in, fields, stored, pairs_in, totalled = (sem(n) for n in (
        "su_zeroed", "su_iotas", "su_loaded", "su_edges_in", "su_fields", "su_stored", "su_pairs_in", "su_totalled"))
    q2 = slice(0, PAIRP)
    pair = m.AGG[:, 0:2 * PAIRE].bitcast(I32).rearrange("p (i e) -> p i e", i=2)
    later = m.AGG[:, 2 * PAIRE:3 * PAIRE]
    ei = m.SC[:, 0:3 * ERJ * P].bitcast(I32).rearrange("p (f j e) -> p f j e", f=3, j=ERJ)
    ew = m.SC[:, 3 * ERJ * P:4 * ERJ * P].rearrange("p (j e) -> p j e", j=ERJ)
    ef = m.WT[:, 0:ERJ * 4 * P].rearrange("p (j f e) -> p j f e", j=ERJ, f=4)
    with nc.Block() as block:
        @block.gpsimd
        def _(g):
            g.memset(m.ident[:, :], 0.0).then_inc(iotas, 1)
            g.wait_ge(iotas, 1)
            g.affine_select(out=m.ident[:, :], in_=m.ident[:, :], compare_op=ALU.not_equal, fill=1.0,
                            base=0, pattern=[[-1, P]], channel_multiplier=1).then_inc(iotas, 1)
            g.iota(m.iota[:, :], [[1, P]], base=0, channel_multiplier=0,
                   allow_small_or_imprecise_dtypes=True).then_inc(iotas, 1)
            g.memset(m.ones[:, :], 1.0).then_inc(iotas, 1)
            g.memset(m.upper[:, :], 1.0).then_inc(iotas, 1)
            g.wait_ge(iotas, 5)
            g.affine_select(out=m.upper[:, :], in_=m.upper[:, :], compare_op=ALU.is_gt, fill=0.0,
                            base=0, pattern=[[1, P]], channel_multiplier=-1).then_inc(iotas, 1)
            g.memset(m.valid[:, :], 1.0).then_inc(iotas, 1)
            g.wait_ge(iotas, 7)
            g.affine_select(out=m.valid[:, :], in_=m.valid[:, :], compare_op=ALU.is_gt, fill=0.0,
                            base=N, pattern=[[-P, NT]], channel_multiplier=-1).then_inc(iotas, 1)

        @block.vector
        def _(v):
            v.memset(m.HB[:, NT - 1, :], 0.0).then_inc(zeroed, 1)
            v.memset(ei[:, 0, ERJ - 1, :], 0).then_inc(zeroed, 1)
            v.memset(ei[:, 1, ERJ - 1, :], PADDST).then_inc(zeroed, 1)
            v.memset(ei[:, 2, ERJ - 1, :], 0).then_inc(zeroed, 1)
            v.memset(ew[:, ERJ - 1, :], 0.0).then_inc(zeroed, 1)
            v.wait_ge(edges_in, 12 * 16)
            q = slice(0, ERP)
            v.tensor_copy(ef[q, :, 0, :], ei[q, 1]).then_inc(fields, 1)
            v.tensor_copy(ef[q, :, 2, :], ei[q, 0]).then_inc(fields, 1)
            v.tensor_copy(ef[q, :, 3, :], ew[q]).then_inc(fields, 1)
            v.scalar_tensor_tensor(ef[q, :, 1, :], ei[q, 0], float(R), ei[q, 2], ALU.mult, ALU.add).then_inc(fields, 1)
            v.wait_ge(pairs_in, 32)
            v.tensor_tensor(later[q2], pair[q2, 0], pair[q2, 1], ALU.is_gt).then_inc(fields, 1)
            v.memset(m.small[:, 0:1], 0.0).then_inc(fields, 1)
            v.wait_ge(fields, 6)
            v.tensor_reduce(m.small[q2, 0:1], later[q2], AX, ALU.add).then_inc(fields, 1)
            v.wait_ge(totalled, 1)
            v.tensor_copy(m.unsorted[:, :], m.ps[0][0:1, 0:1]).then_inc(fields, 1)

        @block.tensor
        def _(pe):
            pe.wait_ge(fields, 7)
            pe.wait_ge(iotas, 4)
            pe.matmul(m.ps[0][:, 0:1], m.ones[:, :], m.small[:, 0:1], start=True, stop=True).then_inc(totalled, 1)

        @block.sync
        def _(s):
            s.dma_start(m.HB[:, 0:NT - 1, :], a["x"][0:(NT - 1) * P].rearrange("(t p) d -> p t d", p=P)).then_inc(loaded, 16)
            s.wait_ge(zeroed, 5)
            s.dma_start(m.HB[0:LAST, NT - 1, :], a["x"][(NT - 1) * P:N]).then_inc(loaded, 16)
            full = (ERJ - 1) * ERP
            for dst, name in ((ei[:, 0], "src"), (ei[:, 1], "dst"), (ei[:, 2], "edge_type_16"), (ew, "edge_weight")):
                v = a[name]
                s.dma_start(dst[0:ERP, 0:ERJ - 1, :], v[0:full * P].rearrange("(j p e) -> p j e", p=ERP, e=P)).then_inc(edges_in, 16)
                s.dma_start(dst[0:EFULL - full, ERJ - 1, :], v[full * P:EFULL * P].rearrange("(p e) -> p e", e=P)).then_inc(edges_in, 16)
                s.dma_start(dst[EFULL - full:EFULL - full + 1, ERJ - 1, 0:EREST], v[EFULL * P:E].rearrange("(p e) -> p e", p=1)).then_inc(edges_in, 16)
            for i in range(2):
                s.dma_start(pair[q2, i], a["dst"][i:i + E - 1].rearrange("(p e) -> p e", p=PAIRP)).then_inc(pairs_in, 16)
            s.wait_ge(fields, 4)
            s.dma_start(m.edg.rearrange("(j p) (f e) -> p j f e", p=ERP, f=4), ef[0:ERP]).then_inc(stored, 16)
            s.dma_start(m.dsts.rearrange("(j p e) -> p j e", p=ERP, e=P), ef[0:ERP, :, 0, :]).then_inc(stored, 16)
            s.wait_ge(stored, 32)
            s.wait_ge(loaded, 32)
            s.dma_start(m.xs.rearrange("(t p) d -> p t d", p=P), m.HB).then_inc(stored, 16)
            s.wait_ge(stored, 48)
            s.wait_ge(fields, 8)


def sort_edges(nc, ctx, m):
    sem = lambda n: semaphore(nc, m, f"so_{n}")
    loaded, chunk_in, chunk_used, ranked, placed, moved, iotas, carry = (sem(n) for n in (
        "loaded", "chunk_in", "chunk_used", "ranked", "placed", "moved", "iotas", "carry"))
    NC = 16
    CE = ETILES * P // NC
    dch, pos = m.AGG[:, 0:CE], m.AGG[:, CE:2 * CE]
    mask = m.WT[:, 0:CE]
    rec = m.SC[:, 0:4 * ETILES].rearrange("p (i f) -> p i f", f=4)
    rank, mine = m.SC[:, 4 * ETILES:5 * ETILES], m.SC[:, 5 * ETILES:6 * ETILES]
    less, same = m.small[:, 0:1], m.small[:, 1:2]
    one_rec, one_rank = m.small[:, 4:8], m.smalli[:, 0:1]
    dcol = rec[:, :, 0]
    with nc.Block() as block:
        @block.sync
        def _(s):
            unsorted = s.value_load(m.unsorted[0:1, 0:1], min_val=0, max_val=E)
            with s.If(unsorted > 0):
                for f in range(4):
                    s.dma_start(rec[:, :, f], m.edg[:, f * P:(f + 1) * P].rearrange("i e -> e i")).then_inc(loaded, 16)
                with s.Fori(0, NC) as c:
                    s.wait_ge(chunk_used, c + 1)
                    s.dma_start(dch, m.dsts[bass.ds(c * CE, CE)].partition_broadcast(P)).then_inc(chunk_in, 16)
                s.wait_ge(placed, 16 * ETILES)
                with s.Fori(0, ETILES) as i:
                    s.dma_start(m.edg[bass.ds(i, 1), :].rearrange("o (f e) -> (o f) e", f=4),
                                m.srec[bass.ds(i * P, P), :].rearrange("e f -> f e")).then_inc(moved, 16)
                    s.wait_ge(moved, i * 16 + 16)
                    s.sem_inc(carry, 1)
            s.nop()

        @block.vector
        def _(v):
            unsorted = v.value_load(m.unsorted[0:1, 0:1], min_val=0, max_val=E)
            with v.If(unsorted > 0):
                v.sem_inc(chunk_used, 1)
                v.wait_ge(iotas, 2)
                v.wait_ge(loaded, 64)
                v.memset(rank, 0.0)
                with v.Fori(0, NC) as c:
                    v.wait_ge(chunk_in, c * 16 + 16)
                    v.sem_inc(carry, 1)
                    with v.Fori(0, ETILES) as i:
                        v.drain()
                        v.tensor_scalar(mask, pos, col(mine, i), None, ALU.is_lt)
                        v.drain()
                        v.scalar_tensor_tensor(mask, dch, col(dcol, i), mask, ALU.is_equal, ALU.mult, accum_out=same)
                        v.drain()
                        v.tensor_scalar(mask, dch, col(dcol, i), 0.0, ALU.is_lt, ALU.add, accum_out=less)
                        v.drain()
                        v.tensor_tensor(col(rank, i), col(rank, i), same, ALU.add)
                        v.drain()
                        v.tensor_tensor(col(rank, i), col(rank, i), less, ALU.add)
                    v.drain()
                    v.tensor_scalar(mine, mine, -float(CE), None, ALU.add).then_inc(chunk_used, 1)
                v.drain()
                v.sem_inc(ranked, 1)
            v.nop()

        @block.gpsimd
        def _(g):
            unsorted = g.value_load(m.unsorted[0:1, 0:1], min_val=0, max_val=E)
            with g.If(unsorted > 0):
                g.iota(pos, [[1, CE]], base=0, channel_multiplier=0, allow_small_or_imprecise_dtypes=True).then_inc(iotas, 1)
                g.iota(mine, [[P, ETILES]], base=0, channel_multiplier=1, allow_small_or_imprecise_dtypes=True).then_inc(iotas, 1)
                g.wait_ge(ranked, 1)
                with g.Fori(0, ETILES) as i:
                    g.drain()
                    g.tensor_copy(one_rank, col(rank, i))
                    g.tensor_copy(one_rec, rec[:, bass.ds(i, 1), :].rearrange("p i f -> p (i f)"))
                    g.drain()
                    g.indirect_dma_start(m.srec, bass.IndirectOffsetOnAxis(ap=one_rank, axis=0), one_rec, None).then_inc(placed, 16)
                    g.wait_ge(placed, i * 16 + 16)
                    g.sem_inc(carry, 1)
            g.nop()


def schedule(nc, ctx, m):
    sem = lambda n: semaphore(nc, m, n)
    rows_in, iotas, v_done, idx_ready, rows_got, turned, copied, stored = (sem(n) for n in (
        "sc_rows_in", "sc_iotas", "sc_vector", "sc_idx", "sc_rows", "sc_turned", "sc_copied", "sc_stored"))
    ends_in, ends, ends_out = (sem(n) for n in ("sc_ends_in", "sc_ends", "sc_ends_out"))
    t = ETILES
    ln, aw, pin, dif, junk, io = (m.WT[:, i * t:(i + 1) * t] for i in range(6))
    scol, icol, wcol, ncol, vcol = (m.small[0:SP_, i * SJ:(i + 1) * SJ] for i in range(5))
    wint = m.smalli[0:SP_, 0:SJ]
    iint = m.smalli[0:SP_, SJ:2 * SJ]
    gr = m.SC[0:SP_, 0:SJ * 4 * P].rearrange("p (j f) -> p j f", j=SJ)
    rel = m.G[0:SP_, 0:SJ * P].rearrange("p (j e) -> p j e", j=SJ)
    tabs = (m.TDR, m.TCI, m.TSI, m.TEA)
    with nc.Block() as block:
        @block.sync
        def _(s):
            for j, e in ((0, 0), (1, P - 1)):
                s.dma_start(m.ab[0:ERP, j, :], m.edg[:, e:e + 1].rearrange("(j p) e -> p (j e)", p=ERP)).then_inc(ends_in, 16)
            s.wait_ge(ends, 4)
            for j in range(2):
                s.dma_start(m.abd[j].rearrange("(j p) -> p j", p=ERP), m.ab[0:ERP, j, :]).then_inc(ends_out, 16)
            s.wait_ge(ends_out, 32)
            s.dma_start(aw, m.abd[0].partition_broadcast(P)).then_inc(rows_in, 16)
            s.dma_start(ln, m.abd[1].partition_broadcast(P)).then_inc(rows_in, 16)
            s.wait_ge(rows_got, 16 * SJ)
            s.dma_start(m.keyd.rearrange("(j p) e -> p j e", p=SP_), gr[:, :, 0:P]).then_inc(stored, 16)
            s.wait_ge(v_done, 4 + 6 * SJ)
            s.dma_start(m.reld.rearrange("(j p) e -> p j e", p=SP_), rel).then_inc(stored, 16)
            s.dma_start(m.wind.rearrange("(j p) -> p j", p=SP_), wint).then_inc(stored, 16)
            s.wait_ge(stored, 48)
            s.dma_start(m.win[:, :], m.wind.rearrange("(a s) -> a s", a=1)).then_inc(rows_in, 16)
            s.wait_ge(rows_in, 48)

        @block.gpsimd
        def _(g):
            g.iota(scol, [[SP_, SJ]], base=0, channel_multiplier=1, allow_small_or_imprecise_dtypes=True).then_inc(iotas, 1)
            g.iota(io, [[1, t]], base=0, channel_multiplier=0, allow_small_or_imprecise_dtypes=True).then_inc(iotas, 1)
            g.wait_ge(idx_ready, 1)
            for j in range(SJ):
                g.indirect_dma_start(gr[:, j, :], None, m.edg, bass.IndirectOffsetOnAxis(ap=iint[:, j:j + 1], axis=0)).then_inc(rows_got, 16)

        @block.vector
        def _(v):
            q = slice(0, ERP)
            v.wait_ge(ends_in, 32)
            v.tensor_copy(m.abi[q, :, :], m.ab[q, :, :]).then_inc(ends, 1)
            v.wait_ge(ends, 1)
            v.tensor_scalar(m.abi[q, :, :], m.abi[q, :, :], P.bit_length() - 1, None, ALU.arith_shift_right).then_inc(ends, 1)
            v.wait_ge(ends, 2)
            v.tensor_copy(m.ab[q, :, :], m.abi[q, :, :]).then_inc(ends, 1)
            v.wait_ge(ends, 3)
            v.scalar_tensor_tensor(m.ab[q, 1, :], m.ab[q, 1, :], 1.0, m.ab[q, 0, :], ALU.add, ALU.subtract).then_inc(ends, 1)
            v.wait_ge(rows_in, 32)
            v.wait_ge(iotas, 2)
            v.tensor_tensor_scan(pin, m.ones[:, 0:1].broadcast_to([P, t]), ln, 0.0, ALU.mult, ALU.add).then_inc(v_done, 1)
            v.tensor_tensor(dif, aw, ln, ALU.add).then_inc(v_done, 1)
            v.wait_ge(v_done, 2)
            v.tensor_tensor(dif, dif, pin, ALU.subtract).then_inc(v_done, 1)
            for j in range(SJ):
                v.wait_ge(v_done, 3 + j)
                v.tensor_scalar(junk[0:SP_], pin[0:SP_], scol[:, j:j + 1], 0.0, ALU.is_le, ALU.add,
                                accum_out=icol[:, j:j + 1]).then_inc(v_done, 1)
            v.wait_ge(v_done, 3 + SJ)
            v.tensor_scalar(icol, icol, float(t - 1), None, ALU.min).then_inc(v_done, 1)
            v.wait_ge(v_done, 4 + SJ)
            v.tensor_copy(iint, icol).then_inc(idx_ready, 1)
            for j in range(SJ):
                v.wait_ge(v_done, 4 + SJ + j)
                v.scalar_tensor_tensor(junk[0:SP_], io[0:SP_], icol[:, j:j + 1], dif[0:SP_], ALU.is_equal, ALU.mult,
                                       accum_out=vcol[:, j:j + 1]).then_inc(v_done, 1)
            v.wait_ge(v_done, 4 + 2 * SJ)
            v.tensor_tensor(wcol, vcol, scol, ALU.add).then_inc(v_done, 1)
            v.wait_ge(v_done, 5 + 2 * SJ)
            v.tensor_scalar(ncol, wcol, -float(P), None, ALU.mult).then_inc(v_done, 1)
            v.tensor_scalar(wcol, wcol, float(NT - 1), None, ALU.min).then_inc(v_done, 1)
            v.wait_ge(v_done, 7 + 2 * SJ)
            v.tensor_copy(wint, wcol).then_inc(v_done, 1)
            v.wait_ge(rows_got, 16 * SJ)
            for j in range(SJ):
                v.tensor_scalar(rel[:, j, :], gr[:, j, 0:P], ncol[:, j:j + 1], None, ALU.add).then_inc(v_done, 1)
            for j in range(SJ):
                v.wait_ge(turned, j + 1)
                last = None
                for f, tab in enumerate(tabs):
                    last = v.tensor_copy(tab[:, j * SP_:(j + 1) * SP_], m.ps[j % 2][:, f * SP_:(f + 1) * SP_])
                    if f < 3:
                        last.then_inc(v_done, 1)
                last.then_inc(copied, 1)

        @block.tensor
        def _(pe):
            pe.wait_ge(v_done, 8 + 3 * SJ)
            for j in range(SJ):
                if j >= 2:
                    pe.wait_ge(copied, j - 1)
                for f in range(4):
                    src = rel[:, j, :] if f == 0 else gr[:, j, f * P:(f + 1) * P]
                    last = pe.transpose(m.ps[j % 2][:, f * SP_:(f + 1) * SP_], src, m.ident[0:SP_, 0:SP_])
                last.then_inc(turned, 1)


UNROLL = 7
assert NT % UNROLL == 0


def row_tiles(v, body):
    with v.Fori(0, NT // UNROLL) as i:
        for k in range(UNROLL):
            body(i * UNROLL + k)


def finish_moments(v, m, c, done, stats_in, root_done, turn, again=False):
    st, mean, var, rstd, tmp = m.st, m.mean, m.var, m.rstd, m.tmp
    v.wait_ge(done, c)
    v.tensor_tensor(tmp[:, :], st[:, :, 1], st[:, :, 4], ALU.subtract).then_inc(done, 1)
    v.tensor_tensor(mean[:, :], st[:, :, 1], st[:, :, 4], ALU.add).then_inc(done, 1)
    v.tensor_tensor(var[:, :], st[:, :, 2], st[:, :, 5], ALU.add).then_inc(done, 1)
    v.wait_ge(done, c + 3)
    v.tensor_tensor(tmp[:, :], tmp[:, :], tmp[:, :], ALU.mult).then_inc(done, 1)
    v.tensor_scalar(mean[:, :], mean[:, :], 0.5, None, ALU.mult).then_inc(done, 1)
    v.tensor_scalar(var[:, :], var[:, :], 1.0 / D, None, ALU.mult).then_inc(done, 1)
    v.wait_ge(done, c + 6)
    v.scalar_tensor_tensor(var[:, :], tmp[:, :], 0.25, var[:, :], ALU.mult, ALU.add).then_inc(done, 1)
    v.wait_ge(done, c + 7)
    v.tensor_scalar(tmp[:, :], var[:, :], EPS, None, ALU.add).then_inc(stats_in, 1)
    v.wait_ge(root_done, turn)
    v.reciprocal(rstd[:, :], rstd[:, :]).then_inc(done, 1)
    v.wait_ge(done, c + 8)
    if again:
        v.tensor_copy(m.mean4, mean).then_inc(done, 1)
        v.tensor_copy(m.rstd4, rstd).then_inc(done, 1)
        v.tensor_tensor(var, var, rstd, ALU.mult).then_inc(done, 1)
        v.wait_ge(done, c + 11)
        v.tensor_tensor(var, var, rstd, ALU.mult).then_inc(done, 1)
        v.wait_ge(done, c + 12)
        v.tensor_scalar(tmp, var, EPS, None, ALU.add).then_inc(stats_in, 1)
        v.wait_ge(root_done, turn + 1)
        v.reciprocal(rstd, rstd).then_inc(done, 1)
        v.wait_ge(done, c + 13)
        v.tensor_tensor(rstd, rstd, m.rstd4, ALU.mult).then_inc(done, 1)
        v.wait_ge(done, c + 14)


def moments(nc, ctx, m, name, src=None, make=None, nmake=0, again=False):
    sem = lambda n: semaphore(nc, m, f"{name}_{n}")
    done, stats_in, root_done = (sem(n) for n in ("vector", "variance", "root"))
    with nc.Block() as block:
        @block.scalar
        def _(s):
            for i in range(2 if again else 1):
                s.wait_ge(stats_in, i + 1)
                s.activation(m.rstd[:, :], m.tmp[:, :], ACT.Sqrt).then_inc(root_done, 1)

        @block.vector
        def _(v):
            if make is not None:
                make(v, done)
                v.wait_ge(done, nmake)
            c = nmake
            if src is not None:
                row_tiles(v, lambda t: v.bn_stats(at(m.st, t), at(src, t)).then_inc(done, 1))
                c += NT
            finish_moments(v, m, c, done, stats_in, root_done, 1, again)


def standardise(v, m, x, t, out, chain, ready, affine=True, relu=False):
    if not affine:
        v.tensor_scalar(out, at(x, t), col(m.mean, t), col(m.rstd, t), ALU.subtract, ALU.mult).then_inc(ready, 1)
        return
    n = 2 if relu else 1
    v.scalar_tensor_tensor(out, at(x, t), col(m.mean, t), m.VG[:, :], ALU.subtract, ALU.mult).then_inc(chain, 1)
    v.wait_ge(chain, t * n + 1)
    if not relu:
        v.scalar_tensor_tensor(out, out, col(m.rstd, t), m.VB[:, :], ALU.mult, ALU.add).then_inc(ready, 1)
        return
    v.scalar_tensor_tensor(out, out, col(m.rstd, t), m.VB[:, :], ALU.mult, ALU.add).then_inc(chain, 1)
    v.wait_ge(chain, t * n + 2)
    v.tensor_scalar(out, out, 0.0, None, ALU.max).then_inc(ready, 1)


def basis_area(m):
    return m.SC[:, 0:B * C2 * D].rearrange("p (b c o) -> p b c o", b=B, c=C2)


def relation_weights(nc, ctx, m, l, basis, att):
    sem = lambda n: semaphore(nc, m, f"rw{l}_{n}")
    loaded, mixed = sem("loaded"), sem("mixed")
    bs = basis_area(m)
    wt = m.WT.rearrange("p (c r o) -> p c r o", c=C2, r=R)
    with nc.Block() as block:
        @block.sync
        def _(s):
            for b in range(B):
                s.dma_start(bs[:, b], basis[b].rearrange("(c p) o -> p c o", p=P)).then_inc(loaded, 16)
            s.dma_start(m.ATT[:, :], att.rearrange("r b -> (r b)").partition_broadcast(P)).then_inc(loaded, 16)
            s.wait_ge(loaded, 16 * (B + 1))

        @block.vector
        def _(v):
            v.wait_ge(loaded, 16 * (B + 1))
            for b in range(B):
                for r in range(R):
                    w = m.ATT[:, r * B + b:r * B + b + 1]
                    if b == 0:
                        v.tensor_scalar(wt[:, :, r, :], bs[:, b], w, None, ALU.mult).then_inc(mixed, 1)
                    else:
                        v.wait_ge(mixed, (b - 1) * R + r + 1)
                        v.scalar_tensor_tensor(wt[:, :, r, :], bs[:, b], w, wt[:, :, r, :], ALU.mult, ALU.add).then_inc(mixed, 1)


def relation_product(nc, ctx, m, l, root, bias, affine):
    sem = lambda n: semaphore(nc, m, f"rp{l}_{n}")
    staged, turned, turn_free, group_done, group_read, root_done, root_read = (sem(n) for n in (
        "staged", "turned", "turn_read", "group_done", "group_read", "root_done", "root_read"))
    stored = [sem(f"stored{g}") for g in range(4)]
    loaded, chain, biased = sem("loaded"), sem("vector"), sem("biased")
    bias_row = m.G[:, 0:D]
    nloads = 4 if affine else 2
    wt = m.WT.rearrange("p (c r o) -> p c r o", c=C2, r=R)
    hst = m.SC[:, 0:4 * 1024].rearrange("p (g n) -> p g n", g=4)
    hs = m.SC[:, 4096:4096 + 512].rearrange("p (k d) -> p k d", k=2)
    ht = m.SC[:, 4608:4608 + 512].rearrange("p (k c n) -> p k c n", k=2, c=C2)
    psT, psR = (m.ps[4], m.ps[6]), (m.ps[5], m.ps[7])
    with nc.Block() as block:
        @block.tensor
        def _(pe):
            pe.wait_ge(loaded, 16 * nloads)
            pe.sem_inc(turned, 2)
            pe.sem_inc(root_done, 2)

            def turn(t, k):
                pe.wait_ge(staged, t + 1)
                pe.wait_ge(turn_free, t + 1)
                for c in range(C2):
                    last = pe.transpose(psT[k][:, c * P:(c + 1) * P], hs[:, k, c * P:(c + 1) * P], m.ident[:, :])
                last.then_inc(turned, 1)

            def group(t, k, g):
                pe.wait_ge(group_read, t * 4 + g + 1)
                for c in range(C2):
                    for b in range(2):
                        r = 4 * g + 2 * b
                        last = pe.matmul(m.ps[2 * (g % 2) + b][:, :], ht[:, k, c, :],
                                         wt[:, c, r:r + 2, :].rearrange("p r o -> p (r o)"), start=(c == 0), stop=(c == 1))
                last.then_inc(group_done, 1)

            turn(0, 0)

            def body(t, k, last):
                pe.wait_ge(turn_free, t + 3)
                group(t, k, 0)
                group(t, k, 1)
                if not last:
                    turn(t + 1, 1 - k)
                group(t, k, 2)
                group(t, k, 3)
                pe.wait_ge(root_read, t + 1)
                for c in range(C2):
                    mm = pe.matmul(psR[k][:, 0:D], ht[:, k, c, :], m.ROOT[:, c, :], start=(c == 0), stop=(c == 1))
                mm.then_inc(root_done, 1)
            tiles(pe, body)

        @block.scalar
        def _(s):
            s.sem_inc(group_read, 2)

            def body(t, k, last):
                for g in range(4):
                    s.wait_ge(group_done, t * 4 + g + 1)
                    s.wait_ge(stored[g], t * 16 + 16)
                    for b in range(2):
                        if g == 3 and b == 1:
                            s.activation(at(m.AGG3, t)[:, 0:D], m.ps[3][:, D:2 * D], ACT.Copy)
                        mm = s.activation(hst[:, g, b * 512:(b + 1) * 512], m.ps[2 * (g % 2) + b][:, :], ACT.Copy)
                    mm.then_inc(group_read, 1)
            tiles(s, body)

        @block.vector
        def _(v):
            v.sem_inc(turn_free, 2)
            v.sem_inc(root_read, 2)

            def turn_out(t, k):
                v.wait_ge(turned, t + 3)
                v.wait_ge(root_done, t + 1)
                v.tensor_copy(ht[:, k].rearrange("p c n -> p (c n)"), psT[k][:, 0:D]).then_inc(turn_free, 1)

            def stage(t, k):
                standardise(v, m, m.HB, t, hs[:, k, :], chain, staged, affine=affine, relu=affine)

            v.wait_ge(loaded, 16 * nloads)
            stage(0, 0)
            turn_out(0, 0)

            def body(t, k, last):
                v.wait_ge(staged, t + 1)
                v.tensor_tensor(at(m.HB, t), hs[:, k, :], bias_row, ALU.add).then_inc(biased, 1)
                if not last:
                    stage(t + 1, 1 - k)
                    turn_out(t + 1, 1 - k)
                v.wait_ge(biased, t + 1)
                v.wait_ge(root_done, t + 3)
                v.tensor_tensor(at(m.HB, t), psR[k][:, 0:D], at(m.HB, t), ALU.add).then_inc(root_read, 1)
            tiles(v, body)

        @block.sync
        def _(s):
            s.dma_start(m.ROOT, root.rearrange("(c p) o -> p c o", p=P)).then_inc(loaded, 16)
            s.dma_start(bias_row, bias.partition_broadcast(P)).then_inc(loaded, 16)
            if affine:
                for row, x in zip((m.VG, m.VB), affine):
                    s.dma_start(row[:, :], x.partition_broadcast(P)).then_inc(loaded, 16)
            for g in range(4):
                s.sem_inc(stored[g], 16)

            def body(t, k, last):
                for g in range(4):
                    s.wait_ge(group_read, t * 4 + g + 3)
                    s.dma_start(m.hrel[bass.ds(t * P, P), g * 1024:(g + 1) * 1024], hst[:, g, :]).then_inc(stored[g], 16)
            tiles(s, body)
            for g in range(4):
                s.wait_ge(stored[g], 16 * (NT + 1))


def relation_sum(nc, ctx, m, l, basis=None, att=None):
    sem = lambda n: semaphore(nc, m, f"rs{l}_{n}")
    idx_ready, scaled, onehot, summed, added = (sem(n) for n in ("idx", "scaled", "onehot", "summed", "added"))
    asked = sem("asked")
    landed = [sem(f"landed{k}") for k in range(BATCH)]
    init = sem("init")
    rows = m.hrel.rearrange("n (r o) -> (n r) o", r=R)
    g8 = m.G.rearrange("p (k d) -> p k d", k=BATCH)
    gs, oh, ix = m.GS, m.OH, m.IX
    mixing = basis is not None
    bs = basis_area(m)
    wt = m.WT.rearrange("p (c r o) -> p c r o", c=C2, r=R)
    basis_in, mixed = sem("basis_in"), sem("mixed")
    with nc.Block() as block:
        @block.sync
        def _(s):
            if mixing:
                for b in range(B):
                    s.dma_start(bs[:, b], basis[b].rearrange("(c p) o -> p c o", p=P)).then_inc(basis_in, 16)
                s.dma_start(m.ATT[:, :], att.rearrange("r b -> (r b)").partition_broadcast(P)).then_inc(basis_in, 16)
            s.nop()

        @block.scalar
        def _(s):
            s.sem_inc(scaled, BATCH)
            for k in range(BATCH):
                s.activation(gs[:, k, D:D + 1], m.ones[:, 0:1], ACT.Copy).then_inc(init, 1)
            s.activation(ix[:, 0, :], m.TCI[:, 0:BATCH], ACT.Copy).then_inc(idx_ready, 1)

            def body(b, q, last):
                if not last:
                    s.activation(ix[:, 1 - q, :], m.TCI[:, bass.ds(b * BATCH + BATCH, BATCH)], ACT.Copy).then_inc(idx_ready, 1)
                for k in range(BATCH):
                    st = b * BATCH + k
                    s.wait_ge(landed[k], b * 16 + 16)
                    s.wait_ge(summed, st + 1)
                    s.activation(gs[:, k, 0:D], g8[:, k, :], ACT.Copy, scale=col(m.TEA, st)).then_inc(scaled, 1)
            batches(s, body)

        @block.gpsimd
        def _(g):
            def body(b, q, last):
                g.wait_ge(idx_ready, b + 1)
                for k in range(BATCH):
                    g.wait_ge(scaled, b * BATCH + k + 1)
                    g.sem_inc(asked, 1)
                    g.indirect_dma_start(g8[:, k, :], None, rows, bass.IndirectOffsetOnAxis(ap=ix[:, q, k:k + 1], axis=0)).then_inc(landed[k], 16)
            batches(g, body)

        @block.vector
        def _(v):
            v.sem_inc(added, BATCH)
            if l == 1:
                v.memset(m.AGG3[:, :, D:D + 1], 1.0)
            one_hots(v, m, 0, 0, onehot)

            def body(b, q, last):
                if not last:
                    one_hots(v, m, b + 1, 1 - q, onehot)
                add_windows(nc, v, m, b, summed, added, D + 1 if l == 1 else D)
            if not mixing:
                batches(v, body)
            else:
                v.memset(m.WT, 0.0).then_inc(mixed, 1)
                v.wait_ge(basis_in, 16 * (B + 1))
                with v.Fori(0, B) as b:
                    with v.Fori(0, R // 4) as i:
                        for q in range(2):
                            batch = b * (R // 2) + i * 2 + q
                            body(batch, q, False)
                            for n in range(2):
                                r = i * 4 + q * 2 + n
                                v.wait_ge(mixed, b * R + 1)
                                w = wt[:, :, bass.ds(r, 1), :].rearrange("p c a o -> p c (a o)")
                                base = bs[:, bass.ds(b, 1), :, :].rearrange("p a c o -> p (a c) o")
                                v.scalar_tensor_tensor(w, base, col(m.ATT, r * B + b), w, ALU.mult, ALU.add).then_inc(mixed, 1)
                with v.Fori(B * R // 4, NBATCH // 2 - 1) as i:
                    for q in range(2):
                        body(i * 2 + q, q, False)
                body(NBATCH - 2, 0, False)
                body(NBATCH - 1, 1, True)

        @block.tensor
        def _(pe):
            pe.sem_inc(summed, BATCH)
            pe.wait_ge(init, BATCH)

            def body(b, q, last):
                pe.wait_ge(onehot, b + 1)
                for k in range(BATCH):
                    st = b * BATCH + k
                    pe.wait_ge(scaled, st + 1 + BATCH)
                    pe.wait_ge(added, st + 1)
                    pe.matmul(m.ps[k][:, 0:D + 1], oh[:, q, k, :], gs[:, k, 0:D + 1], start=True, stop=True).then_inc(summed, 1)
            batches(pe, body)


def one_hots(v, m, b, q, onehot):
    v.tensor_tensor(m.OH[:, q], m.iota[:, :].unsqueeze(1).broadcast_to([P, BATCH, P]),
                    m.TDR[:, bass.ds(b * BATCH, BATCH)].unsqueeze(2).broadcast_to([P, BATCH, P]), ALU.is_equal).then_inc(onehot, 1)


def windows(nc, m, engine, st, n):
    _, values = nc.values_load_multi_w_load_instructions(m.win[0:1, bass.ds(st, n)], engines=[engine], min_val=0, max_val=NT - 1)
    return values


def add_window(v, m, b, k, w, summed, added, width):
    st = b * BATCH + k
    v.wait_ge(summed, st + 1 + BATCH)
    v.wait_ge(added, st + BATCH)
    acc = at(m.AGG3, w)[:, 0:width]
    v.tensor_tensor(acc, m.ps[k][:, 0:width], acc, ALU.add).then_inc(added, 1)


def add_windows(nc, v, m, b, summed, added, width):
    for half in range(2):
        for k, w in enumerate(windows(nc, m, mybir.EngineType.DVE, b * BATCH + half * 4, 4), half * 4):
            add_window(v, m, b, k, w, summed, added, width)


def residual_norm(nc, ctx, m, a):
    sem = lambda n: semaphore(nc, m, f"rn_{n}")
    loaded, x_in, done, stats_in, root_done, joined, stored = (sem(n) for n in (
        "loaded", "x_in", "vector", "variance", "root", "joined", "stored"))
    with nc.Block() as block:
        @block.sync
        def _(s):
            s.dma_start(m.VG[:, :], a["L0_gnn_ln2_g"].partition_broadcast(P)).then_inc(loaded, 16)
            s.dma_start(m.VB[:, :], a["L0_gnn_ln2_b"].partition_broadcast(P)).then_inc(loaded, 16)
            s.dma_start(m.XV, m.xs.rearrange("(t p) d -> p t d", p=P)).then_inc(x_in, 16)
            s.wait_ge(joined, 1)
            s.dma_start(m.x1.rearrange("(t p) d -> p t d", p=P), m.XV).then_inc(stored, 16)
            s.wait_ge(stored, 16)

        @block.scalar
        def _(s):
            s.wait_ge(stats_in, 1)
            s.activation(m.rstd[:, :], m.tmp[:, :], ACT.Sqrt).then_inc(root_done, 1)

        @block.vector
        def _(v):
            v.wait_ge(loaded, 32)
            row_tiles(v, lambda t: v.scalar_tensor_tensor(at(m.HB, t), at(m.HB, t), col(m.mean, t), m.VG[:, :],
                                                          ALU.subtract, ALU.mult).then_inc(done, 1))
            v.wait_ge(done, NT)
            row_tiles(v, lambda t: v.scalar_tensor_tensor(at(m.HB, t), at(m.HB, t), col(m.rstd, t), m.VB[:, :],
                                                          ALU.mult, ALU.add).then_inc(done, 1))
            v.wait_ge(done, 2 * NT)
            v.wait_ge(x_in, 16)
            v.scalar_tensor_tensor(m.XV, m.HB, 0.0, m.XV, ALU.max, ALU.add).then_inc(joined, 1)
            v.wait_ge(joined, 1)
            row_tiles(v, lambda t: v.bn_stats(at(m.st, t), at(m.XV, t)).then_inc(done, 1))
            finish_moments(v, m, 3 * NT, done, stats_in, root_done, 1)
            row_tiles(v, lambda t: v.tensor_scalar(at(m.HB, t), at(m.XV, t), col(m.mean, t), col(m.rstd, t),
                                                   ALU.subtract, ALU.mult).then_inc(done, 1))


def select_rows(nc, ctx, m, a):
    sem = lambda n: semaphore(nc, m, f"sl_{n}")
    loaded, done, pe_done, stored, iot = (sem(n) for n in ("loaded", "vector", "tensor", "stored", "iota"))
    W = m.MW
    s = m.small
    all_w = m.WT[:, 0:NP]
    key = m.SC[:, 0:NP]
    cnt, kk, m1, b1, T, cand, fl, tf = (s[:, i:i + 1] for i in range(8))
    Ti, ci, ii, one_i = (m.smalli[:, i:i + 1] for i in range(4))
    eq, gt, pre, off = (m.SEL[:, i * NT:(i + 1) * NT] for i in range(4))
    shifts = ((24, 7), (18, 6), (12, 6), (6, 6), (0, 6))
    wrb = m.VG
    with nc.Block() as block:
        @block.gpsimd
        def _(g):
            g.iota(ii, [[0, 1]], base=0, channel_multiplier=1).then_inc(iot, 1)

        @block.sync
        def _(e):
            e.dma_start(wrb[:, :], a["L0_ffn_wr"].rearrange("d o -> (d o)").partition_broadcast(P)).then_inc(loaded, 16)
            e.dma_start(b1, a["L0_ffn_br"].partition_broadcast(P)).then_inc(loaded, 16)
            e.wait_ge(done, 6)
            e.dma_start(m.wd.rearrange("(t p) -> p t", p=P), m.SEL[:, 0:NT]).then_inc(stored, 16)
            e.wait_ge(stored, 16)
            e.dma_start(all_w, m.wd.partition_broadcast(P)).then_inc(loaded, 16)

        @block.vector
        def _(v):
            c = [0]

            def step(ins):
                c[0] += 1
                ins.then_inc(done, 1)
                v.wait_ge(done, c[0])
            v.wait_ge(loaded, 32)
            v.wait_ge(iot, 1)
            step(v.tensor_tensor(m.XV, m.HB, wrb[:, :].unsqueeze(1).broadcast_to([P, NT, D]), ALU.mult))
            step(v.tensor_reduce(W, m.XV, AX, ALU.add))
            step(v.tensor_scalar(W, W, b1, None, ALU.add))
            step(v.tensor_tensor(eq, W, m.valid[:, :], ALU.mult))
            step(v.tensor_scalar(gt, m.valid[:, :], 1.0, BIG, ALU.subtract, ALU.mult))
            step(v.tensor_tensor(eq, eq, gt, ALU.add))
            v.wait_ge(loaded, 48)
            step(v.tensor_scalar(key, all_w, 0.0, 0.0, ALU.is_ge, ALU.add, accum_out=cnt))
            step(v.tensor_scalar(m1, cnt, float(TOPK), None, ALU.is_ge))
            step(v.tensor_scalar(fl, m1, 2.0, 1.0, ALU.mult, ALU.subtract))
            step(v.tensor_scalar(kk, m1, float(2 * TOPK - N - 1), float(N + 1 - TOPK), ALU.mult, ALU.add))
            step(v.tensor_scalar(key, all_w, fl, None, ALU.mult))
            step(v.tensor_scalar(key[:, N:NP], all_w[:, N:NP], 1.0, None, ALU.mult))
            step(v.memset(Ti, 0))
            for n, (sh, bits) in enumerate(shifts):
                step(v.tensor_scalar(ci, ii, (1 << bits) - 1, sh, ALU.bitwise_and, ALU.logical_shift_left))
                step(v.tensor_tensor(ci, ci, Ti, ALU.bitwise_or))
                step(v.tensor_scalar(m.SC2, key, ci.bitcast(F32), 0.0, ALU.is_ge, ALU.add, accum_out=cnt))
                step(v.tensor_tensor(tf, cnt, kk, ALU.is_ge))
                v.wait_ge(pe_done, n + 1)
                step(v.tensor_scalar(tf, m.ps[0][:, 0:1], float(1 << bits) / P, -1.0, ALU.mult, ALU.add))
                step(v.tensor_copy(one_i, tf))
                step(v.tensor_scalar(one_i, one_i, sh, None, ALU.logical_shift_left))
                step(v.tensor_tensor(Ti, Ti, one_i, ALU.bitwise_or))
            step(v.tensor_scalar(T, Ti.bitcast(F32), fl, None, ALU.mult))
            step(v.tensor_scalar(gt, m.SEL[:, 0:NT], T, None, ALU.is_gt))
            step(v.tensor_reduce(cnt, gt, AX, ALU.add))
            step(v.tensor_scalar(eq, m.SEL[:, 0:NT], T, None, ALU.is_equal))
            v.wait_ge(pe_done, 6)
            step(v.tensor_copy(pre, m.ps[1][:, 0:NT]))
            step(v.tensor_copy(off, m.ps[1][:, 64:64 + NT]))
            step(v.tensor_copy(kk, m.ps[1][:, 128:129]))
            step(v.tensor_tensor_scan(m.tmp[:, :], m.ones[:, 0:1].broadcast_to([P, NT]), off, 0.0, ALU.mult, ALU.add))
            step(v.tensor_tensor(m.tmp[:, :], m.tmp[:, :], off, ALU.subtract))
            step(v.tensor_tensor(pre, pre, m.tmp[:, :], ALU.add))
            step(v.tensor_scalar(kk, kk, -1.0, float(TOPK), ALU.mult, ALU.add))
            step(v.tensor_scalar(pre, pre, kk, None, ALU.is_lt))
            step(v.tensor_tensor(eq, eq, pre, ALU.mult))
            step(v.tensor_tensor(eq, eq, gt, ALU.add))
            step(v.tensor_tensor(W, W, eq, ALU.mult))

        @block.tensor
        def _(pe):
            base = 13
            for n in range(len(shifts)):
                pe.wait_ge(done, base + 8 * n + 4)
                pe.matmul(m.ps[0][:, 0:1], m.ones[:, :], tf, start=True, stop=True).then_inc(pe_done, 1)
            pe.wait_ge(done, base + 8 * len(shifts) + 4)
            pe.matmul(m.ps[1][:, 0:NT], m.upper[:, :], eq, start=True, stop=True)
            pe.matmul(m.ps[1][:, 64:64 + NT], m.ones[:, :], eq, start=True, stop=True)
            pe.matmul(m.ps[1][:, 128:129], m.ones[:, :], cnt, start=True, stop=True).then_inc(pe_done, 1)


def feed_forward(nc, ctx, m, name, src, w1, b1, w2, b2, act, out_steps, nout, result, xv, spill, affine=None):
    sem = lambda n: semaphore(nc, m, f"{name}_{n}")
    loaded, staged, turned, turn_read, up, gelu, down, outs = (sem(n) for n in (
        "loaded", "staged", "turned", "turn_read", "up", "gelu", "down", "outs"))
    F = DFF // P
    xv_in, chain, stats, spilled = (sem(n) for n in ("xv_in", "vector", "stats", "spilled"))
    W1 = m.WT[:, 0:C2 * DFF].rearrange("p (c f) -> p c f", c=C2)
    W2 = m.WT[:, 2048:2048 + F * D].rearrange("p (f d) -> p f d", f=F)
    hid = m.SC[:, 0:2 * DFF].rearrange("p (k f n) -> p k f n", k=2, f=F)
    hs = m.SC[:, 4096:4096 + 512].rearrange("p (k d) -> p k d", k=2)
    ht = m.SC[:, 4608:4608 + 512].rearrange("p (k c n) -> p k c n", k=2, c=C2)
    nloads = 6 if affine else 4
    b1c = m.small[:, 0:F]
    psT, psY = (m.ps[4], m.ps[6]), (m.ps[5], m.ps[7])
    with nc.Block() as block:
        @block.sync
        def _(s):
            s.dma_start(W1, w1.rearrange("(c p) f -> p c f", p=P)).then_inc(loaded, 16)
            s.dma_start(W2, w2.rearrange("(f p) d -> p f d", p=P)).then_inc(loaded, 16)
            s.dma_start(b1c, b1.rearrange("(f p) -> p f", p=P)).then_inc(loaded, 16)
            s.dma_start(m.BO, b2.partition_broadcast(P)).then_inc(loaded, 16)
            if affine:
                for row, x in zip((m.VG, m.VB), affine):
                    s.dma_start(row[:, :], x.partition_broadcast(P)).then_inc(loaded, 16)
            s.dma_start(m.XV, xv.rearrange("(t p) d -> p t d", p=P)).then_inc(xv_in, 16)

            def body(t, k, last):
                s.wait_ge(outs, t * nout + 3 * nout)
                s.dma_start(spill[bass.ds(t * P, P), :], at(result, t)).then_inc(spilled, 16)
            tiles(s, body)
            s.wait_ge(spilled, 16 * NT)

        @block.gpsimd
        def _(g):
            def body(t, k, last):
                g.wait_ge(turned, t + 1)
                g.tensor_copy(hs[:, k, :], at(src, t)).then_inc(staged, 1)
            if not affine:
                tiles(g, body)
            g.nop()

        @block.tensor
        def _(pe):
            pe.wait_ge(loaded, nloads * 16)
            pe.sem_inc(turned, 2)
            pe.sem_inc(down, 2)

            def turn(t, k):
                pe.wait_ge(staged, t + 1)
                pe.wait_ge(turn_read, t + 1)
                for c in range(C2):
                    last = pe.transpose(psT[k][:, c * P:(c + 1) * P], hs[:, k, c * P:(c + 1) * P], m.ident[:, :])
                last.then_inc(turned, 1)

            turn(0, 0)

            def body(t, k, last):
                pe.wait_ge(turn_read, t + 3)
                for f in range(F):
                    if f % 4 == 0:
                        pe.wait_ge(gelu, t * F + f + 4)
                    for c in range(C2):
                        mm = pe.matmul(m.ps[2 * k + f // 4][:, (f % 4) * P:(f % 4 + 1) * P], W1[:, c, f * P:(f + 1) * P], ht[:, k, c, :],
                                       start=(c == 0), stop=(c == 1))
                    if f % 4 == 3:
                        mm.then_inc(up, 1)
                if not last:
                    turn(t + 1, 1 - k)
                pe.wait_ge(outs, t * nout + 1)
                for f in range(F):
                    pe.wait_ge(gelu, t * F + f + 1 + 2 * F)
                    mm = pe.matmul(psY[k][:, 0:D], hid[:, k, f, :], W2[:, f, :], start=(f == 0), stop=(f == F - 1))
                mm.then_inc(down, 1)
            tiles(pe, body)

        @block.scalar
        def _(s):
            s.wait_ge(loaded, nloads * 16)
            s.sem_inc(gelu, 2 * F)

            def body(t, k, last):
                s.wait_ge(down, t + 1)
                for f in range(F):
                    if f % 4 == 0:
                        s.wait_ge(up, t * 2 + f // 4 + 1)
                    s.activation(hid[:, k, f, :], m.ps[2 * k + f // 4][:, (f % 4) * P:(f % 4 + 1) * P], act, bias=b1c[:, f:f + 1]).then_inc(gelu, 1)
            tiles(s, body)

        @block.vector
        def _(v):
            v.wait_ge(loaded, nloads * 16)
            v.sem_inc(turn_read, 2)
            v.sem_inc(outs, 2 * nout)

            def turn_out(t, k):
                v.wait_ge(turned, t + 3)
                v.wait_ge(down, t + 1)
                v.tensor_copy(ht[:, k].rearrange("p c n -> p (c n)"), psT[k][:, 0:D]).then_inc(turn_read, 1)

            def stage(t, k):
                if affine:
                    standardise(v, m, src, t, hs[:, k, :], chain, staged)

            stage(0, 0)
            turn_out(0, 0)
            v.wait_ge(xv_in, 16)

            def body(t, k, last):
                if not last:
                    stage(t + 1, 1 - k)
                    turn_out(t + 1, 1 - k)
                v.wait_ge(down, t + 3)
                out_steps(v, t, psY[k][:, 0:D], outs)
                v.wait_ge(outs, t * nout + 3 * nout)
                v.bn_stats(at(m.st, t), at(result, t)).then_inc(stats, 1)
            tiles(v, body)


def make_qkv(nc, ctx, m, a):
    sem = lambda n: semaphore(nc, m, f"qkv_{n}")
    loaded, staged, turned, turn_read, prod, q_out, kv_out, scaled = (sem(n) for n in (
        "loaded", "staged", "turned", "turn_read", "product", "q_out", "kv_out", "scaled"))
    stored = [sem(f"stored{k}") for k in range(2)]
    W = m.WT[:, 0:C2 * 3 * D].rearrange("p (c f) -> p c f", c=C2)
    bq = m.WT[:, 1536:1536 + 3 * D]
    hs = m.SC[:, 4096:4096 + 512].rearrange("p (k d) -> p k d", k=2)
    ht = m.SC[:, 4608:4608 + 512].rearrange("p (k c n) -> p k c n", k=2, c=C2)
    qv = m.SC[:, 0:4 * D].rearrange("p (k j d) -> p k j d", k=2, j=2)
    qr = m.SC[:, 1024:1024 + 2 * D].rearrange("p (k d) -> p k d", k=2)
    psT = (m.ps[4], m.ps[6])
    chain = sem("vector")
    with nc.Block() as block:
        @block.sync
        def _(s):
            s.dma_start(W, a["L1_gnn_Wqkv"].rearrange("(c p) f -> p c f", p=P)).then_inc(loaded, 16)
            s.dma_start(bq, a["L1_gnn_bqkv"].partition_broadcast(P)).then_inc(loaded, 16)
            s.dma_start(m.VG[:, :], a["L1_gnn_ln_attn_g"].partition_broadcast(P)).then_inc(loaded, 16)
            s.dma_start(m.VB[:, :], a["L1_gnn_ln_attn_b"].partition_broadcast(P)).then_inc(loaded, 16)
            for k in range(2):
                s.sem_inc(stored[k], 32)

            def body(t, k, last):
                s.wait_ge(scaled, t + 1)
                s.dma_start(m.qt[bass.ds(t * P, P), :], qv[:, k, 0, :]).then_inc(stored[k], 16)
                s.wait_ge(kv_out, t * 2 + 2)
                s.dma_start(m.vt[bass.ds(t * P, P), :], qv[:, k, 1, :]).then_inc(stored[k], 16)
            tiles(s, body)
            s.wait_ge(stored[0], 32 * (NT // 2 + 2))
            s.wait_ge(stored[1], 32 * (NT // 2 + 1))

        @block.tensor
        def _(pe):
            pe.wait_ge(loaded, 64)
            pe.sem_inc(turned, 2)
            pe.sem_inc(prod, 2)

            def turn(t, k):
                pe.wait_ge(staged, t + 1)
                pe.wait_ge(turn_read, t + 1)
                for c in range(C2):
                    last = pe.transpose(psT[k][:, c * P:(c + 1) * P], hs[:, k, c * P:(c + 1) * P], m.ident[:, :])
                last.then_inc(turned, 1)

            turn(0, 0)

            def body(t, k, last):
                if not last:
                    turn(t + 1, 1 - k)
                pe.wait_ge(turn_read, t + 3)
                pe.wait_ge(q_out, t + 1)
                for n, (lo, hi) in enumerate(((0, 512), (512, 768))):
                    for c in range(C2):
                        mm = pe.matmul(m.ps[2 * k + n][:, 0:hi - lo], ht[:, k, c, :], W[:, c, lo:hi], start=(c == 0), stop=(c == 1))
                mm.then_inc(prod, 1)
            tiles(pe, body)

        @block.scalar
        def _(s):
            def body(t, k, last):
                s.wait_ge(q_out, t + 3)
                s.activation(qv[:, k, 0, :], qr[:, k, :], ACT.Copy, scale=float(D) ** -0.5).then_inc(scaled, 1)
            with s.Fori(0, (NT - 1) // 2) as i:
                for k in range(2):
                    s.wait_ge(stored[k], i * 32 + 32)
                    body(i * 2 + k, k, False)
            s.wait_ge(stored[0], 32 * (NT // 2 + 1))
            body(NT - 1, 0, True)

        @block.vector
        def _(v):
            v.wait_ge(loaded, 64)
            v.sem_inc(turn_read, 2)
            v.sem_inc(q_out, 2)

            def turn_out(t, k):
                v.wait_ge(turned, t + 3)
                v.wait_ge(prod, t + 1)
                v.tensor_copy(ht[:, k].rearrange("p c n -> p (c n)"), psT[k][:, 0:D]).then_inc(turn_read, 1)

            def stage(t, k):
                standardise(v, m, m.XV, t, hs[:, k, :], chain, staged)

            stage(0, 0)
            turn_out(0, 0)
            stage(1, 1)

            def body(t, k, last, i, more=True):
                if not last:
                    turn_out(t + 1, 1 - k)
                if more:
                    stage(t + 2, k)
                v.wait_ge(prod, t + 3)
                v.wait_ge(stored[k], i * 32 + 32)
                v.tensor_tensor(at(m.HB, t), m.ps[2 * k][:, D:2 * D], bq[:, D:2 * D], ALU.add).then_inc(kv_out, 1)
                v.tensor_tensor(qv[:, k, 1, :], m.ps[2 * k + 1][:, 0:D], bq[:, 2 * D:3 * D], ALU.add).then_inc(kv_out, 1)
                v.tensor_tensor(qr[:, k, :], m.ps[2 * k][:, 0:D], bq[:, 0:D], ALU.add).then_inc(q_out, 1)
            with v.Fori(0, (NT - 3) // 2) as i:
                for k in range(2):
                    body(i * 2 + k, k, False, i)
            body(NT - 3, 0, False, NT // 2 - 1)
            body(NT - 2, 1, False, NT // 2 - 1, more=False)
            body(NT - 1, 0, True, NT // 2, more=False)


def edge_scores(nc, ctx, m):
    sem = lambda n: semaphore(nc, m, f"es_{n}")
    idx_ready, onehot, turned, turn_out, keys, mult, reduced = (sem(n) for n in (
        "idx", "onehot", "turned", "turn_out", "keys", "multiplied", "reduced"))
    asked = sem("asked")
    landed = [sem(f"landed{k}") for k in range(BATCH)]
    g8 = m.G.rearrange("p (k d) -> p k d", k=BATCH)
    oh, ix = m.OH, m.IX
    oht = m.GS.rearrange("p k d -> p (k d)")[:, 0:2 * 4 * P].rearrange("p (u k e) -> p u k e", u=2, k=4)
    pr = m.WT[:, 0:8 * D].rearrange("p (u k d) -> p u k d", u=2, k=4)
    sc3 = m.SC.rearrange("p (s h) -> p s h", h=H)
    NU = STEPS // 4
    psT = [m.ps[4], m.ps[5]]
    with nc.Block() as block:
        @block.scalar
        def _(s):
            s.sem_inc(turn_out, 2)

            def evac(u, w):
                s.wait_ge(turned, u + 1)
                s.wait_ge(keys, u * 4 + 1)
                s.activation(oht[:, w].rearrange("p k e -> p (k e)"), psT[w][:, :], ACT.Copy).then_inc(turn_out, 1)

            s.activation(ix[:, 0, :], m.TSI[:, 0:BATCH], ACT.Copy).then_inc(idx_ready, 1)
            evac(0, 0)

            def body(b, q, last):
                if not last:
                    s.wait_ge(mult, b * BATCH + BATCH)
                    s.activation(ix[:, 1 - q, :], m.TSI[:, bass.ds(b * BATCH + BATCH, BATCH)], ACT.Copy).then_inc(idx_ready, 1)
                evac(b * 2 + 1, 1)
                if not last:
                    evac(b * 2 + 2, 0)
            batches(s, body)

        @block.gpsimd
        def _(g):
            def body(b, q, last):
                g.wait_ge(idx_ready, b + 1)
                for k in range(BATCH):
                    g.wait_ge(mult, b * BATCH + k + 1)
                    g.sem_inc(asked, 1)
                    g.indirect_dma_start(g8[:, k, :], None, m.qt, bass.IndirectOffsetOnAxis(ap=ix[:, q, k:k + 1], axis=0)).then_inc(landed[k], 16)
            batches(g, body)

        @block.tensor
        def _(pe):
            pe.sem_inc(keys, 8)

            def turn(u, w, q, half):
                pe.wait_ge(turn_out, u + 1)
                for k in range(4):
                    mm = pe.transpose(psT[w][:, k * P:(k + 1) * P], oh[:, q, 4 * half + k, :], m.ident[:, :])
                mm.then_inc(turned, 1)

            def unit(b, u, w):
                pe.wait_ge(turn_out, u + 3)
                for k, win in enumerate(windows(nc, m, mybir.EngineType.PE, u * 4, 4)):
                    st = u * 4 + k
                    pe.wait_ge(mult, st + 5)
                    pe.matmul(m.ps[k][:, 0:D], oht[:, w, k, :], at(m.HB, win), start=True, stop=True).then_inc(keys, 1)

            pe.wait_ge(onehot, 1)
            turn(0, 0, 0, 0)

            def body(b, q, last):
                turn(b * 2 + 1, 1, q, 1)
                unit(b, b * 2, 0)
                if not last:
                    pe.wait_ge(onehot, b + 2)
                    turn(b * 2 + 2, 0, 1 - q, 0)
                unit(b, b * 2 + 1, 1)
            batches(pe, body)

        @block.vector
        def _(v):
            v.sem_inc(mult, BATCH)
            one_hots(v, m, 0, 0, onehot)

            def body(b, q, last):
                if not last:
                    one_hots(v, m, b + 1, 1 - q, onehot)
                for k in range(BATCH):
                    st = b * BATCH + k
                    v.wait_ge(landed[k], b * 16 + 16)
                    v.wait_ge(keys, st + 9)
                    v.tensor_tensor(pr[:, k // 4, k % 4, :], m.ps[k % 4][:, 0:D], g8[:, k, :], ALU.mult).then_inc(mult, 1)
                    if k % 4 == 3:
                        v.wait_ge(mult, st + 9)
                        v.tensor_reduce(sc3[:, bass.ds(st - 3, 4), :].rearrange("p s h -> p (s h)"),
                                        pr[:, k // 4].rearrange("p k (h e) -> p (k h) e", h=H), AX, ALU.add).then_inc(reduced, 1)
            batches(v, body)


def edge_softmax(nc, ctx, m):
    sem = lambda n: semaphore(nc, m, f"sm_{n}")
    loaded, packed, turned, unturned, done, pe_done, expd, ready = (sem(n) for n in (
        "loaded", "packed", "turned", "unturned", "vector", "tensor", "exp", "ready"))
    L = CL + 8
    S, PEN, F, Bk = (m.R1[:, i * L:(i + 1) * L] for i in range(4))
    rel = F
    key = Bk
    stage = m.G.rearrange("p (k n) -> p k n", k=4)
    sc = m.SC.rearrange("p (c j h) -> p j h c", c=CH, j=CS)
    NG = CS // 4
    rowK = m.rows
    row = lambda i: rowK[0:1, i, :]
    cF, cB, cKf, cKl, cL, cR = (m.small[:, i:i + 1] for i in range(6))
    with nc.Block() as block:
        @block.sync
        def _(s):
            for h in range(H):
                s.dma_start(rel[h * CH:(h + 1) * CH, 0:CL], m.reld.rearrange("(c j) e -> c (j e)", c=CH)).then_inc(loaded, 16)
                s.dma_start(key[h * CH:(h + 1) * CH, 0:CL], m.keyd.rearrange("(c j) e -> c (j e)", c=CH)).then_inc(loaded, 16)

        @block.gpsimd
        def _(g):
            for i in range(NG):
                if i >= 2:
                    g.wait_ge(turned, i - 1)
                for k in range(4):
                    mm = g.tensor_copy(stage[:, i % 2, k * P:(k + 1) * P].rearrange("p (h c) -> p h c", h=H), sc[:, 4 * i + k])
                mm.then_inc(packed, 1)

        @block.tensor
        def _(pe):
            for i in range(NG):
                pe.wait_ge(packed, i + 1)
                if i >= 2:
                    pe.wait_ge(unturned, i - 1)
                for k in range(4):
                    mm = pe.transpose(m.ps[i % 2][:, k * P:(k + 1) * P], stage[:, i % 2, k * P:(k + 1) * P], m.ident[:, :])
                mm.then_inc(turned, 1)
            pe.wait_ge(ready, 1)
            for i, c in enumerate((cF, cB, cKf, cKl)):
                mm = pe.transpose(m.ps[4][0:1, i * P:(i + 1) * P], c, m.ident[:, :])
            mm.then_inc(pe_done, 1)
            pe.wait_ge(ready, 2)
            for i in range(2):
                mm = pe.matmul(m.ps[5][:, i:i + 1], row(8 + i), m.ones[0:1, 0:1], start=True, stop=True)
            mm.then_inc(pe_done, 1)
            for i in range(NG):
                pe.wait_ge(expd, i + 1)
                if i >= 2:
                    pe.wait_ge(unturned, NG + i - 1)
                for k in range(4):
                    mm = pe.transpose(m.ps[i % 2][:, k * P:(k + 1) * P], S[:, (4 * i + k) * P:(4 * i + k + 1) * P], m.ident[:, :])
                mm.then_inc(turned, 1)

        @block.scalar
        def _(s):
            for i in range(NG):
                s.wait_ge(turned, i + 1)
                s.activation(S[:, i * 512:(i + 1) * 512], m.ps[i % 2][:, :], ACT.Copy).then_inc(unturned, 1)
            s.wait_ge(ready, 3)
            for i in range(NG):
                s.activation(S[:, i * 512:(i + 1) * 512], S[:, i * 512:(i + 1) * 512], ACT.Exp).then_inc(expd, 1)

        @block.vector
        def _(v):
            c = [0]

            def step(ins, wait=True):
                c[0] += 1
                ins.then_inc(done, 1)
                if wait:
                    v.wait_ge(done, c[0])
            v.wait_ge(loaded, 16 * 2 * H)
            SS, FF, BB = S[:, 0:CL], F[:, 0:CL], Bk[:, 0:CL]
            p0, p1 = PEN[:, 0:CL], PEN[:, 1:CL + 1]
            step(v.tensor_scalar(PEN[:, 0:CL], rel[:, 0:CL], 0.0, None, ALU.is_ge))
            step(v.scalar_tensor_tensor(rel[:, 0:CL], rel[:, 0:CL], float(P) - 0.5, PEN[:, 0:CL], ALU.is_lt, ALU.mult))
            v.wait_ge(unturned, NG)
            step(v.tensor_tensor(SS, SS, FF, ALU.mult))
            step(v.tensor_scalar(FF, FF, 1.0, BIG, ALU.subtract, ALU.mult))
            step(v.tensor_tensor(SS, SS, FF, ALU.add), wait=False)
            step(v.tensor_tensor(PEN[:, 1:CL], key[:, 1:CL], key[:, 0:CL - 1], ALU.is_equal))
            step(v.tensor_scalar(PEN[:, 1:CL], PEN[:, 1:CL], 1.0, BIG, ALU.subtract, ALU.mult), wait=False)
            step(v.memset(PEN[:, 0:1], 0.0), wait=False)
            step(v.memset(PEN[:, CL:CL + 1], 0.0), wait=False)
            step(v.tensor_copy(cKf, key[:, 0:1]), wait=False)
            step(v.tensor_copy(cKl, key[:, CL - 1:CL]))
            step(v.tensor_tensor_scan(FF, p0, SS, -BIG, ALU.add, ALU.max))
            step(v.tensor_tensor_scan(BB[:, ::-1], p1[:, ::-1], FF[:, ::-1], -BIG, ALU.add, ALU.max))
            step(v.tensor_copy(cF, F[:, CL - 1:CL]), wait=False)
            step(v.tensor_copy(cB, Bk[:, 0:1]))
            v.sem_inc(ready, 1)
            v.wait_ge(pe_done, 1)
            step(v.tensor_copy(rowK[0:1, 0:4, :].rearrange("p a b -> p (a b)"), m.ps[4][0:1, :]))
            rF, rB, rKf, rKl, pv, ps_, pn, t1, rL, rR, oL, oR, t2 = (row(i) for i in range(13))
            step(v.memset(pv, 0.0))
            step(v.tensor_tensor(pv[:, 1:P], rKf[:, 1:P], rKl[:, 0:P - 1], ALU.is_equal))
            step(v.memset(pv.rearrange("p (h c) -> p h c", h=H)[:, :, 0:1], 0.0))
            step(v.tensor_scalar(pv, pv, 1.0, BIG, ALU.subtract, ALU.mult))
            step(v.tensor_tensor(ps_, rKf, rKl, ALU.is_equal))
            step(v.tensor_scalar(ps_, ps_, 1.0, BIG, ALU.subtract, ALU.mult))
            step(v.tensor_tensor(t1, pv, ps_, ALU.add))
            step(v.tensor_tensor_scan(oL, t1, rF, -BIG, ALU.add, ALU.max))
            step(v.memset(rL, -BIG))
            step(v.tensor_tensor(rL[:, 1:P], oL[:, 0:P - 1], pv[:, 1:P], ALU.add))
            step(v.memset(pn, -BIG))
            step(v.tensor_copy(pn[:, 0:P - 1], pv[:, 1:P]))
            step(v.tensor_tensor(t2, pn, ps_, ALU.add))
            step(v.tensor_tensor_scan(oR[:, ::-1], t2[:, ::-1], rB[:, ::-1], -BIG, ALU.add, ALU.max))
            step(v.memset(rR, -BIG))
            step(v.tensor_tensor(rR[:, 0:P - 1], oR[:, 1:P], pn[:, 0:P - 1], ALU.add))
            v.sem_inc(ready, 1)
            v.wait_ge(pe_done, 2)
            step(v.tensor_copy(m.small[:, 4:6], m.ps[5][:, 0:2]))
            step(v.tensor_tensor_scan(FF, p0, SS, cL, ALU.add, ALU.max))
            step(v.tensor_tensor_scan(BB[:, ::-1], p1[:, ::-1], FF[:, ::-1], cR, ALU.add, ALU.max))
            step(v.tensor_tensor(SS, SS, BB, ALU.subtract))
            v.sem_inc(ready, 1)
            for i in range(NG):
                v.wait_ge(turned, NG + i + 1)
                for k in range(4):
                    mm = v.tensor_copy(sc[:, 4 * i + k], m.ps[i % 2][:, k * P:(k + 1) * P].rearrange("p (h c) -> p h c", h=H))
                mm.then_inc(unturned, 1)


def edge_values(nc, ctx, m):
    sem = lambda n: semaphore(nc, m, f"ev_{n}")
    idx_ready, weighted, pcols, onehot, summed, added, cleared, asked = (sem(n) for n in (
        "idx", "weighted", "pcols", "onehot", "summed", "added", "cleared", "asked"))
    landed = [sem(f"landed{k}") for k in range(BATCH)]
    U = BATCH // 2
    g8 = m.G.rearrange("p (k d) -> p k d", k=BATCH)
    sc3 = m.SC.rearrange("p (s h) -> p s h", h=H)
    gs, oh, ix = m.GS, m.OH, m.IX
    x2_in = sem("x2_in")
    with nc.Block() as block:
        @block.sync
        def _(s):
            s.dma_start(m.HB, m.x2.rearrange("(t p) d -> p t d", p=P)).then_inc(x2_in, 16)
            s.wait_ge(x2_in, 16)

        @block.scalar
        def _(s):
            s.activation(ix[:, 0, :], m.TSI[:, 0:BATCH], ACT.Copy).then_inc(idx_ready, 1)

            def body(b, q, last):
                if not last:
                    s.wait_ge(weighted, b * BATCH + BATCH)
                    s.activation(ix[:, 1 - q, :], m.TSI[:, bass.ds(b * BATCH + BATCH, BATCH)], ACT.Copy).then_inc(idx_ready, 1)
                for w in range(2):
                    s.wait_ge(summed, b * BATCH + w * U + U)
                    s.activation(gs[:, w * U:w * U + U, D:AW], sc3[:, bass.ds(b * BATCH + w * U, U), :], ACT.Copy).then_inc(pcols, 1)
            batches(s, body)

        @block.gpsimd
        def _(g):
            def body(b, q, last):
                g.wait_ge(idx_ready, b + 1)
                for k in range(BATCH):
                    g.wait_ge(weighted, b * BATCH + k + 1)
                    g.sem_inc(asked, 1)
                    g.indirect_dma_start(g8[:, k, :], None, m.vt, bass.IndirectOffsetOnAxis(ap=ix[:, q, k:k + 1], axis=0)).then_inc(landed[k], 16)
            batches(g, body)

        @block.vector
        def _(v):
            v.sem_inc(added, BATCH)
            v.sem_inc(weighted, BATCH)
            v.memset(m.AGG3, 0.0).then_inc(cleared, 1)
            v.wait_ge(cleared, 1)
            one_hots(v, m, 0, 0, onehot)

            def weigh(b, k):
                v.wait_ge(landed[k], b * 16 + 16)
                v.wait_ge(summed, b * BATCH + k + 1)
                v.tensor_tensor(gs[:, k, 0:D].rearrange("p (h e) -> p h e", h=H), g8[:, k, :].rearrange("p (h e) -> p h e", h=H),
                                sc3[:, bass.ds(b * BATCH + k, 1), :].rearrange("p s h -> p (s h)").unsqueeze(2).broadcast_to([P, H, DH]),
                                ALU.mult).then_inc(weighted, 1)

            for k in range(U):
                weigh(0, k)

            def body(b, q, last):
                if not last:
                    one_hots(v, m, b + 1, 1 - q, onehot)
                win = windows(nc, m, mybir.EngineType.DVE, b * BATCH, BATCH)
                for w in range(2):
                    for k in range(w * U, w * U + U):
                        if w == 0:
                            weigh(b, k + U)
                        elif not last:
                            weigh(b + 1, k - U)
                        add_window(v, m, b, k, win[k], summed, added, AW)
            batches(v, body)

        @block.tensor
        def _(pe):
            pe.sem_inc(summed, BATCH)

            def body(b, q, last):
                pe.wait_ge(onehot, b + 1)
                for w in range(2):
                    pe.wait_ge(pcols, b * 2 + w + 1)
                    for k in range(w * U, w * U + U):
                        pe.wait_ge(weighted, b * BATCH + k + 1 + BATCH)
                        pe.wait_ge(added, b * BATCH + k + 1)
                        pe.matmul(m.ps[k][:, 0:AW], oh[:, q, k, :], gs[:, k, :], start=True, stop=True).then_inc(summed, 1)
            batches(pe, body)


def slice_weights(nc, ctx, m, a):
    sem = lambda n: semaphore(nc, m, f"sw_{n}")
    loaded, zeroed, turned, out_, prod, done = (sem(n) for n in ("loaded", "zeroed", "turned", "read", "product", "vector"))
    s_ = m.TS
    with nc.Block() as block:
        @block.sync
        def _(s):
            s.dma_start(s_.wf, a["L1_ffn_W_fx"].rearrange("(c p) f -> p c f", p=P)).then_inc(loaded, 16)
            s.dma_start(s_.wx, a["L1_ffn_W_x"].rearrange("(c p) f -> p c f", p=P)).then_inc(loaded, 16)
            s.dma_start(s_.wo, a["L1_ffn_W_out"].rearrange("(c p) f -> p c f", p=P)).then_inc(loaded, 16)
            s.dma_start(s_.bfx, a["L1_ffn_b_fx"].partition_broadcast(P)).then_inc(loaded, 16)
            s.dma_start(m.VB[:, :], a["L1_ffn_b_out"].partition_broadcast(P)).then_inc(loaded, 16)
            s.dma_start(s_.bx, a["L1_ffn_b_x"].rearrange("(c p) -> p c", p=P)).then_inc(loaded, 16)
            s.dma_start(s_.bs, a["L1_ffn_b_slice"].partition_broadcast(P)).then_inc(loaded, 16)
            s.dma_start(s_.rt, a["L1_ffn_temperature"].rearrange("a h b c -> (a h b c)").partition_broadcast(P)).then_inc(loaded, 16)
            s.wait_ge(zeroed, 6)
            for dst, n in ((s_.ws, "W_slice"), (s_.wq, "W_q"), (s_.wk, "W_k"), (s_.wv, "W_v")):
                for i in range(2):
                    s.dma_start(dst[i * 64:(i + 1) * 64, i * 64:(i + 1) * 64], a["L1_ffn_" + n]).then_inc(loaded, 16)
            s.wait_ge(loaded, 16 * 16)

        @block.vector
        def _(v):
            c = [0]

            def step(ins):
                c[0] += 1
                ins.then_inc(done, 1)
                v.wait_ge(done, c[0])
            for x in (s_.ws, s_.wq, s_.wk, s_.wv, s_.tkb.rearrange("p a b -> p (a b)"), s_.atb.rearrange("p a b -> p (a b)")):
                v.memset(x, 0.0).then_inc(zeroed, 1)
            v.memset(s_.zero, 0.0)
            v.wait_ge(loaded, 16 * 16)
            step(v.tensor_scalar(s_.rt, s_.rt, 0.1, 5.0, ALU.max, ALU.min))
            step(v.reciprocal(s_.rt, s_.rt))
            for j in range(4):
                v.wait_ge(turned, j + 1)
                step(v.tensor_copy(s_.wxt[:, j], m.ps[j][:, 0:C2 * P].rearrange("p (c i) -> p c i", c=C2)))
            v.wait_ge(prod, 1)
            rt3 = s_.rt.unsqueeze(2).broadcast_to([P, H, G])
            for cc in range(C2):
                step(v.tensor_tensor(s_.wl[:, cc].rearrange("p (h g) -> p h g", h=H), m.ps[4 + cc][:, :].rearrange("p (h g) -> p h g", h=H), rt3, ALU.mult))
            bl3 = s_.bl.rearrange("p (h g) -> p h g", h=H)
            step(v.tensor_tensor(bl3, m.ps[6][:, :].rearrange("p (h g) -> p h g", h=H), s_.bs.unsqueeze(1).broadcast_to([P, H, G]), ALU.add))
            step(v.tensor_tensor(bl3, bl3, rt3, ALU.mult))

        @block.scalar
        def _(s):
            s.wait_ge(loaded, 16 * 16)
            for j in range(4):
                s.activation(s_.bxb[:, j, :], m.ones[:, :], ACT.Copy, scale=s_.bx[:, j:j + 1]).then_inc(out_, 1)

        @block.tensor
        def _(pe):
            pe.wait_ge(loaded, 16 * 16)
            for j in range(4):
                for c in range(C2):
                    mm = pe.transpose(m.ps[j][:, c * P:(c + 1) * P], s_.wx[:, c, j * P:(j + 1) * P], m.ident[:, :])
                mm.then_inc(turned, 1)
            pe.wait_ge(done, 6)
            pe.wait_ge(out_, 4)
            for j in range(4):
                for c in range(C2):
                    pe.matmul(m.ps[4 + c][:, j * P:(j + 1) * P], s_.wxt[:, j, c, :], s_.ws, start=True, stop=True)
                mm = pe.matmul(m.ps[6][:, j * P:(j + 1) * P], s_.bxb[:, j, :], s_.ws, start=True, stop=True)
            mm.then_inc(prod, 1)


def slice_pass(nc, ctx, m):
    sem = lambda n: semaphore(nc, m, f"sp_{n}")
    staged, turned, turn_read, prod, fx_out, mx_out, exp_out, w_out, tok, chain, init = (sem(n) for n in (
        "staged", "turned", "turn_read", "product", "fx_out", "shifted", "exp", "weights", "tokens", "vector", "init"))
    s_ = m.TS
    psT = (m.ps[4], m.ps[7])
    W3 = m.R1[:, 0:NT * INNER].rearrange("p (t n) -> p t n", t=NT)
    kept, shifting = sem("kept"), sem("shifting")
    with nc.Block() as block:
        @block.gpsimd
        def _(g):
            def body(t, k, last):
                g.wait_ge(w_out, t + 3)
                g.tensor_copy(at(W3, t), s_.wst[:, k, :]).then_inc(kept, 1)
            g.sem_inc(kept, 2)
            tiles(g, body)

        @block.tensor
        def _(pe):
            pe.sem_inc(turned, 2)
            pe.sem_inc(prod, 2)
            pe.sem_inc(tok, 2)
            pe.wait_ge(init, 2)
            fx2 = s_.fx[:, 0].rearrange("p j n -> p (j n)")
            token_bank = lambda j: m.ps[5 + j // 2][:, (j % 2) * (P + 1):(j % 2 + 1) * (P + 1)]

            def turn(t, k):
                pe.wait_ge(staged, t + 1)
                pe.wait_ge(turn_read, t + 1)
                for c in range(C2):
                    last = pe.transpose(psT[k][:, c * P:(c + 1) * P], s_.hs[:, k, c * P:(c + 1) * P], m.ident[:, :])
                last.then_inc(turned, 1)

            def project(t, k):
                pe.wait_ge(turn_read, t + 3)
                pe.wait_ge(mx_out, t + 1)
                pe.wait_ge(fx_out, t + 1)
                for n, w in enumerate((s_.wf, s_.wl)):
                    for c in range(C2):
                        mm = pe.matmul(m.ps[2 * k + n][:, :], s_.ht[:, k, c, :], w[:, c, :], start=(c == 0), stop=(c == 1))
                mm.then_inc(prod, 1)

            for i in range(2):
                pe.matmul(m.ps[5 + i][:, 0:2 * (P + 1)], s_.zero, fx2[:, 0:2 * (P + 1)], start=True, stop=False, skip_group_check=True)
            turn(0, 0)
            project(0, 0)
            turn(1, 1)
            project(1, 1)
            turn(2, 0)

            def body(t, k, ahead):
                if ahead >= 3:
                    turn(t + 3, 1 - k)
                if ahead >= 2:
                    project(t + 2, k)
                pe.wait_ge(w_out, t + 3)
                pe.wait_ge(fx_out, t + 3)
                for j in range(4):
                    mm = pe.matmul(token_bank(j), s_.wst[:, k, j * P:(j + 1) * P], s_.fx[:, k, j, :],
                                   start=False, stop=False, skip_group_check=True)
                mm.then_inc(tok, 1)
            tiles_ahead(pe, body)
            for i in range(2):
                mm = pe.matmul(m.ps[5 + i][:, 0:2 * (P + 1)], s_.zero, fx2[:, 0:2 * (P + 1)], start=False, stop=True, skip_group_check=True)
            mm.then_inc(tok, 1)

        @block.scalar
        def _(s):
            def body(t, k, last):
                s.wait_ge(prod, t + 3)
                s.wait_ge(tok, t + 1)
                s.activation(s_.fx[:, k, :, 0:P], m.ps[2 * k][:, :].rearrange("p (j n) -> p j n", j=4), ACT.Copy).then_inc(fx_out, 1)
                s.wait_ge(mx_out, t + 3)
                s.activation(s_.lg[:, k, :], s_.lg[:, k, :], ACT.Exp).then_inc(exp_out, 1)
            tiles(s, body)

        @block.vector
        def _(v):
            v.sem_inc(turn_read, 2)
            v.sem_inc(mx_out, 2)
            v.sem_inc(fx_out, 2)
            v.sem_inc(w_out, 2)
            for k in range(2):
                v.memset(s_.fx[:, k].rearrange("p j n -> p (j n)"), 1.0).then_inc(init, 1)

            def turn_out(t, k):
                v.wait_ge(turned, t + 3)
                v.wait_ge(prod, t + 1)
                v.tensor_copy(s_.ht[:, k].rearrange("p c n -> p (c n)"), psT[k][:, 0:D]).then_inc(turn_read, 1)

            def stage(t, k):
                standardise(v, m, m.HB, t, s_.hs[:, k, :], None, staged, affine=False)

            lg3 = lambda k: s_.lg[:, k, :].rearrange("p (h g) -> p h g", h=H)

            def shift(t, k):
                v.wait_ge(w_out, t + 1)
                v.wait_ge(prod, t + 3)
                v.tensor_tensor(s_.lg[:, k, :], m.ps[2 * k + 1][:, :], s_.bl, ALU.add).then_inc(shifting, 1)
                v.wait_ge(shifting, t * 2 + 1)
                v.wait_ge(mx_out, t + 2)
                v.tensor_reduce(s_.mx, lg3(k), AX, ALU.max).then_inc(shifting, 1)
                v.wait_ge(shifting, t * 2 + 2)
                v.tensor_tensor(lg3(k), lg3(k), s_.mx.unsqueeze(2).broadcast_to([P, H, G]), ALU.subtract).then_inc(mx_out, 1)

            def weights(t, k):
                v.wait_ge(w_out, t + 2)
                v.wait_ge(exp_out, t + 1)
                v.tensor_reduce(s_.sm, lg3(k), AX, ALU.add).then_inc(chain, 1)
                v.wait_ge(chain, t * 3 + 1)
                v.reciprocal(s_.sm, s_.sm).then_inc(chain, 1)
                v.wait_ge(chain, t * 3 + 2)
                v.tensor_scalar(s_.sm, s_.sm, col(m.valid, t), None, ALU.mult).then_inc(chain, 1)
                v.wait_ge(chain, t * 3 + 3)
                v.wait_ge(tok, t + 1)
                v.wait_ge(kept, t + 1)
                v.tensor_tensor(s_.wst[:, k, :].rearrange("p (h g) -> p h g", h=H), lg3(k),
                                s_.sm.unsqueeze(2).broadcast_to([P, H, G]), ALU.mult).then_inc(w_out, 1)

            stage(0, 0)
            stage(1, 1)
            turn_out(0, 0)
            stage(2, 0)
            turn_out(1, 1)
            stage(3, 1)
            shift(0, 0)
            turn_out(2, 0)

            def body(t, k, ahead):
                if ahead >= 1:
                    shift(t + 1, 1 - k)
                if ahead >= 4:
                    stage(t + 4, k)
                if ahead >= 3:
                    turn_out(t + 3, 1 - k)
                weights(t, k)
            tiles_ahead(v, body)
            v.wait_ge(tok, NT + 3)
            a4 = s_.acc.rearrange("p (i n) -> p i n", i=2)
            for i in range(2):
                v.tensor_copy(a4[:, i], m.ps[5 + i][:, 0:2 * (P + 1)]).then_inc(init, 1)
            v.wait_ge(init, 4)
            a3 = s_.acc.rearrange("p (j n) -> p j n", j=4)
            for j in range(4):
                v.scalar_tensor_tensor(a3[:, j, 0:P], s_.bfx[:, j * P:(j + 1) * P], a3[:, j, P:P + 1], a3[:, j, 0:P], ALU.mult, ALU.add)


def slice_tokens(nc, ctx, m):
    sem = lambda n: semaphore(nc, m, f"st_{n}")
    done, pe_done, exp_out, at_ready = (sem(n) for n in ("vector", "tensor", "exp", "rows"))
    s_ = m.TS
    a3 = s_.acc.rearrange("p (j n) -> p j n", j=4)
    scale = float(DS) ** -0.5
    halves = ((slice(0, 64), slice(0, 64)), (slice(64, 128), slice(64, 128)))
    with nc.Block() as block:
        @block.vector
        def _(v):
            c = [0]

            def step(ins):
                c[0] += 1
                ins.then_inc(done, 1)
                v.wait_ge(done, c[0])
            step(v.tensor_scalar(s_.nr, a3[:, :, P:P + 1].rearrange("p j n -> p (j n)"), 1e-5, None, ALU.add))
            step(v.reciprocal(s_.nr, s_.nr))
            for rows, cols in halves:
                step(v.tensor_tensor(s_.tkb[rows, :, cols], a3[rows, :, cols], s_.nr[rows, :].unsqueeze(2).broadcast_to([64, 4, 64]), ALU.mult))
            assert c[0] == 4
            v.wait_ge(pe_done, 1)
            step(v.tensor_copy(s_.t1.rearrange("p j n -> p (j n)"), m.ps[0][:, :]))
            v.wait_ge(pe_done, 2)
            step(v.tensor_copy(s_.qT.rearrange("p j n -> p (j n)"), m.ps[1][:, :]))
            step(v.tensor_copy(s_.kT.rearrange("p j n -> p (j n)"), m.ps[2][:, :]))
            step(v.tensor_copy(s_.vv.rearrange("p j n -> p (j n)"), m.ps[3][:, :]))
            v.wait_ge(pe_done, 3)
            p3 = m.ps[4][:, :].rearrange("p (j n) -> p j n", j=4)
            for rows, cols in halves:
                step(v.tensor_copy(s_.att[rows], p3[rows, :, cols]))
            step(v.tensor_reduce(s_.am, s_.att, AX, ALU.max))
            step(v.tensor_tensor(s_.att, s_.att, s_.am.unsqueeze(2).broadcast_to([P, 4, 64]), ALU.subtract))
            v.wait_ge(exp_out, 1)
            step(v.tensor_reduce(s_.am, s_.att, AX, ALU.add))
            step(v.reciprocal(s_.am, s_.am))
            for rows, cols in halves:
                step(v.tensor_tensor(s_.atb[rows, :, cols], s_.att[rows], s_.am[rows, :].unsqueeze(2).broadcast_to([64, 4, 64]), ALU.mult))
            assert c[0] == 16
            v.wait_ge(pe_done, 4)
            step(v.tensor_copy(s_.t1.rearrange("p j n -> p (j n)"), m.ps[5][:, :]))
            v.wait_ge(pe_done, 5)
            step(v.tensor_copy(s_.qT.rearrange("p j n -> p (j n)"), m.ps[6][:, :]))
            v.wait_ge(pe_done, 6)
            for i in range(2):
                step(v.tensor_copy(s_.mo[:, 2 * i:2 * i + 2, :].rearrange("p j n -> p (j n)"), m.ps[i][:, :]))

        @block.scalar
        def _(s):
            s.wait_ge(done, 12)
            s.activation(s_.att, s_.att, ACT.Exp, scale=scale).then_inc(exp_out, 1)

        @block.tensor
        def _(pe):
            J = lambda ap, j: ap[:, j * P:(j + 1) * P]
            pe.wait_ge(done, 4)
            for j in range(4):
                mm = pe.transpose(J(m.ps[0], j), s_.tkb[:, j, :], m.ident[:, :])
            mm.then_inc(pe_done, 1)
            pe.wait_ge(done, 5)
            for j in range(4):
                pe.matmul(J(m.ps[1], j), s_.wq, s_.t1[:, j, :], start=True, stop=True)
                pe.matmul(J(m.ps[2], j), s_.wk, s_.t1[:, j, :], start=True, stop=True)
                mm = pe.matmul(J(m.ps[3], j), s_.t1[:, j, :], s_.wv, start=True, stop=True)
            mm.then_inc(pe_done, 1)
            pe.wait_ge(done, 8)
            for j in range(4):
                mm = pe.matmul(J(m.ps[4], j), s_.qT[:, j, :], s_.kT[:, j, :], start=True, stop=True)
            mm.then_inc(pe_done, 1)
            pe.wait_ge(done, 16)
            for j in range(4):
                mm = pe.transpose(J(m.ps[5], j), s_.atb[:, j, :], m.ident[:, :])
            mm.then_inc(pe_done, 1)
            pe.wait_ge(done, 17)
            for j in range(4):
                mm = pe.matmul(J(m.ps[6], j), s_.vv[:, j, :], s_.t1[:, j, :], start=True, stop=True)
            mm.then_inc(pe_done, 1)
            pe.wait_ge(done, 18)
            for j in range(4):
                mm = pe.matmul(m.ps[j // 2][:, (j % 2) * D:(j % 2 + 1) * D], s_.qT[:, j, :], s_.wo[:, j, :], start=True, stop=True)
            mm.then_inc(pe_done, 1)


def slice_output(nc, ctx, m, out):
    sem = lambda n: semaphore(nc, m, f"so_{n}")
    staged, turned, turn_read, prod, summed = (sem(n) for n in ("staged", "turned", "turn_read", "product", "summed"))
    loaded = [sem(f"loaded{k}") for k in range(2)]
    stored = [sem(f"stored{k}") for k in range(2)]
    chain = sem("bias")
    s_ = m.TS
    W3 = m.R1[:, 0:NT * INNER].rearrange("p (t n) -> p t n", t=NT)
    x3, ot = s_.hs, s_.ot
    with nc.Block() as block:
        @block.sync
        def _(s):
            for k in range(2):
                s.sem_inc(stored[k], 16)

            def load(t, k):
                s.dma_start(x3[:, k, :], m.x3[bass.ds(t * P, P), :]).then_inc(loaded[k], 16)

            def store(t, k):
                s.wait_ge(summed, t + 1)
                s.dma_start(out[bass.ds(t * P, P), :], ot[:, k, :]).then_inc(stored[k], 16)
            load(0, 0)
            load(1, 1)
            with s.Fori(0, (NT - 3) // 2) as i:
                for k in range(2):
                    store(i * 2 + k, k)
                    load(i * 2 + k + 2, k)
            store(NT - 3, 0)
            load(NT - 1, 0)
            store(NT - 2, 1)
            s.wait_ge(summed, NT)
            s.dma_start(out[(NT - 1) * P:N, :], ot[0:LAST, 0, :]).then_inc(stored[0], 16)
            s.wait_ge(stored[0], 16 * (NT // 2 + 2))
            s.wait_ge(stored[1], 16 * (NT // 2 + 1))

        @block.gpsimd
        def _(g):
            def body(t, k, last):
                g.wait_ge(turned, t + 1)
                g.tensor_copy(s_.wst[:, k, :], at(W3, t)).then_inc(staged, 1)
            tiles(g, body)

        @block.tensor
        def _(pe):
            pe.sem_inc(turned, 2)
            pe.sem_inc(prod, 2)

            def turn(t, k):
                pe.wait_ge(staged, t + 1)
                pe.wait_ge(turn_read, t + 1)
                for j in range(4):
                    mm = pe.transpose(m.ps[k][:, j * P:(j + 1) * P], s_.wst[:, k, j * P:(j + 1) * P], m.ident[:, :])
                mm.then_inc(turned, 1)
            turn(0, 0)

            def body(t, k, last):
                if not last:
                    turn(t + 1, 1 - k)
                pe.wait_ge(turn_read, t + 3)
                pe.wait_ge(chain, t + 1)
                for j in range(4):
                    mm = pe.matmul(m.ps[2 + k][:, 0:D], s_.wtt[:, k, j * P:(j + 1) * P], s_.mo[:, j, :], start=(j == 0), stop=(j == 3))
                mm.then_inc(prod, 1)
            tiles(pe, body)

        @block.scalar
        def _(s):
            s.sem_inc(turn_read, 2)

            def body(t, k, last):
                s.wait_ge(turned, t + 3)
                s.wait_ge(prod, t + 1)
                s.activation(s_.wtt[:, k, :], m.ps[k][:, :], ACT.Copy).then_inc(turn_read, 1)
            tiles(s, body)

        @block.vector
        def _(v):
            v.sem_inc(chain, 2)

            def body(t, k, i):
                v.wait_ge(prod, t + 3)
                v.wait_ge(stored[k], i * 16 + 16)
                v.tensor_tensor(ot[:, k, :], m.ps[2 + k][:, 0:D], m.VB[:, :], ALU.add).then_inc(chain, 1)
                v.wait_ge(chain, t + 3)
                v.wait_ge(loaded[k], i * 16 + 16)
                v.tensor_tensor(ot[:, k, :], ot[:, k, :], x3[:, k, :], ALU.add).then_inc(summed, 1)
            with v.Fori(0, (NT - 1) // 2) as i:
                for k in range(2):
                    body(i * 2 + k, k, i)
            body(NT - 1, 0, NT // 2)


def gnn_program(nc, a, out):
    with ExitStack() as ctx:
        ctx.enter_context(nc.allow_non_contiguous_dma(reason="small vectors and tables"))
        sb = lambda n, s, d=F32: ctx.enter_context(nc.sbuf_tensor(n, s, d))
        dr = lambda n, s, d=F32: nc.dram_tensor(n, s, d).ap()
        m = Mem()
        m.semaphores = []
        m.ps = [ctx.enter_context(nc.psum_tensor(f"bank{i}", [P, 512], F32)) for i in range(8)]
        big = NT * AW + NT * D + C2 * R * D
        m.R1 = sb("R1", [P, big])[:, :]
        m.AGG = m.R1[:, 0:NT * AW]
        m.AGG3 = m.AGG.rearrange("p (t d) -> p t d", t=NT)
        m.XV = m.R1[:, 0:NT * D].rearrange("p (t d) -> p t d", t=NT)
        m.HB = m.R1[:, NT * AW:NT * AW + NT * D].rearrange("p (t d) -> p t d", t=NT)
        m.WT = m.R1[:, NT * (AW + D):big]
        m.SC = sb("SC", [P, STEPS * H])[:, :]
        m.TDR, m.TCI, m.TSI, m.TEA = (sb(n, [P, STEPS])[:, :] for n in ("TDR", "TCI", "TSI", "TEA"))
        m.G = sb("G", [P, BATCH * D])[:, :]
        m.GS = sb("GS", [P, BATCH, AW])[:, :, :]
        m.OH = sb("OH", [P, 2, BATCH, P])[:, :, :, :]
        m.IX = sb("IX", [P, 2, BATCH], I32)[:, :, :]
        m.win = sb("win", [1, STEPS], I32)
        m.unsorted = sb("unsorted", [1, 1], I32)
        m.ident, m.iota, m.ones, m.upper = (sb(n, [P, P]) for n in ("ident", "iota", "ones", "upper"))
        m.valid = sb("valid", [P, NT])
        m.ab = sb("ab", [P, 2, ERJ])
        m.abi = sb("abi", [P, 2, ERJ], I32)
        m.small = sb("small", [P, 40])[:, :]
        m.smalli = sb("smalli", [P, 16], I32)[:, :]
        m.VG, m.VB = sb("VG", [P, D]), sb("VB", [P, D])
        m.ROOT = m.SC[:, 5120:5120 + C2 * D].rearrange("p (c o) -> p c o", c=C2)
        m.ATT = sb("ATT", [P, R * B])
        m.st = sb("st", [P, NT, 6])[:, :, :]
        m.mean, m.var, m.rstd, m.tmp = (sb(n, [P, NT])[:, :] for n in ("mean", "var", "rstd", "tmp"))
        m.mean4, m.rstd4 = (sb(n, [P, NT])[:, :] for n in ("mean4", "rstd4"))
        m.MW = sb("MW", [P, NT])[:, :]
        m.BO = m.G[:, 0:D]
        m.SEL = m.G[:, 0:4 * NT]
        m.SC2 = m.AGG[:, 0:NP]
        m.rc = m.rstd
        m.rows = m.OH.rearrange("p a b c -> p (a b) c")
        m.hrel = dr("hrel", (NP, R * D))
        m.edg = dr("edg", (ETILES, 4 * P))
        m.abd = dr("abd", (2, ETILES))
        m.dsts = dr("dsts", (ETILES * P,))
        m.srec = dr("srec", (ETILES * P, 4))
        m.keyd, m.reld = dr("keyd", (STEPS, P)), dr("reld", (STEPS, P))
        m.wind = dr("wind", (STEPS,), I32)
        m.wd = dr("wd", (NP,))
        m.xs, m.x1, m.x2 = (dr(n, (NP, D)) for n in ("x0", "x1", "x2"))
        m.x3 = dr("x3", (NP, D))
        m.qt, m.vt = dr("qt", (NP, D)), dr("vt", (NP, D))
        s_ = m.TS = Mem()
        o = [0]

        def part(base, shape):
            n = 1
            for x in shape:
                n *= x
            ap = base[:, o[0]:o[0] + n]
            o[0] += n
            if len(shape) == 2:
                ap = ap.rearrange("p (a b) -> p a b", a=shape[0])
            if len(shape) == 3:
                ap = ap.rearrange("p (a b c) -> p a b c", a=shape[0], b=shape[1])
            return ap
        s_.wf, s_.wx, s_.wl = (part(m.WT, (C2, INNER)) for _ in range(3))
        s_.wo = part(m.WT, (4, D))
        s_.wxt = part(m.WT, (4, C2, P))
        s_.ws, s_.wq, s_.wk, s_.wv = (part(m.WT, (P,)) for _ in range(4))
        s_.bxb = part(m.WT, (4, P))
        s_.bfx, s_.bl = part(m.WT, (INNER,)), part(m.WT, (INNER,))
        s_.bx, s_.bs, s_.rt, s_.nr, s_.am, s_.mx, s_.sm = (part(m.WT, (n,)) for n in (4, G, H, 4, 4, H, H))
        assert o[0] <= C2 * R * D
        o[0] = 0
        s_.hs = part(m.SC, (2, D))
        s_.ot = part(m.SC, (2, D))
        s_.ht = part(m.SC, (2, C2, P))
        s_.lg = part(m.SC, (2, INNER))
        s_.wst = part(m.SC, (2, INNER))
        s_.fx = part(m.SC, (2, 4, P + 1))
        s_.acc = part(m.SC, (4 * (P + 1),))
        s_.att = part(m.SC, (4, 64))
        s_.zero = part(m.SC, (P,))
        assert o[0] <= STEPS * H
        o[0] = 0
        s_.tkb, s_.atb, s_.t1, s_.qT = (part(m.G, (4, P)) for _ in range(4))
        o[0] = 0
        oh = m.OH.rearrange("p a b c -> p (a b c)")
        s_.kT, s_.vv = part(oh, (4, P)), part(oh, (4, P))
        s_.mo = part(oh, (4, D))
        s_.wtt = s_.lg

        A3 = m.AGG3[:, :, 0:D]
        setup(nc, ctx, m, a)
        sort_edges(nc, ctx, m)
        schedule(nc, ctx, m)
        tiled = lambda ap: ap.rearrange("(t p) d -> p t d", p=P)
        moments(nc, ctx, m, "ln0", m.HB)
        relation_weights(nc, ctx, m, 1, a["L0_gnn_basis1"], a["L0_gnn_att1"])
        relation_product(nc, ctx, m, 1, a["L0_gnn_root1"], a["L0_gnn_bias1"], None)
        relation_sum(nc, ctx, m, 1, a["L0_gnn_basis2"], a["L0_gnn_att2"])

        def mean_and_residual(v, done):
            v.reciprocal(m.tmp, m.AGG3[:, :, D:D + 1].rearrange("p t o -> p (t o)")).then_inc(done, 1)
            v.wait_ge(done, 1)
            row_tiles(v, lambda t: v.scalar_tensor_tensor(at(m.HB, t), at(A3, t), col(m.tmp, t), at(m.HB, t),
                                                          ALU.mult, ALU.add).then_inc(done, 1))
        moments(nc, ctx, m, "ln1", m.HB, make=mean_and_residual, nmake=1 + NT)
        relation_product(nc, ctx, m, 2, a["L0_gnn_root2"], a["L0_gnn_bias2"], (a["L0_gnn_ln1_g"], a["L0_gnn_ln1_b"]))
        relation_sum(nc, ctx, m, 2)
        recycle_semaphores(nc, m)
        moments(nc, ctx, m, "ln2", m.HB, make=mean_and_residual, nmake=1 + NT)
        residual_norm(nc, ctx, m, a)
        select_rows(nc, ctx, m, a)

        def gated(v, t, psum, outs):
            tmp = m.GS[:, 0, 0:D]
            v.wait_ge(outs, t * 3 + 6)
            v.tensor_tensor(tmp, psum, m.BO, ALU.add).then_inc(outs, 1)
            v.wait_ge(outs, t * 3 + 7)
            v.scalar_tensor_tensor(tmp, tmp, col(m.MW, t), at(m.HB, t), ALU.mult, ALU.add).then_inc(outs, 1)
            v.wait_ge(outs, t * 3 + 8)
            v.tensor_tensor(at(m.XV, t), at(m.XV, t), tmp, ALU.add).then_inc(outs, 1)
        feed_forward(nc, ctx, m, "ff0", m.HB, a["L0_ffn_w1"], a["L0_ffn_b1"], a["L0_ffn_w2"], a["L0_ffn_b2"],
                     ACT.Gelu_apprx_tanh, gated, 3, result=m.XV, xv=m.x1, spill=m.x2)
        moments(nc, ctx, m, "ln45", again=True)
        make_qkv(nc, ctx, m, a)
        recycle_semaphores(nc, m)
        edge_scores(nc, ctx, m)
        edge_softmax(nc, ctx, m)
        edge_values(nc, ctx, m)

        def attended(v, done):
            s3 = m.AGG3[:, :, D:AW]
            r3 = m.G[:, 0:NT * H].rearrange("p (t h) -> p t h", t=NT)
            v.tensor_scalar(r3, s3, 0.0, None, ALU.is_equal).then_inc(done, 1)
            v.wait_ge(done, 1)
            v.tensor_tensor(r3, r3, s3, ALU.add).then_inc(done, 1)
            v.wait_ge(done, 2)
            v.reciprocal(r3, r3).then_inc(done, 1)
            v.wait_ge(done, 3)
            for h in range(H):
                ah = m.AGG3[:, :, h * DH:(h + 1) * DH]
                v.tensor_tensor(ah, ah, r3[:, :, h:h + 1].broadcast_to([P, NT, DH]), ALU.mult).then_inc(done, 1)
            row_tiles(v, lambda t: v.tensor_scalar(at(m.HB, t), at(m.HB, t), col(m.mean4, t), col(m.rstd4, t),
                                                   ALU.subtract, ALU.mult).then_inc(done, 1))
            v.wait_ge(done, 3 + H + NT)
            v.tensor_tensor(m.HB, m.HB, A3, ALU.add).then_inc(done, 1)
        moments(nc, ctx, m, "ln6", m.HB, make=attended, nmake=4 + H + NT)

        def residual(v, t, psum, outs):
            tmp = m.GS[:, 0, 0:D]
            v.wait_ge(outs, t * 3 + 6)
            v.tensor_tensor(tmp, psum, m.BO, ALU.add).then_inc(outs, 1)
            v.tensor_tensor(at(m.HB, t), at(m.HB, t), at(m.XV, t), ALU.add).then_inc(outs, 1)
            v.wait_ge(outs, t * 3 + 8)
            v.tensor_tensor(at(m.HB, t), at(m.HB, t), tmp, ALU.add).then_inc(outs, 1)
        feed_forward(nc, ctx, m, "ff1", m.HB, a["L1_gnn_W_in"], a["L1_gnn_b_in"], a["L1_gnn_W_out"], a["L1_gnn_b_out"],
                     ACT.Gelu, residual, 3, result=m.HB, xv=m.x2, spill=m.x3,
                     affine=(a["L1_gnn_ln_res_g"], a["L1_gnn_ln_res_b"]))
        moments(nc, ctx, m, "ln7")
        slice_weights(nc, ctx, m, a)
        slice_pass(nc, ctx, m)
        slice_tokens(nc, ctx, m)
        slice_output(nc, ctx, m, out)


_INS = ['x', 'src', 'dst', 'edge_type_16', 'edge_weight', 'L0_gnn_basis1', 'L0_gnn_att1', 'L0_gnn_root1', 'L0_gnn_bias1',
        'L0_gnn_ln1_g', 'L0_gnn_ln1_b', 'L0_gnn_basis2', 'L0_gnn_att2', 'L0_gnn_root2', 'L0_gnn_bias2', 'L0_gnn_ln2_g',
        'L0_gnn_ln2_b', 'L0_ffn_wr', 'L0_ffn_br', 'L0_ffn_w1', 'L0_ffn_b1', 'L0_ffn_w2', 'L0_ffn_b2', 'L1_gnn_Wqkv',
        'L1_gnn_bqkv', 'L1_gnn_ln_attn_g', 'L1_gnn_ln_attn_b', 'L1_gnn_ln_res_g', 'L1_gnn_ln_res_b', 'L1_gnn_W_in',
        'L1_gnn_b_in', 'L1_gnn_W_out', 'L1_gnn_b_out', 'L1_ffn_W_fx', 'L1_ffn_b_fx', 'L1_ffn_W_x', 'L1_ffn_b_x',
        'L1_ffn_W_slice', 'L1_ffn_b_slice', 'L1_ffn_W_q', 'L1_ffn_W_k', 'L1_ffn_W_v', 'L1_ffn_W_out', 'L1_ffn_b_out',
        'L1_ffn_temperature']


def kernel(**inputs):
    import numpy as _np
    import concourse.bacc as _bacc
    from concourse import mybir as _mybir
    from concourse.bass_utils import run_bass_kernel_spmd as _run

    nc = _bacc.Bacc("TRN2", target_bir_lowering=False, num_devices=1)
    arrays, args = {}, {}
    for name in _INS:
        x = _np.ascontiguousarray(inputs[name])
        arrays[f"in_{name}"] = x
        args[name] = nc.dram_tensor(f"in_{name}", x.shape, _mybir.dt.from_np(x.dtype), kind="ExternalInput").ap()
    out = nc.dram_tensor("out_0", (N, D), F32, kind="ExternalOutput").ap()
    gnn_program(nc, args, out)
    r = _run(nc, [arrays], core_ids=[0])
    return r.results[0]["out_0"]
```
